# Optimizing a Trainium2 kernel written in Bass

```python
import numpy as np
import jax
import jax.numpy as jnp

def _softmax(x, axis=-1):
    return jax.nn.softmax(x, axis=axis)

def _gelu(x):
    return jax.nn.gelu(x, approximate=True)

def _silu(x):
    return jax.nn.silu(x)

def _sigmoid(x):
    return jax.nn.sigmoid(x)

def _layernorm(x, axis=-1, eps=1e-05):
    m = jnp.mean(x, axis=axis, keepdims=True)
    v = jnp.var(x, axis=axis, keepdims=True)
    return (x - m) / jnp.sqrt(v + eps)

def _scatter_add(tgt, idx, src, axis=0):
    return tgt.at[idx].add(src)

def _segment_sum(src, seg, n):
    return jax.ops.segment_sum(src, seg, n)
kernel_name = 'mk_xattn_ffn_d2_seqx_r8_266f6f'

def setup_inputs(seed: int=0):
    np.random.seed(seed)
    _w = jnp.asarray

    def _rec_inputs():
        import jax
        import jax.numpy as jnp
        _rk = jax.random.key(seed)
        x = -0.000125 + 0.9999 * jax.random.normal(jax.random.fold_in(_rk, 1), (16, 56, 512), jnp.float32)
        _lenS = 56 - jax.random.randint(jax.random.fold_in(_rk, 7), (16,), 0, max(1, 56 // 4) + 1, jnp.int32)
        _lenS2 = 1500 - jax.random.randint(jax.random.fold_in(_rk, 8), (16,), 0, max(1, 1500 // 4) + 1, jnp.int32)
        _ctx_4096P = jax.random.normal(jax.random.fold_in(_rk, 11), (16, 16, 512), jnp.float32)
        _ctx_4096c = jax.random.dirichlet(jax.random.fold_in(_rk, 511), 0.3 * jnp.ones((16,), jnp.float32), (16, 1500))
        _ctx_4096t = jnp.einsum('bsk,bkd->bsd', _ctx_4096c, _ctx_4096P)
        _ctx_4096t = _ctx_4096t * jax.lax.rsqrt(jnp.mean(jnp.square(_ctx_4096t)) + 1e-12) * 0.953939
        ctx_4096 = -1.52775e-05 + 0.999936 * (_ctx_4096t + 0.3 * jax.random.normal(jax.random.fold_in(_rk, 611), (16, 1500, 512), jnp.float32))
        return (x, ctx_4096)
    x, ctx_4096 = _rec_inputs()

    def _L0_xattn_setup():
        import jax, jax.numpy as jnp
        import numpy as np
        import math
        EPS = 1e-05
        LAMBDA = 0.6

        def _crucial_k(C):
            f = math.floor(LAMBDA * C)
            return f + f % 2

        def _conv1d(y, w):
            return jax.lax.conv_general_dilated(y, w, window_strides=(1,), padding=((3, 3),), dimension_numbers=('NCH', 'OIH', 'NCH'))

        def _norm_active(z, gamma, beta):
            mu = jnp.mean(z, axis=(0, 2), keepdims=True)
            var = jnp.mean((z - mu) ** 2, axis=(0, 2), keepdims=True)
            zn = (z - mu) * jax.lax.rsqrt(var + EPS)
            zn = zn * gamma.reshape(1, -1, 1) + beta.reshape(1, -1, 1)
            return jax.nn.sigmoid(jax.nn.relu(zn))
        key = jax.random.key(seed)
        k1, k2, k3 = jax.random.split(key, 3)
        B, C, L = (32, 32, 512)
        x = jax.random.normal(k1, (B, C, L), dtype=jnp.float32)
        channel_map = jax.random.normal(k2, (B, C, L), dtype=jnp.float32)
        fan_in = 2 * 7
        bound = 1.0 / math.sqrt(fan_in)
        conv_w = jax.random.uniform(k3, (1, 2, 7), jnp.float32, -bound, bound)
        bn_gamma = jnp.ones((1,), jnp.float32)
        bn_beta = jnp.zeros((1,), jnp.float32)
        return {'x': x, 'channel_map': channel_map, 'conv_w': conv_w, 'bn_gamma': bn_gamma, 'bn_beta': bn_beta}
    _L0_xattn_all = _L0_xattn_setup()
    _L0_xattn_in = {k: v for k, v in _L0_xattn_all.items() if k in ('conv_w', 'bn_gamma', 'bn_beta')}
    del _L0_xattn_all

    def _L0_ffn_setup():
        import jax, jax.numpy as jnp
        import numpy as np
        DIM = 512
        INTER = 128
        E = 16
        GROUPS = 4
        LIM = 2
        K = 2
        SHARED_INTER = 2 * INTER
        SCALE = 1.0
        key = jax.random.key(seed)
        ks = jax.random.split(key, 16)

        def n(k, shape, s=0.02):
            return jax.random.normal(k, shape, jnp.float32) * s
        return {'x': jax.random.normal(ks[0], (1, 256, DIM), jnp.float32), 'router_w': n(ks[1], (DIM, E)), 'router_b': n(ks[2], (E,)), 'router_bias': n(ks[3], (E,), 1.0), 'ew1': n(ks[4], (E, DIM, INTER)), 'eb1': n(ks[5], (E, INTER)), 'ew2': n(ks[6], (E, DIM, INTER)), 'eb2': n(ks[7], (E, INTER)), 'ew3': n(ks[8], (E, INTER, DIM)), 'eb3': n(ks[9], (E, DIM)), 'sw1': n(ks[10], (DIM, SHARED_INTER)), 'sb1': n(ks[11], (SHARED_INTER,)), 'sw2': n(ks[12], (DIM, SHARED_INTER)), 'sb2': n(ks[13], (SHARED_INTER,)), 'sw3': n(ks[14], (SHARED_INTER, DIM)), 'sb3': n(ks[15], (DIM,))}
    _L0_ffn_all = _L0_ffn_setup()
    _L0_ffn_in = {k: v for k, v in _L0_ffn_all.items() if k in ('router_w', 'router_b', 'router_bias', 'ew1', 'eb1', 'ew2', 'eb2', 'ew3', 'eb3', 'sw1', 'sb1', 'sw2', 'sb2', 'sw3', 'sb3')}
    del _L0_ffn_all

    def _L1_xattn_setup():
        import jax, jax.numpy as jnp
        import numpy as np
        TEXT_DIM = 512
        FEATURE_DIM = 512

        def _xavier_uniform(key, shape):
            fan_in, fan_out = (shape[1], shape[0])
            limit = float(np.sqrt(6.0 / (fan_in + fan_out)))
            return jax.random.uniform(key, shape, jnp.float32, -limit, limit)
        key = jax.random.key(seed)
        k1, k2, k3, k4 = jax.random.split(key, 4)
        text = jax.random.normal(k1, (8, 256, TEXT_DIM), jnp.float32)
        features = jax.random.normal(k2, (8, 72, FEATURE_DIM), jnp.float32)
        Wq = _xavier_uniform(k3, (FEATURE_DIM, TEXT_DIM))
        bq = jnp.zeros((FEATURE_DIM,), jnp.float32)
        Wk = _xavier_uniform(k4, (FEATURE_DIM, FEATURE_DIM))
        bk = jnp.zeros((FEATURE_DIM,), jnp.float32)
        return {'text': text, 'features': features, 'Wq': Wq, 'bq': bq, 'Wk': Wk, 'bk': bk}
    _L1_xattn_all = _L1_xattn_setup()
    _L1_xattn_in = {k: v for k, v in _L1_xattn_all.items() if k in ('Wq', 'bq', 'Wk', 'bk')}
    del _L1_xattn_all

    def _L1_ffn_setup():
        import jax, jax.numpy as jnp
        import numpy as np
        B, S, D, O, E, R = (4, 256, 512, 512, 8, 16)
        SCALING = 32.0 / 16.0
        MAX_THRESHOLD = 0.125
        key = jax.random.key(seed)
        ks = jax.random.split(key, 8)
        return {'x': jax.random.normal(ks[0], (B, S, D), jnp.float32), 'W_base': jax.random.normal(ks[1], (O, D), jnp.float32) * (1.0 / np.sqrt(D)), 'b_base': jax.random.normal(ks[2], (O,), jnp.float32) * 0.02, 'W_gate': jax.random.normal(ks[3], (E, D), jnp.float32) * (1.0 / np.sqrt(D)), 'W_thr': jax.random.normal(ks[4], (D,), jnp.float32) * (1.0 / np.sqrt(D)), 'b_thr': jax.random.normal(ks[5], (1,), jnp.float32) * 0.02, 'A_w': jax.random.normal(ks[6], (E, R, D), jnp.float32) * (1.0 / np.sqrt(D)), 'B_w': jax.random.normal(ks[7], (E, O, R), jnp.float32) * (1.0 / np.sqrt(R))}
    _L1_ffn_all = _L1_ffn_setup()
    _L1_ffn_in = {k: v for k, v in _L1_ffn_all.items() if k in ('W_base', 'b_base', 'W_gate', 'W_thr', 'b_thr', 'A_w', 'B_w')}
    del _L1_ffn_all
    return {'x': x, 'ctx_4096': ctx_4096, 'L0_xattn_conv_w': _L0_xattn_in['conv_w'], 'L0_xattn_bn_gamma': _L0_xattn_in['bn_gamma'], 'L0_xattn_bn_beta': _L0_xattn_in['bn_beta'], 'L0_ffn_router_w': _L0_ffn_in['router_w'], 'L0_ffn_router_b': _L0_ffn_in['router_b'], 'L0_ffn_router_bias': _L0_ffn_in['router_bias'], 'L0_ffn_ew1': _L0_ffn_in['ew1'], 'L0_ffn_eb1': _L0_ffn_in['eb1'], 'L0_ffn_ew2': _L0_ffn_in['ew2'], 'L0_ffn_eb2': _L0_ffn_in['eb2'], 'L0_ffn_ew3': _L0_ffn_in['ew3'], 'L0_ffn_eb3': _L0_ffn_in['eb3'], 'L0_ffn_sw1': _L0_ffn_in['sw1'], 'L0_ffn_sb1': _L0_ffn_in['sb1'], 'L0_ffn_sw2': _L0_ffn_in['sw2'], 'L0_ffn_sb2': _L0_ffn_in['sb2'], 'L0_ffn_sw3': _L0_ffn_in['sw3'], 'L0_ffn_sb3': _L0_ffn_in['sb3'], 'L1_xattn_Wq': _L1_xattn_in['Wq'], 'L1_xattn_bq': _L1_xattn_in['bq'], 'L1_xattn_Wk': _L1_xattn_in['Wk'], 'L1_xattn_bk': _L1_xattn_in['bk'], 'L1_ffn_W_base': _L1_ffn_in['W_base'], 'L1_ffn_b_base': _L1_ffn_in['b_base'], 'L1_ffn_W_gate': _L1_ffn_in['W_gate'], 'L1_ffn_W_thr': _L1_ffn_in['W_thr'], 'L1_ffn_b_thr': _L1_ffn_in['b_thr'], 'L1_ffn_A_w': _L1_ffn_in['A_w'], 'L1_ffn_B_w': _L1_ffn_in['B_w']}

def reference(x, ctx_4096, L0_xattn_conv_w, L0_xattn_bn_gamma, L0_xattn_bn_beta, L0_ffn_router_w, L0_ffn_router_b, L0_ffn_router_bias, L0_ffn_ew1, L0_ffn_eb1, L0_ffn_ew2, L0_ffn_eb2, L0_ffn_ew3, L0_ffn_eb3, L0_ffn_sw1, L0_ffn_sb1, L0_ffn_sw2, L0_ffn_sb2, L0_ffn_sw3, L0_ffn_sb3, L1_xattn_Wq, L1_xattn_bq, L1_xattn_Wk, L1_xattn_bk, L1_ffn_W_base, L1_ffn_b_base, L1_ffn_W_gate, L1_ffn_W_thr, L1_ffn_b_thr, L1_ffn_A_w, L1_ffn_B_w):
    import jax
    import jax.numpy as jnp

    def _L0_xattn_ref(x, channel_map, conv_w, bn_gamma, bn_beta):
        import jax, jax.numpy as jnp
        import numpy as np
        import math
        EPS = 1e-05
        LAMBDA = 0.6

        def _crucial_k(C):
            f = math.floor(LAMBDA * C)
            return f + f % 2

        def _conv1d(y, w):
            return jax.lax.conv_general_dilated(y, w, window_strides=(1,), padding=((3, 3),), dimension_numbers=('NCH', 'OIH', 'NCH'))

        def _norm_active(z, gamma, beta):
            mu = jnp.mean(z, axis=(0, 2), keepdims=True)
            var = jnp.mean((z - mu) ** 2, axis=(0, 2), keepdims=True)
            zn = (z - mu) * jax.lax.rsqrt(var + EPS)
            zn = zn * gamma.reshape(1, -1, 1) + beta.reshape(1, -1, 1)
            return jax.nn.sigmoid(jax.nn.relu(zn))
        B, C, L = x.shape
        k = _crucial_k(C)
        cm = jnp.moveaxis(channel_map, 1, 2)
        _, topk_idx = jax.lax.top_k(cm, k)
        b_idx = jnp.arange(B)[:, None, None]
        l_idx = jnp.arange(L)[None, :, None]
        mask = jnp.zeros((B, L, C), x.dtype).at[b_idx, l_idx, topk_idx].set(1.0)
        crucial_channels = jnp.moveaxis(mask, 2, 1)
        subcrucial_channels = 1.0 - crucial_channels
        crucial_features = crucial_channels * x
        subcrucial_features = subcrucial_channels * x
        c_max = jnp.max(crucial_features, axis=1, keepdims=True)
        c_avg = jnp.mean(crucial_features, axis=1, keepdims=True) * (C / k)
        s_max = jnp.max(subcrucial_features, axis=1, keepdims=True)
        s_avg = jnp.mean(subcrucial_features, axis=1, keepdims=True) * (C / (C - k))
        crucial_x = jnp.concatenate([c_max, c_avg], axis=1)
        subcrucial_x = jnp.concatenate([s_max, s_avg], axis=1)
        A_S1 = _norm_active(_conv1d(crucial_x, conv_w), bn_gamma, bn_beta)
        A_S2 = _norm_active(_conv1d(subcrucial_x, conv_w), bn_gamma, bn_beta)
        return crucial_features * A_S1 + subcrucial_features * A_S2

    def _L0_ffn_ref(x, router_w, router_b, router_bias, ew1, eb1, ew2, eb2, ew3, eb3, sw1, sb1, sw2, sb2, sw3, sb3):
        import jax, jax.numpy as jnp
        import numpy as np
        DIM = 512
        INTER = 128
        E = 16
        GROUPS = 4
        LIM = 2
        K = 2
        SHARED_INTER = 2 * INTER
        SCALE = 1.0
        shape = x.shape
        xt = x.reshape(-1, DIM)
        T = xt.shape[0]
        logits = xt @ router_w + router_b
        scores = jax.nn.softmax(logits.astype(jnp.float32), axis=-1) + router_bias
        g = scores.reshape(T, GROUPS, E // GROUPS)
        _, gidx = jax.lax.top_k(g.max(axis=-1), LIM)
        keep = jnp.zeros((T, GROUPS), bool).at[jnp.arange(T)[:, None], gidx].set(True)
        masked = jnp.where(keep[:, :, None], g, -jnp.inf).reshape(T, E)
        _, idx = jax.lax.top_k(masked, K)
        vals = (jnp.take_along_axis(scores, idx, axis=1) * SCALE).astype(x.dtype)
        gate = jnp.zeros((T, E), x.dtype).at[jnp.arange(T)[:, None], idx].add(vals)

        def step(y, p):
            w1, b1, w2, b2, w3, b3, ge = p
            h = jax.nn.silu(xt @ w1 + b1) * (xt @ w2 + b2)
            return (y + ge[:, None] * (h @ w3 + b3), None)
        y, _ = jax.lax.scan(step, jnp.zeros_like(xt), (ew1, eb1, ew2, eb2, ew3, eb3, gate.T))
        z = jax.nn.silu(xt @ sw1 + sb1) * (xt @ sw2 + sb2) @ sw3 + sb3
        return (y + z).reshape(shape)

    def _L1_xattn_ref(text, features, Wq, bq, Wk, bk):
        import jax, jax.numpy as jnp
        import numpy as np
        TEXT_DIM = 512
        FEATURE_DIM = 512

        def _xavier_uniform(key, shape):
            fan_in, fan_out = (shape[1], shape[0])
            limit = float(np.sqrt(6.0 / (fan_in + fan_out)))
            return jax.random.uniform(key, shape, jnp.float32, -limit, limit)
        Q = jnp.einsum('btx,dx->btd', text, Wq) + bq
        K = jnp.einsum('bpx,dx->bpd', features, Wk) + bk
        scale = 1.0 / jnp.sqrt(jnp.asarray(K.shape[-1], K.dtype))
        scores = jnp.einsum('btd,bpd->btp', Q, K) * scale
        attn = jax.nn.softmax(scores, axis=-1)
        attended = jnp.einsum('btp,bpd->btd', attn, features)
        return attended

    def _L1_ffn_ref(x, W_base, b_base, W_gate, W_thr, b_thr, A_w, B_w):
        import jax, jax.numpy as jnp
        import numpy as np
        B, S, D, O, E, R = (4, 256, 512, 512, 8, 16)
        SCALING = 32.0 / 16.0
        MAX_THRESHOLD = 0.125
        base = jnp.einsum('bsd,od->bso', x, W_base) + b_base
        xf = x.reshape(-1, D)
        gate = jax.nn.softmax(xf @ W_gate.T, axis=-1)
        thr = jax.nn.sigmoid(xf @ W_thr + b_thr[0]) * MAX_THRESHOLD
        adapted = gate - thr[:, None]
        selected = (adapted >= 0).astype(x.dtype)
        w = adapted * selected
        wsum = jnp.sum(w, axis=-1, keepdims=True)
        wsum = jnp.where(wsum == 0, jnp.ones_like(wsum), wsum)
        w = w / wsum
        h = jnp.einsum('nd,erd->ner', xf, A_w)
        moe = jnp.einsum('ner,ne,eor->no', h, w, B_w) * SCALING
        return base + moe.reshape(base.shape)
    x = x + _L0_xattn_ref(_layernorm(x, axis=-1), ctx_4096, L0_xattn_conv_w, L0_xattn_bn_gamma, L0_xattn_bn_beta)
    x = x + _L0_ffn_ref(_layernorm(x, axis=-1), L0_ffn_router_w, L0_ffn_router_b, L0_ffn_router_bias, L0_ffn_ew1, L0_ffn_eb1, L0_ffn_ew2, L0_ffn_eb2, L0_ffn_ew3, L0_ffn_eb3, L0_ffn_sw1, L0_ffn_sb1, L0_ffn_sw2, L0_ffn_sb2, L0_ffn_sw3, L0_ffn_sb3)
    x = x + _L1_xattn_ref(_layernorm(x, axis=-1), ctx_4096, L1_xattn_Wq, L1_xattn_bq, L1_xattn_Wk, L1_xattn_bk)
    x = x + _L1_ffn_ref(_layernorm(x, axis=-1), L1_ffn_W_base, L1_ffn_b_base, L1_ffn_W_gate, L1_ffn_W_thr, L1_ffn_b_thr, L1_ffn_A_w, L1_ffn_B_w)
    return x

_drawn_inputs = setup_inputs


def setup_inputs(seed=0):
    import zlib

    import numpy as np

    out = dict(_drawn_inputs(seed))
    spreads = {'L1_xattn_bq': (0.0, 0.621), 'L1_xattn_bk': (0.0, 2.0)}
    factors = {'L0_ffn_router_w': 8.0,
     'L0_ffn_router_b': 64.0,
     'L0_ffn_eb1': 25.106,
     'L0_ffn_eb2': 24.545,
     'L0_ffn_sb1': 50.461,
     'L0_ffn_sb2': 49.659,
     'L0_ffn_sb3': 4.273,
     'L1_ffn_b_base': 6.875}
    for name, (base, spread) in spreads.items():
        noise = np.random.default_rng([zlib.crc32(name.encode()), seed]).standard_normal(out[name].shape)
        drawn = base * np.exp(spread * noise) if base else spread * noise
        out[name] = jnp.asarray(drawn.astype(out[name].dtype))
    for name, factor in factors.items():
        out[name] = (out[name] * factor).astype(out[name].dtype)
    return out
```

```python
from contextlib import ExitStack

import concourse.bass as bass
from concourse import mybir

F32 = mybir.dt.float32
I32 = mybir.dt.int32
ALU = mybir.AluOpType
ACT = mybir.ActivationFunctionType
AX = mybir.AxisListType

P = 128
BIG = 3.0e38
EPS = 1e-5


class Chain:

    def __init__(self, eng, sem, base=0):
        self.eng, self.sem, self.base, self.n = eng, sem, base, 0

    def step(self, ins):
        self.n += 1
        return ins.then_inc(self.sem, 1)

    def settle(self):
        self.eng.wait_ge(self.sem, self.base + self.n)

    def link(self, ins):
        self.step(ins)
        self.settle()


def bass_xattn_ffn_layers(nc, A, out):
    x_dram, ctx_dram = A["x"], A["ctx_4096"]
    B, C, D = x_dram.shape
    S = ctx_dram.shape[1]
    KD = D // P
    SP = 125
    SJ = S // SP
    SG = SJ // 4
    GW = 4 * SP
    R = 64
    T = B // 2
    TOK = B * R
    TOPK = 34
    NS = 40
    E, INTER = A["L0_ffn_ew1"].shape[0], A["L0_ffn_ew1"].shape[2]
    ES = E + 2
    GR = 4
    E1, RK = A["L1_ffn_A_w"].shape[0], A["L1_ffn_A_w"].shape[1]
    SCALE = float(D) ** -0.5

    ctx = ExitStack()
    with ctx:
        def sb(name, shape, dt=F32):
            return ctx.enter_context(nc.sbuf_tensor(name, shape, dt))

        def sem(name):
            return ctx.enter_context(nc.semaphore(name))

        PS = [ctx.enter_context(nc.psum_tensor(f"bank{i}", [P, 512], F32)) for i in range(3, 8)]
        PS3 = ctx.enter_context(nc.psum_tensor("banks012", [P, 3, 512], F32))
        bank = [PS3[:, 0, :], PS3[:, 1, :], PS3[:, 2, :]] + [t[:, :] for t in PS]

        xnat = sb("xnat", [P, T, D])
        normed = sb("normed", [P, T, D])
        xnT = sb("xnT", [P, KD, TOK])
        crucial = normed[:, :, :].rearrange("p t d -> p (t d)").rearrange("p (k n) -> p k n", k=KD)
        qT = crucial
        big = sb("big", [P, 4 * SJ * D])
        slot = [big[:, s * SJ * D:(s + 1) * SJ * D].rearrange("p (j d) -> p j d", j=SJ) for s in range(4)]
        ctxT = [big[:, 2 * SJ * D + s * KD * S:2 * SJ * D + (s + 1) * KD * S].rearrange("p (k s) -> p k s", k=KD)
                for s in range(2)]
        work = sb("work", [P, 7168])
        wq = work[:, 0:2048].rearrange("p (k n) -> p k n", k=KD)
        wk = work[:, 2048:4096].rearrange("p (k n) -> p k n", k=KD)
        wb = work[:, 4096:6144].rearrange("p (k n) -> p k n", k=KD)
        aw = work[:, 6144:6656]
        bw = work[:, 6656:7168].rearrange("p (c n) -> p c n", c=KD)
        w12 = [work[:, 1024 * s:1024 * s + 1024].rearrange("p (m k n) -> p m k n", m=2, k=KD) for s in range(2)]
        w3 = [work[:, 2048 + 512 * s:2560 + 512 * s] for s in range(2)]
        hT = work[:, 3072:4096]
        silu = [work[:, 4096 + 512 * s:4608 + 512 * s] for s in range(2)]
        pair2 = work[:, 5120:6144]
        bias_bc = work[:, 6144:7168].rearrange("p (m n) -> p m n", m=2)
        FT = [work[:, 2000 * s:2000 * s + 2000].rearrange("p (k n) -> p k n", k=KD) for s in range(2)]
        gateT = work[0:E, 4096:5120]
        spare = xnT[:, :, :].rearrange("p k n -> p (k n)")
        qring = spare[:, 0:2 * KD * P].rearrange("p (s k n) -> p s k n", s=2, k=KD)
        probs = spare[:, 1024:1024 + S]
        probsT = spare[:, 2560:2560 + SJ * P].rearrange("p (j n) -> p j n", j=SJ)
        mq = sb("mq", [P, KD, D])
        wbT = sb("wbT", [P, KD, D])
        agT = sb("agT", [P, KD, P + 9])
        bT = sb("bT", [P, D])
        rw = sb("rw", [P, KD, E])
        ident = sb("ident", [P, P])
        pathmean = sb("pathmean", [P, P])
        ones = sb("ones", [P, P])
        lower = sb("lower", [P, GR * GR + E * E])
        reset = sb("reset", [P, KD * C])
        rows12 = big[0:12, 20000:20000 + P]
        gaterows = big[0:E1, 20480:20480 + D]
        b12rows = big[0:ES, 21504:21504 + 2 * P].rearrange("e (m n) -> e m n", m=2)
        eb3 = sb("eb3", [E, D])
        rb_bc = sb("rb_bc", [P, 2, E])
        cw_bc = sb("cw_bc", [P, 16])
        bthr_bc = sb("bthr_bc", [P, 1])
        cols12 = sb("cols12", [P, 12])
        b12 = sb("b12", [P, 2, ES])
        uv = sb("uv", [P, 2, KD])
        bqk = sb("bqk", [P, KD + 2])
        qbk = sb("qbk", [P, T])
        st = sb("st", [P, 2, KD, 2, B])
        cpad = sb("cpad", [P, 2, P + 6])
        zc = sb("zc", [P, P])
        attA = sb("attA", [P, P])
        bnst = sb("bnst", [P, T, 6])
        bnmv = sb("bnmv", [P, T, 2])
        lnv = sb("lnv", [P, T])
        lns = sb("lns", [P, T])
        lnr = sb("lnr", [P, T])
        top = sb("top", [P, KD, NS])
        cand = sb("cand", [P, KD, C])
        f1 = sb("f1", [P, KD, C])
        f2 = sb("f2", [P, KD, C])
        s1 = sb("s1", [P, KD])
        sm = sb("sm", [P, 8])
        lg = sb("lg", [P, T, E])
        lg2 = sb("lg2", [P, T, E])
        tv = sb("tv", [P, T, 4])
        gm = sb("gm", [P, T, GR])
        gq, gq2 = (pair2[:, n:n + T * GR * GR].rearrange("p (t e) -> p t e", t=T) for n in (0, 512))
        gate = sb("gate", [P, T, ES])
        am = sb("am", [P, 8])

        names = """wait_over act_over zeroed bias_loaded x_loaded const_loaded w_loaded ctx_loaded slot_free tp_done tp_evac ctxT_free
            ln_var ln_root ln_ready lnT_done lnT_evac pre_done pre_evac ph1 conv_in bn_a bn_b bn_c sig_in sig_out
            attT delta_ready delta_done delta_added router_done gates_ready gateT_done gateT_evac
            y0_done y_added wexp_loaded wexp_used h_done silu_done hT_ready y_done dve_ln dve_p1 dve_conv
            dve_rt dve_moe dve_at dve_fin pool_bias cslot_loaded cslot_free q_done q_evac q_ring qbk_done qbk_ready
            ft_done ft_act ft_dve s_done neg_bias exp_done pt_done pt_evac o_done o_added gl_done exp9 w_ready
            h9_done hw_ready hwT_done hwT_evac fin_done fin_added stored pre_dve pre_cc logits_exp ft_free1""".split()
        s = {n: sem(n) for n in names}
        ctx_loaded = [sem(f"ctx_loaded{n}") for n in range(2)]
        cslot_loaded = [sem(f"cslot_loaded{n}") for n in range(4)]
        wexp_loaded = [sem(f"wexp_loaded{n}") for n in range(2)]

        def pairs_hw(t):
            return pair2[:, t * P:(t + 1) * P]

        block = ctx.enter_context(nc.Block())

        @block.sync
        def _(sp):
            sp.wait_ge(s["zeroed"], 1)
            for j in range(2):
                sp.dma_start(xnat[R * j:R * j + C, :, :],
                             x_dram.rearrange("(t j) c d -> j c t d", j=2)[j]).then_inc(s["x_loaded"], 16)
            sp.dma_start(ident[:, :], A["ident"]).then_inc(s["const_loaded"], 16)
            sp.dma_start(pathmean[:, :], A["pathmean"]).then_inc(s["const_loaded"], 16)
            sp.dma_start(lower[:, :], A["lower"]).then_inc(s["const_loaded"], 16)
            sp.dma_start(reset[:, :], A["reset"]).then_inc(s["const_loaded"], 16)
            with sp.Fori(0, T) as i:
                for p in range(2):
                    sp.wait_ge(s["slot_free"], 2 * i + p + 1)
                    sp.dma_start(slot[p][0:SP], ctx_dram[2 * i + p].rearrange("(j p) d -> p j d", p=SP)).then_inc(ctx_loaded[p], 16)

            def expert_load(n, sl, e=None, h=None):
                sp.wait_ge(s["wexp_used"], n + 1)
                if h is None:
                    w1, w2, w3d = A["L0_ffn_ew1"][e], A["L0_ffn_ew2"][e], A["L0_ffn_ew3"][e]
                else:
                    c = slice(h * INTER, (h + 1) * INTER)
                    w1, w2, w3d = A["L0_ffn_sw1"][:, c], A["L0_ffn_sw2"][:, c], A["L0_ffn_sw3"][c, :]
                sp.dma_start(w12[sl][:, 0], w1.rearrange("(k p) n -> p k n", p=P)).then_inc(wexp_loaded[sl], 16)
                sp.dma_start(w12[sl][:, 1], w2.rearrange("(k p) n -> p k n", p=P)).then_inc(wexp_loaded[sl], 16)
                sp.dma_start(w3[sl], w3d).then_inc(wexp_loaded[sl], 16)

            sp.wait_ge(s["pre_evac"], PRE_ACT)
            for m, v in enumerate((A["L0_ffn_sb3"], A["L1_ffn_b_base"])):
                sp.dma_start(bias_bc[:, m, :], v.rearrange("(a n) -> a n", a=1).broadcast_to([P, D])).then_inc(s["bias_loaded"], 16)
            for h in range(2):
                expert_load(h, h, h=h)
            with sp.Fori(0, E // 2) as i:
                for p in range(2):
                    expert_load(2 * i + p + 2, p, e=2 * i + p)

            sp.wait_ge(s["ph1"], B)
            with sp.Fori(0, B // 4) as i:
                for p in range(4):
                    sp.wait_ge(s["cslot_free"], 4 * i + p + 1)
                    sp.dma_start(slot[p][0:SP], ctx_dram[4 * i + p].rearrange("(j p) d -> p j d", p=SP)).then_inc(cslot_loaded[p], 16)
            for t in range(T):
                sp.wait_ge(s["fin_added"], t + 1)
                for j in range(2):
                    sp.dma_start(out[2 * t + j], xnat[R * j:R * j + C, t, :]).then_inc(s["stored"], 16)
            sp.wait_ge(s["stored"], 32 * T)

        @block.gpsimd
        def _(pool):
            pool.memset(xnat[:, :, :], 0.0).then_inc(s["zeroed"], 1)
            pool.memset(ones[:, :], 1.0).then_inc(s["zeroed"], 1)
            pool.memset(gate[:, :, E:ES], 1.0).then_inc(s["zeroed"], 1)
            pool.memset(cpad[:, :, :], 0.0).then_inc(s["zeroed"], 1)
            pool.wait_ge(s["lnT_evac"], T)
            pool.memset(crucial, 0.0).then_inc(s["zeroed"], 1)
            pool.wait_ge(s["bias_loaded"], 32)
            for stage, which in ((2, 0), (4, 1)):
                pool.wait_ge(s["ln_ready"], stage * T)
                for t in range(T):
                    pool.tensor_tensor(xnat[:, t, :], xnat[:, t, :], bias_bc[:, which, :], ALU.add).then_inc(s["pool_bias"], 1)
                if which == 0:
                    pool.wait_ge(s["q_evac"], 2 * KD)
                    pool.wait_ge(s["qbk_done"], 1)
                    with pool.Fori(0, T // 2) as i:
                        for p in range(2):
                            pool.wait_ge(s["o_done"], 2 * i + p + 1)
                            pool.tensor_copy(qring[:, p], qT[:, :, bass.ds((2 * i + p) * P, P)]).then_inc(s["q_ring"], 1)

        @block.scalar
        def _(act):
            def load(dst, src):
                act.dma_start(dst, src).then_inc(s["w_loaded"], 16)

            def row(a):
                return a.rearrange("(a n) -> a n", a=1)

            load(wq, A["L1_xattn_Wq"].rearrange("(k p) n -> p k n", p=P))
            load(wk, A["L1_xattn_Wk"].rearrange("(k p) n -> p k n", p=P))
            load(wb, A["L1_ffn_W_base"].rearrange("(k p) n -> p k n", p=P))
            load(aw, A["L1_ffn_A_w"].rearrange("e r d -> (e r) d"))
            for c in range(KD):
                load(bw[:, c, :].rearrange("p (e r) -> p e r", e=E1),
                     A["L1_ffn_B_w"][:, c * P:(c + 1) * P, :].rearrange("e p r -> p e r"))
            load(rw[:, :, :], A["L0_ffn_router_w"].rearrange("(k p) n -> p k n", p=P))
            load(rows12[0:4, :], A["L1_ffn_W_thr"].rearrange("(k p) -> k p", p=P))
            load(rows12[4:8, :], A["L1_xattn_bk"].rearrange("(k p) -> k p", p=P))
            load(rows12[8:12, :], A["L1_xattn_bq"].rearrange("(k p) -> k p", p=P))
            load(gaterows, A["L1_ffn_W_gate"])
            for m in range(2):
                load(b12rows[0:E, m, :], A[f"L0_ffn_eb{m + 1}"])
                load(b12rows[E:ES, m, :], A[f"L0_ffn_sb{m + 1}"].rearrange("(h p) -> h p", p=P))
            load(eb3[:, :], A["L0_ffn_eb3"])
            load(rb_bc[:, 0, :], row(A["L0_ffn_router_b"]).broadcast_to([P, E]))
            load(rb_bc[:, 1, :], row(A["L0_ffn_router_bias"]).broadcast_to([P, E]))
            load(cw_bc[:, 0:14], A["L0_xattn_conv_w"].rearrange("a c k -> a (c k)").broadcast_to([P, 14]))
            load(cw_bc[:, 14:15], row(A["L0_xattn_bn_gamma"]).broadcast_to([P, 1]))
            load(cw_bc[:, 15:16], row(A["L0_xattn_bn_beta"]).broadcast_to([P, 1]))
            load(bthr_bc[:, :], row(A["L1_ffn_b_thr"]).broadcast_to([P, 1]))
            act.sem_inc(s["tp_evac"], 4)

            def ln_root(stage):
                act.wait_ge(s["ln_var"], stage + 1)
                act.activation(lns[:, :], lnv[:, :], ACT.Sqrt).then_inc(s["ln_root"], 1)

            def ln_evac(stage):
                for t in range(T):
                    act.wait_ge(s["lnT_done"], stage * T + t + 1)
                    act.activation(xnT[:, :, t * P:(t + 1) * P],
                                   bank[4 + t % 4].rearrange("p (k n) -> p k n", k=KD), ACT.Copy).then_inc(s["lnT_evac"], 1)

            ln_root(0)
            ln_evac(0)

            n = [0]

            def pre(dst, src):
                act.activation(dst, src, ACT.Copy).then_inc(s["pre_evac"], 1)

            def pre_wait():
                n[0] += 1
                act.wait_ge(s["pre_done"], n[0])
                return bank[4 + (n[0] - 1) % 4]

            b = pre_wait()
            pre(cols12[:, :], b[:, 0:12])
            pre(b12[:, 0, :], b[:, 16:16 + ES])
            pre(b12[:, 1, :], b[:, 48:48 + ES])
            pre(agT[:, :, P:P + E1], b[:, 80:80 + KD * E1].rearrange("p (k n) -> p k n", k=KD))
            pre(agT[:, :, P + E1], b[:, 0:4])
            b = pre_wait()
            pre(agT[:, :, 0:P], b.rearrange("p (k n) -> p k n", k=KD))
            b = pre_wait()
            pre(bT[:, :], b)
            for k in range(KD):
                b = pre_wait()
                pre(wbT[:, k, :], b)
            for k in range(KD):
                b = pre_wait()
                pre(mq[:, k, :], b)
            b = pre_wait()
            pre(uv[:, :, :], b[:, 0:8].rearrange("p (m k) -> p m k", m=2))
            pre(bqk[:, 5:6], b[:, 8:9])

            with act.Fori(0, T) as i:
                for p in range(2):
                    act.wait_ge(s["ctxT_free"], 2 * i + p + 1)
                    for g in range(KD * SG):
                        act.wait_ge(s["tp_done"], (2 * i + p) * KD * SG + g + 1)
                        act.activation(ctxT[p][:, g // SG, (g % SG) * GW:(g % SG + 1) * GW],
                                       bank[g % 4][:, 0:GW], ACT.Copy).then_inc(s["tp_evac"], 1)

            act.wait_ge(s["bn_c"], 1)
            act.activation(sm[:, 4:5], sm[:, 3:4], ACT.Sqrt).then_inc(s["sig_out"], 1)
            act.wait_ge(s["sig_in"], 1)
            act.activation(zc[:, :], zc[:, :], ACT.Sigmoid).then_inc(s["sig_out"], 1)

            ln_root(1)
            ln_evac(1)

            act.wait_ge(s["gates_ready"], 1)
            act.activation(lg2[:, :, :], lg[:, :, :], ACT.Exp).then_inc(s["logits_exp"], 1)

            def expert(n, e):
                for h in range(2):
                    act.wait_ge(s["h_done"], 2 * n + h + 1)
                    act.sem_inc(s["act_over"], 1)
                    act.activation(silu[h], bank[2 * h], ACT.Silu,
                                   bias=b12[:, 0, e]).then_inc(s["silu_done"], 1)

            for h in range(2):
                expert(h, slice(E + h, E + h + 1))
            with act.Fori(0, E // 2) as i:
                for p in range(2):
                    expert(2 * i + p + 2, bass.ds(2 * i + p, 1))

            ln_root(2)
            ln_evac(2)
            for y in range(2 * KD):
                act.wait_ge(s["q_done"], y + 1)
                act.activation(qT[:, y // 2, (y % 2) * 512:(y % 2 + 1) * 512], bank[4 + y % 4], ACT.Identity,
                               bias=uv[:, 1, y // 2:y // 2 + 1]).then_inc(s["q_evac"], 1)

            with act.Fori(0, T // 2) as i:
                for p in range(2):
                    pair = 2 * i + p
                    for g in range(0, 24, 2):
                        act.wait_ge(s["ft_done"], pair * 24 + g + 1)
                        if g >= 8 or g < 8:
                            act.wait_ge(s["s_done"], pair * 6 + g // 4 + 1)
                        act.activation(FT[g // 4 % 2][:, g % 4, :], bank[3 + g % 4][:, 0:GW], ACT.Copy).then_inc(s["ft_act"], 1)
                    act.wait_ge(s["neg_bias"], pair + 1)
                    act.activation(probs.rearrange("p (g n) -> p g n", g=SG), PS3[:, :, 0:GW], ACT.Exp,
                                   bias=am[:, 2:3], scale=SCALE, accum_out=am[:, 3:4]).then_inc(s["exp_done"], 1)
                    for g in range(SG):
                        act.wait_ge(s["pt_done"], pair * SG + g + 1)
                        act.activation(probsT[0:SP, 4 * g:4 * g + 4, :], bank[3 + g][0:SP, :].rearrange("p (j n) -> p j n", j=4),
                                       ACT.Copy).then_inc(s["pt_evac"], 1)

            ln_root(3)
            ln_evac(3)
            act.wait_ge(s["w_ready"], 1)
            act.activation(lg2[:, :, 0:9], lg[:, :, 0:9], ACT.Exp).then_inc(s["exp9"], 1)
            for t in range(2):
                act.wait_ge(s["hwT_done"], t + 1)
                act.activation(hT[:, t * 512:(t + 1) * 512], bank[2 + t], ACT.Copy).then_inc(s["hwT_evac"], 1)

        @block.tensor
        def _(pe):
            pe.sem_inc(s["slot_free"], 2)
            pe.sem_inc(s["wexp_used"], 2)
            pe.sem_inc(s["cslot_free"], 4)
            pe.sem_inc(s["o_done"], 2)
            pe.sem_inc(s["s_done"], 2)

            def mm(o, l, r, first, last):
                return pe.matmul(o, l, r, start=first, stop=last)

            def ln_turn(stage):
                for t in range(T):
                    pe.wait_ge(s["ln_ready"], stage * T + t + 1)
                    if t >= 4:
                        pe.wait_ge(s["lnT_evac"], stage * T + t - 3)
                    for k in range(KD):
                        ins = pe.transpose(bank[4 + t % 4][:, k * P:(k + 1) * P], normed[:, t, k * P:(k + 1) * P], ident[:, :])
                    ins.then_inc(s["lnT_done"], 1)

            pe.wait_ge(s["const_loaded"], 64)
            ln_turn(0)

            n = [0]
            freed = [0, 0, 0, 0]

            def job(evacs, build):
                if n[0] >= 4:
                    pe.wait_ge(s["pre_evac"], freed[n[0] % 4])
                else:
                    pe.wait_ge(s["lnT_evac"], T)
                build(bank[4 + n[0] % 4]).then_inc(s["pre_done"], 1)
                n[0] += 1
                job.total += evacs
                freed[(n[0] - 1) % 4] = job.total
            job.total = 0

            def j_rows(b):
                pe.transpose(b[:, 0:12], rows12, ident[0:12, 0:12])
                for m in range(2):
                    pe.transpose(b[:, 16 + 32 * m:16 + 32 * m + ES], b12rows[:, m, :], ident[0:ES, 0:ES])
                for k in range(KD):
                    ins = pe.transpose(b[:, 80 + k * E1:80 + (k + 1) * E1], gaterows[:, k * P:(k + 1) * P], ident[0:E1, 0:E1])
                return ins

            def j_aw(b):
                for k in range(KD):
                    ins = pe.transpose(b[:, k * P:(k + 1) * P], aw[:, k * P:(k + 1) * P], ident[:, :])
                return ins

            def j_bw(b):
                for c in range(KD):
                    ins = pe.transpose(b[:, c * P:(c + 1) * P], bw[:, c, :], ident[:, :])
                return ins

            def j_wb(k):
                def build(b):
                    for c in range(KD):
                        ins = pe.transpose(b[:, c * P:(c + 1) * P], wb[:, c, k * P:(k + 1) * P], ident[:, :])
                    return ins
                return build

            def j_mq(x):
                def build(b):
                    for k in range(KD):
                        ins = mm(b, wq[:, k, x * P:(x + 1) * P], wk[:, k, :], k == 0, k == KD - 1)
                    return ins
                return build

            def j_uv(b):
                for m, (w, at) in enumerate(((wq, 4), (wk, 8))):
                    for x in range(KD):
                        for k in range(KD):
                            mm(b[:, 4 * m + x:4 * m + x + 1], w[:, k, x * P:(x + 1) * P], cols12[:, at + k:at + k + 1],
                               k == 0, k == KD - 1)
                pe.wait_ge(s["pre_cc"], 1)
                return mm(b[:, 8:9], ones[:, :], bqk[:, 4:5], True, True)

            pe.wait_ge(s["w_loaded"], W_LOADS * 16)
            job(5, j_rows)
            job(1, j_aw)
            job(1, j_bw)
            for k in range(KD):
                job(1, j_wb(k))
            for k in range(KD):
                job(1, j_mq(k))
            job(2, j_uv)
            assert job.total == PRE_ACT

            with pe.Fori(0, T) as i:
                for p in range(2):
                    pe.wait_ge(ctx_loaded[p], (i + 1) * 16)
                    for g in range(KD * SG):
                        pe.wait_ge(s["tp_evac"], (2 * i + p) * KD * SG + g + 1)
                        k = g // SG
                        for q in range(4):
                            ins = pe.transpose(bank[g % 4][:, q * SP:(q + 1) * SP],
                                               slot[p][0:SP, 4 * (g % SG) + q, k * P:(k + 1) * P], ident[0:SP, 0:SP])
                        ins.then_inc(s["tp_done"], 1)
                    pe.wait_ge(s["tp_done"], (2 * i + p + 1) * KD * SG)
                    pe.sem_inc(s["slot_free"], 1)

            pe.wait_ge(s["pre_evac"], PRE_ACT)
            pe.wait_ge(s["conv_in"], 1)
            for ch in range(2):
                ins = pe.transpose(bank[4][:, ch * P:(ch + 1) * P], st[:, ch].rearrange("p k a b -> p (k a b)"), ident[:, :])
            ins.then_inc(s["bn_a"], 1)
            pe.wait_ge(s["bn_b"], 1)
            mm(bank[5][:, 0:1], pathmean[:, :], sm[:, 0:1], True, True).then_inc(s["bn_a"], 1)
            pe.wait_ge(s["bn_b"], 2)
            mm(bank[5][:, 1:2], pathmean[:, :], sm[:, 2:3], True, True).then_inc(s["bn_a"], 1)
            pe.wait_ge(s["sig_out"], 2)
            pe.transpose(bank[6][:, 0:P], zc[:, :], ident[:, :]).then_inc(s["attT"], 1)

            pe.wait_ge(s["delta_ready"], 1)
            for t in range(T):
                if t >= 4:
                    pe.wait_ge(s["delta_added"], t - 3)
                for k in range(KD):
                    ins = pe.transpose(bank[t % 4][:, k * P:(k + 1) * P], xnT[:, k, t * P:(t + 1) * P], ident[:, :])
                ins.then_inc(s["delta_done"], 1)
            ln_turn(1)

            pe.wait_ge(s["lnT_evac"], 2 * T)
            for t in range(T):
                for k in range(KD):
                    ins = mm(bank[0][:, t * E:(t + 1) * E], xnT[:, k, t * P:(t + 1) * P], rw[:, k, :], k == 0, k == KD - 1)
            ins.then_inc(s["router_done"], 1)

            def expert(n, sl, turn):
                pe.wait_ge(wexp_loaded[sl], turn * 48)
                for h in range(2):
                    if not (isinstance(n, int) and n == 0):
                        pe.wait_ge(s["hT_ready"], 2 * n - 2 + h + 1)
                    for m in range(2):
                        for k in range(KD):
                            ins = mm(bank[2 * h + m], w12[sl][:, m, k, :], xnT[:, k, h * 512:(h + 1) * 512], k == 0, k == KD - 1)
                    ins.then_inc(s["h_done"], 1)
                for t in range(T):
                    if t % 4 == 0:
                        pe.wait_ge(s["hT_ready"], 2 * n + t // 4 + 1)
                    if not (isinstance(n, int) and n == 0 and t < 4):
                        pe.wait_ge(s["y_added"], n * T + t - 3)
                    ins = mm(bank[4 + t % 4], hT[:, t * P:(t + 1) * P], w3[sl], True, True)
                    ins.then_inc(s["y_done"], 1)
                pe.wait_ge(s["y_done"], (n + 1) * T)
                pe.sem_inc(s["wexp_used"], 1)

            pe.wait_ge(s["logits_exp"], 1)
            for h in range(2):
                expert(h, h, 1)
            with pe.Fori(0, E // 2) as i:
                for p in range(2):
                    expert(2 * i + p + 2, p, i + 2)

            for t in range(T):
                pe.wait_ge(s["gates_ready"], 2)
                pe.wait_ge(s["hT_ready"], 2 * ES)
                ins = pe.transpose(bank[t // 4][0:E, (t % 4) * P:(t % 4 + 1) * P], gate[:, t, 0:E], ident[:, :])
            ins.then_inc(s["gateT_done"], 1)
            pe.wait_ge(s["gateT_evac"], 2)
            for t in range(T):
                pe.wait_ge(s["y_added"], ES * T + t - 3)
                mm(bank[4 + t % 4], gateT[:, t * P:(t + 1) * P], eb3[:, :], True, True).then_inc(s["y_done"], 1)
            ln_turn(2)

            pe.wait_ge(s["lnT_evac"], 3 * T)
            for y in range(2 * KD):
                if y >= 4:
                    pe.wait_ge(s["q_evac"], y - 3)
                for k in range(KD):
                    ins = mm(bank[4 + y % 4], mq[:, k, (y // 2) * P:(y // 2 + 1) * P],
                             xnT[:, k, (y % 2) * 512:(y % 2 + 1) * 512], k == 0, k == KD - 1)
                ins.then_inc(s["q_done"], 1)
            for t in range(T):
                for k in range(KD):
                    ins = mm(bank[0][:, t:t + 1], xnT[:, k, t * P:(t + 1) * P], uv[:, 0, k:k + 1], k == 0, k == KD - 1)
            ins.then_inc(s["qbk_done"], 1)
            pe.wait_ge(s["qbk_ready"], 1)
            pe.wait_ge(s["q_evac"], 2 * KD)

            def turn(pair, sl, u):
                g, a = u // 2, u % 2
                for k in range(KD):
                    nn = 4 * u + k
                    w, own = ("ft_act", "ft_dve")[nn % 2], nn // 2
                    pe.wait_ge(s[w], pair * 12 + own + 1)
                    for q in range(4):
                        ins = pe.transpose(bank[3 + nn % 4][:, q * SP:(q + 1) * SP],
                                           slot[sl + a][0:SP, 4 * g + q, k * P:(k + 1) * P], ident[0:SP, 0:SP])
                    ins.then_inc(s["ft_done"], 1)

            def score(pair, p, u):
                g, a = u // 2, u % 2
                pe.wait_ge(s["ft_act"], pair * 12 + 2 * (u + 1) + 2)
                pe.wait_ge(s["ft_dve"], pair * 12 + 2 * (u + 1) + 2)
                for k in range(KD):
                    ins = mm(bank[g][R * a:R * a + R, 0:GW], qring[:, p, k, R * a:R * a + R], FT[u % 2][:, k, :], k == 0, k == KD - 1)
                ins.then_inc(s["s_done"], 1)

            pe.sem_inc(s["ft_act"], 2)
            pe.sem_inc(s["ft_dve"], 2)
            pe.sem_inc(s["exp_done"], 1)
            pe.sem_inc(s["o_added"], 1)
            pe.sem_inc(s["pt_evac"], 1)
            with pe.Fori(0, T // 2) as i:
                for p in range(2):
                    pair = 2 * i + p
                    for a in range(2):
                        pe.wait_ge(cslot_loaded[2 * p + a], (i + 1) * 16)
                    pe.wait_ge(s["q_ring"], pair + 1)
                    pe.wait_ge(s["pt_evac"], pair * SG + 1)
                    turn(pair, 2 * p, 0)
                    for u in range(6):
                        if u < 5:
                            turn(pair, 2 * p, u + 1)
                        if u == 0:
                            pe.wait_ge(s["exp_done"], pair + 1)
                        score(pair, p, u)
                    pe.wait_ge(s["exp_done"], pair + 2)
                    pe.wait_ge(s["ft_act"], (pair + 1) * 12 + 2)
                    pe.wait_ge(s["ft_dve"], (pair + 1) * 12 + 2)
                    for g in range(SG):
                        for q in range(4):
                            ins = pe.transpose(bank[3 + g][0:SP, q * P:(q + 1) * P], probs[:, (4 * g + q) * SP:(4 * g + q + 1) * SP], ident[:, :])
                        ins.then_inc(s["pt_done"], 1)
                    pe.wait_ge(s["o_added"], pair + 1)
                    pe.wait_ge(s["pt_evac"], (pair + 1) * SG + 1)
                    for j in range(SJ):
                        for a in range(2):
                            ins = mm(bank[7][R * a:R * a + R, :], probsT[0:SP, j, R * a:R * a + R], slot[2 * p + a][0:SP, j, :],
                                     j == 0, j == SJ - 1)
                    ins.then_inc(s["o_done"], 1)
                    pe.wait_ge(s["o_done"], pair + 3)
                    pe.sem_inc(s["cslot_free"], 2)

            ln_turn(3)
            pe.wait_ge(s["lnT_evac"], 4 * T)
            for t in range(T):
                for k in range(KD):
                    ins = mm(bank[0][:, t * 9:(t + 1) * 9], xnT[:, k, t * P:(t + 1) * P], agT[:, k, P:P + 9], k == 0, k == KD - 1)
            ins.then_inc(s["gl_done"], 1)
            for t in range(T):
                for k in range(KD):
                    ins = mm(bank[2 + t // 4][:, (t % 4) * P:(t % 4 + 1) * P], xnT[:, k, t * P:(t + 1) * P], agT[:, k, 0:P], k == 0, k == KD - 1)
                if t % 4 == 3:
                    ins.then_inc(s["h9_done"], 1)
            for t in range(T):
                if t % 4 == 0:
                    pe.wait_ge(s["hw_ready"], t // 4 + 1)
                ins = pe.transpose(bank[2 + t // 4][:, (t % 4) * P:(t % 4 + 1) * P], pairs_hw(t), ident[:, :])
                if t % 4 == 3:
                    ins.then_inc(s["hwT_done"], 1)
            for t in range(T):
                if t >= 4:
                    pe.wait_ge(s["fin_added"], t - 3)
                for k in range(KD):
                    mm(bank[4 + t % 4], xnT[:, k, t * P:(t + 1) * P], wbT[:, k, :], k == 0, False)
                pe.wait_ge(s["hwT_evac"], t // 4 + 1)
                mm(bank[4 + t % 4], hT[:, t * P:(t + 1) * P], bT[:, :], False, True).then_inc(s["fin_done"], 1)

        @block.vector
        def _(dve):
            ln = Chain(dve, s["dve_ln"])

            def layernorm(stage):
                for t in range(T):
                    ln.step(dve.bn_stats(bnst[:, t, :], xnat[:, t, :]))
                ln.settle()
                for t in range(T):
                    ln.step(dve.bn_aggr(bnmv[:, t, :], bnst[:, t, :]))
                ln.settle()
                dve.tensor_scalar(lnv[:, :], bnmv[:, :, 1], EPS, None, ALU.add).then_inc(s["ln_var"], 1)
                dve.wait_ge(s["ln_root"], stage + 1)
                ln.link(dve.reciprocal(lnr[:, :], lns[:, :]))
                for t in range(T):
                    dve.tensor_scalar(normed[:, t, :], xnat[:, t, :], bnmv[:, t, 0:1], lnr[:, t:t + 1],
                                      ALU.subtract, ALU.mult).then_inc(s["ln_ready"], 1)

            dve.sem_inc(s["ctxT_free"], 2)
            dve.wait_ge(s["zeroed"], 2)
            dve.wait_ge(s["x_loaded"], 32)
            layernorm(0)

            pc = Chain(dve, s["pre_dve"])
            dve.wait_ge(s["pre_evac"], 1)
            pc.link(dve.tensor_tensor(bqk[:, 0:KD], cols12[:, 4:8], cols12[:, 8:12], ALU.mult))
            dve.tensor_reduce(bqk[:, 4:5], bqk[:, 0:KD], AX.X, ALU.add).then_inc(s["pre_cc"], 1)

            dve.wait_ge(s["lnT_evac"], T)
            dve.wait_ge(s["zeroed"], 5)
            dve.wait_ge(s["const_loaded"], 64)

            STEPS = 19 + 18

            def bc(ap, n):
                return ap.unsqueeze(2).broadcast_to([P, KD, n])

            with dve.Fori(0, T) as i:
                for p in range(2):
                    b = 2 * i + p
                    ch = Chain(dve, s["dve_p1"], b * PH1_STEPS)
                    dve.wait_ge(s["tp_evac"], (b + 1) * KD * SG + 4)
                    ch.step(dve.tensor_copy(cand[:, :, :], ctxT[p][:, :, 0:C]))
                    for r in range(NS // 8):
                        dve.sem_inc(s["wait_over"], 1)
                        for k in range(KD):
                            ch.step(dve.max(top[:, k, 8 * r:8 * r + 8], ctxT[p][:, k, :]))
                        ch.settle()
                        if r < NS // 8 - 1:
                            dve.sem_inc(s["wait_over"], 1)
                            for k in range(KD):
                                ch.step(dve.match_replace(out=ctxT[p][:, k, :], in_to_replace=top[:, k, 8 * r:8 * r + 8],
                                                          in_values=ctxT[p][:, k, :], imm_value=-BIG))
                            ch.settle()
                    dve.sem_inc(s["ctxT_free"], 1)
                    thr = top[:, :, TOPK - 1]
                    ch.link(dve.tensor_tensor(f2[:, :, 0:TOPK], top[:, :, 0:TOPK], bc(thr, TOPK), ALU.is_gt))
                    ch.link(dve.tensor_reduce(s1[:, :], f2[:, :, 0:TOPK], AX.X, ALU.add))
                    ch.link(dve.tensor_scalar(s1[:, :], s1[:, :], -1.0, float(TOPK), ALU.mult, ALU.add))
                    ch.link(dve.tensor_tensor(f1[:, :, :], cand[:, :, :], bc(thr, C), ALU.is_equal))
                    ch.link(dve.tensor_tensor_scan(f2[:, :, :].rearrange("p k c -> p (k c)"), reset[:, :],
                                                   f1[:, :, :].rearrange("p k c -> p (k c)"), 0.0, ALU.mult, ALU.add))
                    ch.link(dve.tensor_tensor(f2[:, :, :], f2[:, :, :], bc(s1[:, :], C), ALU.is_le))
                    ch.link(dve.tensor_tensor(f1[:, :, :], f1[:, :, :], f2[:, :, :], ALU.mult))
                    ch.link(dve.tensor_tensor(f2[:, :, :], cand[:, :, :], bc(thr, C), ALU.is_gt))
                    ch.link(dve.tensor_tensor(f1[:, :, :], f1[:, :, :], f2[:, :, :], ALU.add))
                    cols = bass.ds(b * R, C)
                    ch.link(dve.tensor_tensor(f2[:, :, :], f1[:, :, :], xnT[:, :, cols], ALU.mult))
                    ch.step(dve.tensor_copy(crucial[:, :, cols], f2[:, :, :]))
                    ch.link(dve.tensor_tensor(f1[:, :, :], xnT[:, :, cols], f2[:, :, :], ALU.subtract))
                    for path, f in ((0, f2), (1, f1)):
                        for what, op in ((0, ALU.max), (1, ALU.add)):
                            ch.step(dve.tensor_reduce(st[:, what, :, path, bass.ds(b, 1)], f[:, :, :].unsqueeze(2), AX.X, op))
                    ch.settle()
                    assert ch.n == PH1_STEPS, ch.n
                    dve.sem_inc(s["ph1"], 1)

            cv = Chain(dve, s["dve_conv"])
            cv.step(dve.tensor_scalar(st[:, 1, :, 0, :], st[:, 1, :, 0, :], 1.0 / C, float(C / TOPK), ALU.mult, ALU.mult))
            cv.link(dve.tensor_scalar(st[:, 1, :, 1, :], st[:, 1, :, 1, :], 1.0 / C, float(C / (C - TOPK)), ALU.mult, ALU.mult))
            dve.sem_inc(s["conv_in"], 1)
            dve.wait_ge(s["bn_a"], 1)
            turned = bank[4][:, 0:2 * P].rearrange("p (c n) -> p c n", c=2)
            cv.step(dve.tensor_copy(cpad[:, :, 3:3 + P], turned))
            for q in range(KD):
                here = slice(32 * q, 32 * q + 32)
                if q > 0:
                    cv.step(dve.tensor_copy(cpad[here, :, 0:3], turned[32 * q - 32:32 * q, :, P - 3:P]))
                if q < KD - 1:
                    cv.step(dve.tensor_copy(cpad[here, :, P + 3:P + 6], turned[32 * q + 32:32 * q + 64, :, 0:3]))
            cv.settle()
            dve.wait_ge(s["w_loaded"], W_LOADS * 16)
            for n in range(14):
                win = cpad[:, n // 7, n % 7:n % 7 + P]
                if n == 0:
                    cv.link(dve.tensor_scalar(zc[:, :], win, cw_bc[:, 0:1], None, ALU.mult))
                else:
                    cv.link(dve.scalar_tensor_tensor(out=zc[:, :], in0=win, scalar=cw_bc[:, n:n + 1], in1=zc[:, :],
                                                     op0=ALU.mult, op1=ALU.add))
            cv.link(dve.bn_stats(bnst[:, 0, :], zc[:, :]))
            cv.link(dve.bn_aggr(sm[:, 0:2], bnst[:, 0, :]))
            dve.sem_inc(s["bn_b"], 1)
            dve.wait_ge(s["bn_a"], 2)
            cv.link(dve.tensor_tensor(sm[:, 2:3], sm[:, 0:1], bank[5][:, 0:1], ALU.subtract))
            cv.step(dve.tensor_copy(sm[:, 6:7], bank[5][:, 0:1]))
            cv.link(dve.tensor_tensor(sm[:, 2:3], sm[:, 2:3], sm[:, 2:3], ALU.mult))
            cv.link(dve.tensor_tensor(sm[:, 2:3], sm[:, 2:3], sm[:, 1:2], ALU.add))
            dve.sem_inc(s["bn_b"], 1)
            dve.wait_ge(s["bn_a"], 3)
            cv.link(dve.tensor_scalar(sm[:, 3:4], bank[5][:, 1:2], EPS, None, ALU.add))
            dve.sem_inc(s["bn_c"], 1)
            dve.wait_ge(s["sig_out"], 1)
            cv.link(dve.reciprocal(sm[:, 5:6], sm[:, 4:5]))
            cv.link(dve.tensor_scalar(zc[:, :], zc[:, :], sm[:, 6:7], sm[:, 5:6], ALU.subtract, ALU.mult))
            cv.link(dve.tensor_scalar(zc[:, :], zc[:, :], cw_bc[:, 14:15], cw_bc[:, 15:16], ALU.mult, ALU.add))
            cv.link(dve.tensor_scalar(zc[:, :], zc[:, :], 0.0, None, ALU.max))
            dve.sem_inc(s["sig_in"], 1)
            dve.wait_ge(s["attT"], 1)
            cv.link(dve.tensor_copy(attA[:, :], bank[6][:, 0:P]))
            def gates_of(k, path):
                return attA[:, (2 * k + path) * B:(2 * k + path + 1) * B].unsqueeze(2).broadcast_to([P, B, R])

            for k in range(KD):
                cv.step(dve.tensor_tensor(xnT[:, k, :], xnT[:, k, :], crucial[:, k, :], ALU.subtract))
            cv.settle()
            for k in range(KD):
                for path, a in ((1, xnT), (0, crucial)):
                    v = a[:, k, :].rearrange("p (b c) -> p b c", b=B)
                    cv.step(dve.tensor_tensor(v, v, gates_of(k, path), ALU.mult))
            cv.settle()
            for k in range(KD):
                cv.step(dve.tensor_tensor(xnT[:, k, :], xnT[:, k, :], crucial[:, k, :], ALU.add))
            cv.settle()
            dve.sem_inc(s["delta_ready"], 1)
            for t in range(T):
                dve.wait_ge(s["delta_done"], t + 1)
                dve.tensor_tensor(xnat[:, t, :], xnat[:, t, :], bank[t % 4], ALU.add).then_inc(s["delta_added"], 1)
            dve.wait_ge(s["delta_added"], T)
            layernorm(1)

            rt = Chain(dve, s["dve_rt"])
            dve.wait_ge(s["router_done"], 1)
            logits = bank[0][:, 0:T * E].rearrange("p (t e) -> p t e", t=T)

            def over(ap, n):
                return ap.unsqueeze(2).broadcast_to([P, ap.shape[1], n])

            def per_tile(ap):
                return ap.unsqueeze(1).broadcast_to([P, T, ap.shape[1]])

            rt.link(dve.tensor_tensor(lg[:, :, :], logits, per_tile(rb_bc[:, 0, :]), ALU.add))
            rt.link(dve.tensor_reduce(tv[:, :, 0], lg[:, :, :], AX.X, ALU.max))
            rt.link(dve.tensor_tensor(lg[:, :, :], lg[:, :, :], over(tv[:, :, 0], E), ALU.subtract))
            dve.sem_inc(s["gates_ready"], 1)
            dve.wait_ge(s["logits_exp"], 1)
            rt.link(dve.tensor_reduce(tv[:, :, 1], lg2[:, :, :], AX.X, ALU.add))
            rt.link(dve.reciprocal(tv[:, :, 2], tv[:, :, 1]))
            rt.link(dve.tensor_tensor(lg[:, :, :], lg2[:, :, :], over(tv[:, :, 2], E), ALU.mult))
            rt.link(dve.tensor_tensor(lg[:, :, :], lg[:, :, :], per_tile(rb_bc[:, 1, :]), ALU.add))
            rt.link(dve.tensor_reduce(gm[:, :, :], lg[:, :, :].rearrange("p t (g m) -> p t g m", g=GR), AX.X, ALU.max))

            def ranks(v, n, low, q, q2, res):
                for t in range(T):
                    mine = v[:, t, :].unsqueeze(2).broadcast_to([P, n, n])
                    other = v[:, t, :].unsqueeze(1).broadcast_to([P, n, n])
                    rt.step(dve.tensor_tensor(q(t), other, mine, ALU.is_gt))
                    rt.link(dve.tensor_tensor(q2(t), other, mine, ALU.is_equal))
                    rt.link(dve.tensor_tensor(q2(t), q2(t), low, ALU.mult))
                    rt.link(dve.tensor_tensor(q(t), q(t), q2(t), ALU.add))
                    rt.link(dve.tensor_reduce(res[:, t, :], q(t), AX.X, ALU.add))

            dve.wait_ge(s["pre_evac"], PRE_ACT)

            def sq(tile, n):
                return lambda t: tile[:, t, :].rearrange("p (a b) -> p a b", a=n)

            ranks(gm, GR, lower[:, 0:GR * GR].rearrange("p (a b) -> p a b", a=GR), sq(gq, GR), sq(gq2, GR), tv)
            rt.link(dve.tensor_scalar(gm[:, :, :], tv[:, :, :], 2.0, None, ALU.is_lt))
            keep = gm[:, :, :].unsqueeze(3).broadcast_to([P, T, GR, E // GR])
            sc4 = lg2[:, :, :].rearrange("p t (g m) -> p t g m", g=GR)
            rt.link(dve.tensor_tensor(sc4, lg[:, :, :].rearrange("p t (g m) -> p t g m", g=GR), keep, ALU.mult))
            rt.link(dve.tensor_scalar(gm[:, :, :], gm[:, :, :], -1.0, BIG, ALU.add, ALU.mult))
            rt.link(dve.tensor_tensor(sc4, sc4, keep, ALU.add))
            big16 = lower[:, GR * GR:].rearrange("p (a b) -> p a b", a=E)
            ranks(lg2, E, big16, lambda t: pair2[:, 0:E * E].rearrange("p (a b) -> p a b", a=E), lambda t: pair2[:, E * E:2 * E * E].rearrange("p (a b) -> p a b", a=E), gate[:, :, 0:E])
            rt.link(dve.tensor_scalar(gate[:, :, 0:E], gate[:, :, 0:E], 2.0, None, ALU.is_lt))
            rt.link(dve.tensor_tensor(gate[:, :, 0:E], gate[:, :, 0:E], lg[:, :, :], ALU.mult))
            dve.sem_inc(s["gates_ready"], 1)

            def expert(n, e):
                for h in range(2):
                    dve.wait_ge(s["silu_done"], 2 * n + h + 1)
                    dve.scalar_tensor_tensor(out=hT[:, h * 512:(h + 1) * 512], in0=bank[2 * h + 1], scalar=b12[:, 1, e],
                                             in1=silu[h], op0=ALU.add, op1=ALU.mult).then_inc(s["hT_ready"], 1)
                for t in range(T):
                    dve.wait_ge(s["y_done"], n * T + t + 1)
                    if t == 0:
                        dve.wait_ge(s["y_added"], n * T)
                    dve.scalar_tensor_tensor(out=xnat[:, t, :], in0=bank[4 + t % 4], scalar=gate[:, t, e],
                                             in1=xnat[:, t, :], op0=ALU.mult, op1=ALU.add).then_inc(s["y_added"], 1)

            dve.wait_ge(s["pool_bias"], T)
            for h in range(2):
                expert(h, slice(E + h, E + h + 1))
            with dve.Fori(0, E // 2) as i:
                for p in range(2):
                    expert(2 * i + p + 2, bass.ds(2 * i + p, 1))
            dve.wait_ge(s["gateT_done"], 1)
            for t in range(2):
                dve.tensor_copy(gateT[:, t * 512:(t + 1) * 512], bank[t][0:E, :]).then_inc(s["gateT_evac"], 1)
            for t in range(T):
                dve.wait_ge(s["y_done"], ES * T + t + 1)
                dve.tensor_tensor(xnat[:, t, :], xnat[:, t, :], bank[4 + t % 4], ALU.add).then_inc(s["y_added"], 1)
            dve.wait_ge(s["y_added"], (ES + 1) * T)
            layernorm(2)

            dve.wait_ge(s["qbk_done"], 1)
            dve.tensor_scalar(qbk[:, :], bank[0][:, 0:T], bqk[:, 5:6], None, ALU.add).then_inc(s["qbk_ready"], 1)
            dve.wait_ge(s["qbk_ready"], 1)

            with dve.Fori(0, T // 2) as i:
                for p in range(2):
                    pair = 2 * i + p
                    at = Chain(dve, s["dve_at"], pair * 3)
                    for g in range(1, 24, 2):
                        dve.wait_ge(s["ft_done"], pair * 24 + g + 1)
                        dve.wait_ge(s["s_done"], pair * 6 + g // 4 + 1)
                        dve.tensor_copy(FT[g // 4 % 2][:, g % 4, :], bank[3 + g % 4][:, 0:GW]).then_inc(s["ft_dve"], 1)
                    dve.wait_ge(s["s_done"], (pair + 1) * 6 + 2)
                    at.link(dve.tensor_reduce(am[:, 0:1], PS3[:, :, 0:GW], AX.XY, ALU.max))
                    q = qbk[:, bass.ds(pair, 1)]
                    at.link(dve.tensor_scalar(am[:, 1:2], am[:, 0:1], q, None, ALU.add))
                    dve.tensor_scalar(am[:, 2:3], am[:, 1:2], q, -SCALE, ALU.subtract, ALU.mult).then_inc(s["neg_bias"], 1)
                    dve.wait_ge(s["exp_done"], pair + 2)
                    at.link(dve.reciprocal(am[:, 4:5], am[:, 3:4]))
                    dve.wait_ge(s["o_done"], pair + 3)
                    xr = xnat[:, bass.ds(pair, 1), :]
                    dve.scalar_tensor_tensor(out=xr, in0=bank[7].unsqueeze(1), scalar=am[:, 4:5], in1=xr,
                                             op0=ALU.mult, op1=ALU.add).then_inc(s["o_added"], 1)
            dve.wait_ge(s["o_added"], T + 1)
            layernorm(3)

            fc = Chain(dve, s["dve_fin"])
            dve.wait_ge(s["gl_done"], 1)
            g9 = bank[0][:, 0:T * 9].rearrange("p (t e) -> p t e", t=T)
            fc.link(dve.tensor_reduce(tv[:, :, 0], g9[:, :, 0:E1], AX.X, ALU.max))
            fc.step(dve.tensor_tensor(lg[:, :, 0:E1], g9[:, :, 0:E1], over(tv[:, :, 0], E1), ALU.subtract))
            fc.link(dve.tensor_scalar(lg[:, :, 8:9], g9[:, :, 8:9], bthr_bc[:, 0:1], -1.0, ALU.add, ALU.mult))
            dve.sem_inc(s["w_ready"], 1)
            dve.wait_ge(s["exp9"], 1)
            fc.step(dve.tensor_reduce(tv[:, :, 1], lg2[:, :, 0:E1], AX.X, ALU.add))
            fc.link(dve.tensor_scalar(tv[:, :, 2:3], lg2[:, :, 8:9], 1.0, None, ALU.add))
            fc.link(dve.reciprocal(tv[:, :, 1:3], tv[:, :, 1:3]))
            fc.step(dve.tensor_tensor(lg[:, :, 0:E1], lg2[:, :, 0:E1], over(tv[:, :, 1], E1), ALU.mult))
            fc.link(dve.tensor_scalar(tv[:, :, 3], tv[:, :, 2], 0.125, None, ALU.mult))
            fc.link(dve.tensor_tensor(lg[:, :, 0:E1], lg[:, :, 0:E1], over(tv[:, :, 3], E1), ALU.subtract))
            fc.link(dve.tensor_scalar(lg[:, :, 0:E1], lg[:, :, 0:E1], 0.0, None, ALU.max))
            fc.link(dve.tensor_reduce(tv[:, :, 0], lg[:, :, 0:E1], AX.X, ALU.add))
            fc.link(dve.tensor_scalar(tv[:, :, 1], tv[:, :, 0], 0.0, None, ALU.is_equal))
            fc.link(dve.tensor_tensor(tv[:, :, 0], tv[:, :, 0], tv[:, :, 1], ALU.add))
            fc.link(dve.reciprocal(tv[:, :, 1], tv[:, :, 0]))
            fc.link(dve.tensor_tensor(lg[:, :, 0:E1], lg[:, :, 0:E1], over(tv[:, :, 1], E1), ALU.mult))
            fc.link(dve.tensor_scalar(lg2[:, :, 0:E1], lg[:, :, 0:E1], 2.0, None, ALU.mult))
            for h in range(2):
                dve.wait_ge(s["h9_done"], h + 1)
                for t in range(4 * h, 4 * h + 4):
                    v = bank[2 + h][:, (t % 4) * P:(t % 4 + 1) * P].rearrange("p (e r) -> p e r", e=E1)
                    w = lg2[:, t, 0:E1].unsqueeze(2).broadcast_to([P, E1, RK])
                    fc.step(dve.tensor_tensor(pairs_hw(t).rearrange("p (e r) -> p e r", e=E1), v, w, ALU.mult))
                fc.settle()
                dve.sem_inc(s["hw_ready"], 1)
            dve.wait_ge(s["pool_bias"], 2 * T)
            for t in range(T):
                dve.wait_ge(s["fin_done"], t + 1)
                dve.tensor_tensor(xnat[:, t, :], xnat[:, t, :], bank[4 + t % 4], ALU.add).then_inc(s["fin_added"], 1)


PRE_ACT = 5 + 1 + 1 + 4 + 4 + 2
PH1_STEPS = 1 + 20 + 16 + 9 + 3 + 4
W_LOADS = 4 + 4 + 1 + 3 + 1 + 4 + 1 + 2 + 3 + 1


_INS = ['x', 'ctx_4096', 'L0_xattn_conv_w', 'L0_xattn_bn_gamma', 'L0_xattn_bn_beta', 'L0_ffn_router_w', 'L0_ffn_router_b',
        'L0_ffn_router_bias', 'L0_ffn_ew1', 'L0_ffn_eb1', 'L0_ffn_ew2', 'L0_ffn_eb2', 'L0_ffn_ew3', 'L0_ffn_eb3',
        'L0_ffn_sw1', 'L0_ffn_sb1', 'L0_ffn_sw2', 'L0_ffn_sb2', 'L0_ffn_sw3', 'L0_ffn_sb3', 'L1_xattn_Wq', 'L1_xattn_bq',
        'L1_xattn_Wk', 'L1_xattn_bk', 'L1_ffn_W_base', 'L1_ffn_b_base', 'L1_ffn_W_gate', 'L1_ffn_W_thr', 'L1_ffn_b_thr',
        'L1_ffn_A_w', 'L1_ffn_B_w']


def _constants():
    import numpy as np
    p = np.arange(128)
    path = (p // 16) % 2
    low = [np.tril(np.ones((n, n), np.float32), -1).reshape(-1) for n in (4, 16)]
    reset = np.ones((4, 56), np.float32)
    reset[:, 0] = 0.0
    return {"ident": np.eye(128, dtype=np.float32),
            "pathmean": (path[:, None] == path[None, :]).astype(np.float32) / 64,
            "lower": np.tile(np.concatenate(low), (128, 1)),
            "reset": np.tile(reset.reshape(-1), (128, 1))}


def kernel(**inputs):
    import numpy as _np
    import concourse.bacc as _bacc
    from concourse import mybir as _mybir
    from concourse.bass_utils import run_bass_kernel_spmd as _run

    nc = _bacc.Bacc("TRN2", target_bir_lowering=False, num_devices=1)
    arrays, A = {}, {}
    given = {n: inputs[n] for n in _INS}
    given.update(_constants())
    for name, v in given.items():
        a = _np.ascontiguousarray(v)
        arrays[f"in_{name}_dram"] = a
        A[name] = nc.dram_tensor(f"in_{name}_dram", a.shape, _mybir.dt.from_np(a.dtype), kind="ExternalInput").ap()
    out = nc.dram_tensor("out_0_dram", (16, 56, 512), _mybir.dt.float32, kind="ExternalOutput").ap()
    bass_xattn_ffn_layers(nc, A, out)
    r = _run(nc, [arrays], core_ids=[0])
    return r.results[0]["out_0_dram"]
```

```python
from contextlib import ExitStack

import concourse.bass as bass
from concourse import mybir

F32 = mybir.dt.float32
I32 = mybir.dt.int32
BF16 = mybir.dt.bfloat16
ALU = mybir.AluOpType
ACT = mybir.ActivationFunctionType
AX = mybir.AxisListType

P = 128
BIG = 3.4028235e38
EPS = 1e-5


class Chain:

    def __init__(self, eng, sem, base=0):
        self.eng, self.sem, self.base, self.n = eng, sem, base, 0

    def step(self, ins):
        self.n += 1
        return ins.then_inc(self.sem, 1)

    def settle(self):
        self.eng.wait_ge(self.sem, self.base + self.n)

    def link(self, ins):
        self.step(ins)
        self.settle()


def bass_xattn_ffn_layers(nc, A, out):
    x_dram, ctx_dram = A["x"], A["ctx_4096"]
    B, C, D = x_dram.shape
    S = ctx_dram.shape[1]
    KD = D // P
    SP = 125
    SJ = S // SP
    SG = SJ // 4
    GW = 4 * SP
    R = 64
    T = B // 2
    TOK = B * R
    TOPK = 34
    NS = 40
    E, INTER = A["L0_ffn_ew1"].shape[0], A["L0_ffn_ew1"].shape[2]
    ES = E + 2
    GR = 4
    E1, RK = A["L1_ffn_A_w"].shape[0], A["L1_ffn_A_w"].shape[1]
    SCALE = float(D) ** -0.5

    ctx = ExitStack()
    with ctx:
        def sb(name, shape, dt=F32):
            return ctx.enter_context(nc.sbuf_tensor(name, shape, dt))

        def sem(name):
            return ctx.enter_context(nc.semaphore(name))

        PS = [ctx.enter_context(nc.psum_tensor(f"bank{i}", [P, 512], F32)) for i in range(3, 8)]
        PS3 = ctx.enter_context(nc.psum_tensor("banks012", [P, 3, 512], F32))
        bank = [PS3[:, 0, :], PS3[:, 1, :], PS3[:, 2, :]] + [t[:, :] for t in PS]

        xnat = sb("xnat", [P, T, D])
        normed = sb("normed", [P, T, D])
        xnT = sb("xnT", [P, KD, TOK])
        crucial = normed[:, :, :].rearrange("p t d -> p (t d)").rearrange("p (k n) -> p k n", k=KD)
        qT = crucial
        big = sb("big", [P, 4 * SJ * D])
        slot = [big[:, s * SJ * D:(s + 1) * SJ * D].rearrange("p (j d) -> p j d", j=SJ) for s in range(4)]
        ctxT = [big[:, 2 * SJ * D + s * KD * S:2 * SJ * D + (s + 1) * KD * S].rearrange("p (k s) -> p k s", k=KD)
                for s in range(2)]
        work = sb("work", [P, 7168])
        wq = work[:, 0:2048].rearrange("p (k n) -> p k n", k=KD)
        wk = work[:, 2048:4096].rearrange("p (k n) -> p k n", k=KD)
        wb = work[:, 4096:6144].rearrange("p (k n) -> p k n", k=KD)
        aw = work[:, 6144:6656]
        bw = work[:, 6656:7168].rearrange("p (c n) -> p c n", c=KD)
        w12 = [work[:, 1024 * s:1024 * s + 1024].rearrange("p (m k n) -> p m k n", m=2, k=KD) for s in range(2)]
        w3 = [work[:, 2048 + 512 * s:2560 + 512 * s] for s in range(2)]
        hT = work[:, 3072:4096]
        silu = [work[:, 4096 + 512 * s:4608 + 512 * s] for s in range(2)]
        pair2 = work[:, 5120:6144]
        bias_bc = work[:, 6144:7168].rearrange("p (m n) -> p m n", m=2)
        FT = [work[:, 2000 * s:2000 * s + 2000].rearrange("p (k n) -> p k n", k=KD) for s in range(2)]
        gateT = work[0:E, 4096:5120]
        spare = xnT[:, :, :].rearrange("p k n -> p (k n)")
        qring = spare[:, 0:2 * KD * P].rearrange("p (s k n) -> p s k n", s=2, k=KD)
        probs = spare[:, 1024:1024 + S]
        probsT = spare[:, 2560:2560 + SJ * P].rearrange("p (j n) -> p j n", j=SJ)
        mq = sb("mq", [P, KD, D])
        wbT = sb("wbT", [P, KD, D])
        agT = sb("agT", [P, KD, P + 9])
        bT = sb("bT", [P, D])
        above = [t[:, :, :].rearrange("p k n -> p (k n)")[:, S // 2 * n:S // 2 * (n + 1)].bitcast(BF16)
                 for t in (mq, wbT) for n in range(2)]
        partial = [mq[:, :, :].rearrange("p k n -> p (k n)")[:, S + P * n:S + P * (n + 1)].bitcast(BF16) for n in range(2)]
        identb = sb("identb", [P, P], BF16)
        onesb = sb("onesb", [P, 2], BF16)
        sorted15 = sb("sorted15", [P, KD, 16])
        okay = sb("okay", [P, KD], I32)
        thr_n = sb("thr_n", [P, 2, KD])
        full = sb("full", [P, KD])
        fsum = sb("fsum", [P, 1])
        flag = sb("flag", [1, 1], I32)
        rw = sb("rw", [P, KD, E])
        ident = sb("ident", [P, P])
        pathmean = sb("pathmean", [P, P])
        ones = sb("ones", [P, P])
        lower = sb("lower", [P, GR * GR + E * E])
        reset = sb("reset", [P, KD * C])
        rows12 = big[0:12, 20000:20000 + P]
        gaterows = big[0:E1, 20480:20480 + D]
        b12rows = big[0:ES, 21504:21504 + 2 * P].rearrange("e (m n) -> e m n", m=2)
        eb3 = sb("eb3", [E, D])
        rb_bc = sb("rb_bc", [P, 2, E])
        cw_bc = sb("cw_bc", [P, 16])
        bthr_bc = sb("bthr_bc", [P, 1])
        cols12 = sb("cols12", [P, 12])
        b12 = sb("b12", [P, 2, ES])
        uv = sb("uv", [P, 2, KD])
        bqk = sb("bqk", [P, KD + 2])
        qbk = sb("qbk", [P, T])
        st = sb("st", [P, 2, KD, 2, B])
        cpad = sb("cpad", [P, 2, P + 6])
        zc = sb("zc", [P, P])
        attA = sb("attA", [P, P])
        bnst = sb("bnst", [P, T, 6])
        bnmv = sb("bnmv", [P, T, 2])
        lnv = sb("lnv", [P, T])
        lns = sb("lns", [P, T])
        lnr = sb("lnr", [P, T])
        top = sb("top", [P, KD, NS])
        cand = sb("cand", [P, KD, C])
        sel = [sb(f"sel{n}", [P, KD, C]) for n in range(2)]
        f1 = sb("f1", [P, KD, C])
        f2 = sb("f2", [P, KD, C])
        s1 = sb("s1", [P, KD])
        sm = sb("sm", [P, 8])
        lg, lg2 = (t[:, :, :].rearrange("p k c -> p (k c)")[:, 0:T * E].rearrange("p (t e) -> p t e", t=T) for t in sel)
        tv = sb("tv", [P, T, 4])
        gm = sb("gm", [P, T, GR])
        gq, gq2 = (pair2[:, n:n + T * GR * GR].rearrange("p (t e) -> p t e", t=T) for n in (0, 512))
        gate = cand[:, :, :].rearrange("p k c -> p (k c)")[:, 0:T * ES].rearrange("p (t e) -> p t e", t=T)
        am = sb("am", [P, 8])

        names = """bf_ready searched rows_loaded sums_done partial_ready counts_done cmp_done dve_s pool_sel sel_ready flag_ready fb_tp_done fb_evac dve_fb dve_red pool_cr pool_over full_ready fsum_done fb_done wait_over act_over zeroed bias_loaded x_loaded const_loaded w_loaded ctx_loaded slot_free tp_done tp_evac ctxT_free
            ln_var ln_root ln_ready lnT_done lnT_evac pre_done pre_evac ph1 conv_in bn_a bn_b bn_c sig_in sig_out
            attT delta_ready delta_done delta_added router_done gates_ready gateT_done gateT_evac
            y0_done y_added wexp_loaded wexp_used h_done silu_done hT_ready y_done dve_ln dve_p1 dve_conv
            dve_rt dve_moe dve_at dve_fin pool_bias cslot_loaded cslot_free q_done q_evac q_ring qbk_done qbk_ready
            ft_done ft_act ft_dve s_done neg_bias exp_done pt_done pt_evac o_done o_added gl_done exp9 w_ready
            h9_done hw_ready hwT_done hwT_evac fin_done fin_added stored pre_dve pre_cc logits_exp ft_free1""".split()
        s = {n: sem(n) for n in names}
        ctx_loaded = [sem(f"ctx_loaded{n}") for n in range(2)]
        cslot_loaded = [sem(f"cslot_loaded{n}") for n in range(4)]
        fb_loaded = [sem(f"fb_loaded{n}") for n in range(2)]
        wexp_loaded = [sem(f"wexp_loaded{n}") for n in range(2)]

        def pairs_hw(t):
            return pair2[:, t * P:(t + 1) * P]

        block = ctx.enter_context(nc.Block())

        @block.sync
        def _(sp):
            sp.wait_ge(s["zeroed"], 1)
            for j in range(2):
                sp.dma_start(xnat[R * j:R * j + C, :, :],
                             x_dram.rearrange("(t j) c d -> j c t d", j=2)[j]).then_inc(s["x_loaded"], 16)
            sp.dma_start(ident[:, :], A["ident"]).then_inc(s["const_loaded"], 16)
            sp.dma_start(pathmean[:, :], A["pathmean"]).then_inc(s["const_loaded"], 16)
            sp.dma_start(lower[:, :], A["lower"]).then_inc(s["const_loaded"], 16)
            sp.dma_start(reset[:, :], A["reset"]).then_inc(s["const_loaded"], 16)
            def ctx_load(b, p):
                sp.dma_start(slot[p][0:SP], ctx_dram[b].rearrange("(j p) d -> p j d", p=SP)).then_inc(ctx_loaded[p], 16)

            for p in range(2):
                ctx_load(p, p)
            with sp.Fori(1, T) as i:
                for p in range(2):
                    sp.wait_ge(s["tp_done"], (2 * i + p - 1) * KD * SG)
                    ctx_load(2 * i + p, p)

            sp.wait_ge(s["flag_ready"], 1)
            with sp.If(sp.value_load(flag[0:1, 0:1], min_val=0, max_val=1) > 0):
                for p in range(2):
                    sp.dma_start(slot[p][0:SP], ctx_dram[p].rearrange("(j p) d -> p j d", p=SP)).then_inc(fb_loaded[p], 16)
                with sp.Fori(1, T) as i:
                    for p in range(2):
                        sp.wait_ge(s["fb_tp_done"], (2 * i + p - 1) * KD * SG)
                        sp.dma_start(slot[p][0:SP], ctx_dram[2 * i + p].rearrange("(j p) d -> p j d", p=SP)).then_inc(fb_loaded[p], 16)

            sp.wait_ge(s["searched"], 1)
            def load(dst, src):
                sp.dma_start(dst, src).then_inc(s["rows_loaded"], 16)

            load(rows12[0:4, :], A["L1_ffn_W_thr"].rearrange("(k p) -> k p", p=P))
            load(rows12[4:8, :], A["L1_xattn_bk"].rearrange("(k p) -> k p", p=P))
            load(rows12[8:12, :], A["L1_xattn_bq"].rearrange("(k p) -> k p", p=P))
            load(gaterows, A["L1_ffn_W_gate"])
            for m in range(2):
                load(b12rows[0:E, m, :], A[f"L0_ffn_eb{m + 1}"])
                load(b12rows[E:ES, m, :], A[f"L0_ffn_sb{m + 1}"].rearrange("(h p) -> h p", p=P))

            def expert_load(n, sl, e=None, h=None):
                sp.wait_ge(s["wexp_used"], n + 1)
                if h is None:
                    w1, w2, w3d = A["L0_ffn_ew1"][e], A["L0_ffn_ew2"][e], A["L0_ffn_ew3"][e]
                else:
                    c = slice(h * INTER, (h + 1) * INTER)
                    w1, w2, w3d = A["L0_ffn_sw1"][:, c], A["L0_ffn_sw2"][:, c], A["L0_ffn_sw3"][c, :]
                sp.dma_start(w12[sl][:, 0], w1.rearrange("(k p) n -> p k n", p=P)).then_inc(wexp_loaded[sl], 16)
                sp.dma_start(w12[sl][:, 1], w2.rearrange("(k p) n -> p k n", p=P)).then_inc(wexp_loaded[sl], 16)
                sp.dma_start(w3[sl], w3d).then_inc(wexp_loaded[sl], 16)

            sp.wait_ge(s["pre_evac"], PRE_ACT)
            for m, v in enumerate((A["L0_ffn_sb3"], A["L1_ffn_b_base"])):
                sp.dma_start(bias_bc[:, m, :], v.rearrange("(a n) -> a n", a=1).broadcast_to([P, D])).then_inc(s["bias_loaded"], 16)
            for h in range(2):
                expert_load(h, h, h=h)
            with sp.Fori(0, E // 2) as i:
                for p in range(2):
                    expert_load(2 * i + p + 2, p, e=2 * i + p)

            sp.wait_ge(s["conv_in"], 1)
            with sp.Fori(0, B // 4) as i:
                for p in range(4):
                    sp.wait_ge(s["cslot_free"], 4 * i + p + 1)
                    sp.dma_start(slot[p][0:SP], ctx_dram[4 * i + p].rearrange("(j p) d -> p j d", p=SP)).then_inc(cslot_loaded[p], 16)
            for t in range(T):
                sp.wait_ge(s["fin_added"], t + 1)
                for j in range(2):
                    sp.dma_start(out[2 * t + j], xnat[R * j:R * j + C, t, :]).then_inc(s["stored"], 16)
            sp.wait_ge(s["stored"], 32 * T)

        @block.gpsimd
        def _(pool):
            pool.memset(xnat[:, :, :], 0.0).then_inc(s["zeroed"], 1)
            pool.memset(ones[:, :], 1.0).then_inc(s["zeroed"], 1)
            pool.memset(cpad[:, :, :], 0.0).then_inc(s["zeroed"], 1)
            pool.wait_ge(s["lnT_evac"], T)
            pool.memset(crucial, 0.0).then_inc(s["zeroed"], 1)

            pool.sem_inc(s["pool_sel"], 2)
            pool.wait_ge(s["zeroed"], 4)

            def split(b, p):
                pool.wait_ge(s["sel_ready"], b + 1)
                pool.sem_inc(s["pool_over"], 1)
                cols = bass.ds(b * R, C)
                pool.tensor_tensor(crucial[:, :, cols], sel[p][:, :, :], xnT[:, :, cols], ALU.mult).then_inc(s["pool_cr"], 1)
                pool.wait_ge(s["pool_cr"], b + 1)
                pool.sem_inc(s["pool_over"], 1)
                pool.tensor_tensor(xnT[:, :, cols], xnT[:, :, cols], crucial[:, :, cols], ALU.subtract).then_inc(s["pool_sel"], 1)

            with pool.Fori(0, T) as i:
                for p in range(2):
                    split(2 * i + p, p)
            pool.wait_ge(s["bias_loaded"], 32)
            for stage, which in ((2, 0), (4, 1)):
                pool.wait_ge(s["ln_ready"], stage * T)
                for t in range(T):
                    pool.tensor_tensor(xnat[:, t, :], xnat[:, t, :], bias_bc[:, which, :], ALU.add).then_inc(s["pool_bias"], 1)
                if which == 0:
                    pool.wait_ge(s["q_evac"], 2 * KD)
                    pool.wait_ge(s["qbk_done"], 1)
                    with pool.Fori(0, T // 2) as i:
                        for p in range(2):
                            pool.wait_ge(s["o_done"], 2 * i + p + 1)
                            pool.tensor_copy(qring[:, p], qT[:, :, bass.ds((2 * i + p) * P, P)]).then_inc(s["q_ring"], 1)

        @block.scalar
        def _(act):
            def load(dst, src):
                act.dma_start(dst, src).then_inc(s["w_loaded"], 16)

            def row(a):
                return a.rearrange("(a n) -> a n", a=1)

            load(wq, A["L1_xattn_Wq"].rearrange("(k p) n -> p k n", p=P))
            load(wk, A["L1_xattn_Wk"].rearrange("(k p) n -> p k n", p=P))
            load(wb, A["L1_ffn_W_base"].rearrange("(k p) n -> p k n", p=P))
            load(aw, A["L1_ffn_A_w"].rearrange("e r d -> (e r) d"))
            for c in range(KD):
                load(bw[:, c, :].rearrange("p (e r) -> p e r", e=E1),
                     A["L1_ffn_B_w"][:, c * P:(c + 1) * P, :].rearrange("e p r -> p e r"))
            load(rw[:, :, :], A["L0_ffn_router_w"].rearrange("(k p) n -> p k n", p=P))
            load(eb3[:, :], A["L0_ffn_eb3"])
            load(rb_bc[:, 0, :], row(A["L0_ffn_router_b"]).broadcast_to([P, E]))
            load(rb_bc[:, 1, :], row(A["L0_ffn_router_bias"]).broadcast_to([P, E]))
            load(cw_bc[:, 0:14], A["L0_xattn_conv_w"].rearrange("a c k -> a (c k)").broadcast_to([P, 14]))
            load(cw_bc[:, 14:15], row(A["L0_xattn_bn_gamma"]).broadcast_to([P, 1]))
            load(cw_bc[:, 15:16], row(A["L0_xattn_bn_beta"]).broadcast_to([P, 1]))
            load(bthr_bc[:, :], row(A["L1_ffn_b_thr"]).broadcast_to([P, 1]))
            act.sem_inc(s["tp_evac"], 4)

            def ln_root(stage):
                act.wait_ge(s["ln_var"], stage + 1)
                act.activation(lns[:, :], lnv[:, :], ACT.Sqrt).then_inc(s["ln_root"], 1)

            def ln_evac(stage):
                for t in range(T):
                    act.wait_ge(s["lnT_done"], stage * T + t + 1)
                    act.activation(xnT[:, :, t * P:(t + 1) * P],
                                   bank[4 + t % 4].rearrange("p (k n) -> p k n", k=KD), ACT.Copy).then_inc(s["lnT_evac"], 1)

            ln_root(0)
            ln_evac(0)

            def evac(b, p, g):
                act.wait_ge(s["tp_done"], b * KD * SG + g + 1)
                act.activation(ctxT[p][:, g // SG, (g % SG) * GW:(g % SG + 1) * GW],
                               bank[g % 4][:, 0:GW], ACT.Copy).then_inc(s["tp_evac"], 1)

            def search(b, p, last=False):
                for hp in range(8):
                    act.wait_ge(s["sums_done"], b * 8 + hp + 1)
                    act.activation(partial[hp % 2][0:SP, :], bank[4 + hp % 2][0:SP, 0:2 * P], ACT.Copy).then_inc(s["partial_ready"], 1)
                    if not last:
                        if hp == 0 and not (isinstance(b, int) and b == 0):
                            act.wait_ge(s["cmp_done"], b * 16)
                        for g in NEXT[hp]:
                            evac(b + 1, 1 - p, g)

            for g in range(KD * SG):
                evac(0, 0, g)
            search(0, 0)
            with act.Fori(0, T - 1) as i:
                for p in range(2):
                    search(2 * i + 1 + p, 1 - p)
            search(B - 1, 1, last=True)

            act.wait_ge(s["flag_ready"], 1)
            with act.If(act.value_load(flag[0:1, 0:1], min_val=0, max_val=1) > 0):
                act.sem_inc(s["fb_evac"], 4)
                with act.Fori(0, T) as i:
                    for p in range(2):
                        act.wait_ge(s["ctxT_free"], 2 * i + p + 1)
                        for g in range(KD * SG):
                            act.wait_ge(s["fb_tp_done"], (2 * i + p) * KD * SG + g + 1)
                            act.activation(ctxT[p][:, g // SG, (g % SG) * GW:(g % SG + 1) * GW],
                                           bank[g % 4][:, 0:GW], ACT.Copy).then_inc(s["fb_evac"], 1)

            n = [0]

            def pre(dst, src):
                act.activation(dst, src, ACT.Copy).then_inc(s["pre_evac"], 1)

            def pre_wait():
                n[0] += 1
                act.wait_ge(s["pre_done"], n[0])
                return bank[4 + (n[0] - 1) % 4]

            b = pre_wait()
            pre(agT[:, :, 0:P], b.rearrange("p (k n) -> p k n", k=KD))
            b = pre_wait()
            pre(bT[:, :], b)
            for k in range(KD):
                b = pre_wait()
                pre(wbT[:, k, :], b)
            b = pre_wait()
            pre(cols12[:, :], b[:, 0:12])
            pre(b12[:, 0, :], b[:, 16:16 + ES])
            pre(b12[:, 1, :], b[:, 48:48 + ES])
            pre(agT[:, :, P:P + E1], b[:, 80:80 + KD * E1].rearrange("p (k n) -> p k n", k=KD))
            pre(agT[:, :, P + E1], b[:, 0:4])
            act.wait_ge(s["bn_c"], 1)
            act.activation(sm[:, 4:5], sm[:, 3:4], ACT.Sqrt).then_inc(s["sig_out"], 1)
            act.wait_ge(s["sig_in"], 1)
            act.activation(zc[:, :], zc[:, :], ACT.Sigmoid).then_inc(s["sig_out"], 1)

            ln_root(1)
            ln_evac(1)

            act.wait_ge(s["gates_ready"], 1)
            act.activation(lg2[:, :, :], lg[:, :, :], ACT.Exp).then_inc(s["logits_exp"], 1)

            for k in range(KD):
                b = pre_wait()
                pre(mq[:, k, :], b)
            b = pre_wait()
            pre(uv[:, :, :], b[:, 0:8].rearrange("p (m k) -> p m k", m=2))
            pre(bqk[:, 5:6], b[:, 8:9])


            def expert(n, e):
                for h in range(2):
                    act.wait_ge(s["h_done"], 2 * n + h + 1)
                    act.sem_inc(s["act_over"], 1)
                    act.activation(silu[h], bank[2 * h], ACT.Silu,
                                   bias=b12[:, 0, e]).then_inc(s["silu_done"], 1)

            for h in range(2):
                expert(h, slice(E + h, E + h + 1))
            with act.Fori(0, E // 2) as i:
                for p in range(2):
                    expert(2 * i + p + 2, bass.ds(2 * i + p, 1))

            ln_root(2)
            ln_evac(2)
            for y in range(2 * KD):
                act.wait_ge(s["q_done"], y + 1)
                act.activation(qT[:, y // 2, (y % 2) * 512:(y % 2 + 1) * 512], bank[4 + y % 4], ACT.Identity,
                               bias=uv[:, 1, y // 2:y // 2 + 1]).then_inc(s["q_evac"], 1)

            with act.Fori(0, T // 2) as i:
                for p in range(2):
                    pair = 2 * i + p
                    for g in range(0, 24, 2):
                        act.wait_ge(s["ft_done"], pair * 24 + g + 1)
                        if g >= 8 or g < 8:
                            act.wait_ge(s["s_done"], pair * 6 + g // 4 + 1)
                        act.activation(FT[g // 4 % 2][:, g % 4, :], bank[3 + g % 4][:, 0:GW], ACT.Copy).then_inc(s["ft_act"], 1)
                    act.wait_ge(s["neg_bias"], pair + 1)
                    act.activation(probs.rearrange("p (g n) -> p g n", g=SG), PS3[:, :, 0:GW], ACT.Exp,
                                   bias=am[:, 2:3], scale=SCALE, accum_out=am[:, 3:4]).then_inc(s["exp_done"], 1)
                    for g in range(SG):
                        act.wait_ge(s["pt_done"], pair * SG + g + 1)
                        act.activation(probsT[0:SP, 4 * g:4 * g + 4, :], bank[3 + g][0:SP, :].rearrange("p (j n) -> p j n", j=4),
                                       ACT.Copy).then_inc(s["pt_evac"], 1)

            ln_root(3)
            ln_evac(3)
            act.wait_ge(s["w_ready"], 1)
            act.activation(lg2[:, :, 0:9], lg[:, :, 0:9], ACT.Exp).then_inc(s["exp9"], 1)
            for t in range(2):
                act.wait_ge(s["hwT_done"], t + 1)
                act.activation(hT[:, t * 512:(t + 1) * 512], bank[2 + t], ACT.Copy).then_inc(s["hwT_evac"], 1)

        @block.tensor
        def _(pe):
            pe.sem_inc(s["wexp_used"], 2)
            pe.sem_inc(s["cslot_free"], 4)
            pe.sem_inc(s["o_done"], 2)
            pe.sem_inc(s["s_done"], 2)

            def mm(o, l, r, first, last):
                return pe.matmul(o, l, r, start=first, stop=last)

            def ln_turn(stage):
                for t in range(T):
                    pe.wait_ge(s["ln_ready"], stage * T + t + 1)
                    if t >= 4:
                        pe.wait_ge(s["lnT_evac"], stage * T + t - 3)
                    for k in range(KD):
                        ins = pe.transpose(bank[4 + t % 4][:, k * P:(k + 1) * P], normed[:, t, k * P:(k + 1) * P], ident[:, :])
                    ins.then_inc(s["lnT_done"], 1)

            pe.wait_ge(s["const_loaded"], 64)
            ln_turn(0)

            def turn_ctx(b, p, g):
                pe.wait_ge(s["tp_evac"], b * KD * SG + g + 1)
                for q in range(4):
                    ins = pe.transpose(bank[g % 4][:, q * SP:(q + 1) * SP],
                                       slot[p][0:SP, 4 * (g % SG) + q, (g // SG) * P:(g // SG + 1) * P], ident[0:SP, 0:SP])
                ins.then_inc(s["tp_done"], 1)

            def search(b, p, nxt=None, last=False):
                for hp in range(8):
                    h = hp % 2
                    for j in range(2):
                        pe.wait_ge(s["cmp_done"], b * 16 + hp * 2 + j + 1)
                        for q in range(SJ):
                            ins = pe.matmul(bank[4 + h][0:SP, j * P:(j + 1) * P], above[2 * h + j][:, q * SP:(q + 1) * SP],
                                            identb[:, :], start=q == 0, stop=q == SJ - 1)
                    ins.then_inc(s["sums_done"], 1)
                    if not last:
                        for g in NEXT[hp]:
                            if g == 0:
                                pe.wait_ge(ctx_loaded[1 - p], nxt * 16)
                            turn_ctx(b + 1, 1 - p, g)
                    pe.wait_ge(s["partial_ready"], b * 8 + hp + 1)
                    for j in range(2):
                        ins = pe.matmul(bank[6 + h][:, j:j + 1], partial[h][0:SP, j * P:(j + 1) * P], onesb[0:SP, 0:1],
                                        start=True, stop=True)
                    ins.then_inc(s["counts_done"], 1)

            pe.wait_ge(ctx_loaded[0], 16)
            for g in range(KD * SG):
                turn_ctx(0, 0, g)
            pe.wait_ge(s["bf_ready"], 2)
            search(0, 0, 1)
            with pe.Fori(0, T - 1) as i:
                for p in range(2):
                    search(2 * i + 1 + p, 1 - p, i + 2)
            search(B - 1, 1, last=True)

            pe.wait_ge(s["full_ready"], 1)
            mm(bank[4][0:1, 0:1], ones[:, 0:1], fsum[:, :], True, True).then_inc(s["fsum_done"], 1)
            pe.wait_ge(s["flag_ready"], 1)
            with pe.If(pe.value_load(flag[0:1, 0:1], min_val=0, max_val=1) > 0):
                with pe.Fori(0, T) as i:
                    for p in range(2):
                        pe.wait_ge(fb_loaded[p], (i + 1) * 16)
                        for g in range(KD * SG):
                            pe.wait_ge(s["fb_evac"], (2 * i + p) * KD * SG + g + 1)
                            for q in range(4):
                                ins = pe.transpose(bank[g % 4][:, q * SP:(q + 1) * SP],
                                                   slot[p][0:SP, 4 * (g % SG) + q, (g // SG) * P:(g // SG + 1) * P], ident[0:SP, 0:SP])
                            ins.then_inc(s["fb_tp_done"], 1)

            n = [0]
            freed = [0, 0, 0, 0]

            def job(evacs, build):
                if n[0] >= 4:
                    pe.wait_ge(s["pre_evac"], freed[n[0] % 4])
                build(bank[4 + n[0] % 4]).then_inc(s["pre_done"], 1)
                n[0] += 1
                job.total += evacs
                freed[(n[0] - 1) % 4] = job.total
            job.total = 0

            def j_rows(b):
                pe.transpose(b[:, 0:12], rows12, ident[0:12, 0:12])
                for m in range(2):
                    pe.transpose(b[:, 16 + 32 * m:16 + 32 * m + ES], b12rows[:, m, :], ident[0:ES, 0:ES])
                for k in range(KD):
                    ins = pe.transpose(b[:, 80 + k * E1:80 + (k + 1) * E1], gaterows[:, k * P:(k + 1) * P], ident[0:E1, 0:E1])
                return ins

            def j_aw(b):
                for k in range(KD):
                    ins = pe.transpose(b[:, k * P:(k + 1) * P], aw[:, k * P:(k + 1) * P], ident[:, :])
                return ins

            def j_bw(b):
                for c in range(KD):
                    ins = pe.transpose(b[:, c * P:(c + 1) * P], bw[:, c, :], ident[:, :])
                return ins

            def j_wb(k):
                def build(b):
                    for c in range(KD):
                        ins = pe.transpose(b[:, c * P:(c + 1) * P], wb[:, c, k * P:(k + 1) * P], ident[:, :])
                    return ins
                return build

            def j_mq(x):
                def build(b):
                    for k in range(KD):
                        ins = mm(b, wq[:, k, x * P:(x + 1) * P], wk[:, k, :], k == 0, k == KD - 1)
                    return ins
                return build

            def j_uv(b):
                for m, (w, at) in enumerate(((wq, 4), (wk, 8))):
                    for x in range(KD):
                        for k in range(KD):
                            mm(b[:, 4 * m + x:4 * m + x + 1], w[:, k, x * P:(x + 1) * P], cols12[:, at + k:at + k + 1],
                               k == 0, k == KD - 1)
                pe.wait_ge(s["pre_cc"], 1)
                return mm(b[:, 8:9], ones[:, :], bqk[:, 4:5], True, True)

            pe.wait_ge(s["w_loaded"], W_LOADS * 16)
            job(1, j_aw)
            job(1, j_bw)
            for k in range(KD):
                job(1, j_wb(k))
            pe.wait_ge(s["rows_loaded"], ROW_LOADS * 16)
            job(5, j_rows)
            pe.wait_ge(s["pre_evac"], PRE_ACT - 6)
            pe.wait_ge(s["conv_in"], 1)
            for ch in range(2):
                ins = pe.transpose(bank[4][:, ch * P:(ch + 1) * P], st[:, ch].rearrange("p k a b -> p (k a b)"), ident[:, :])
            ins.then_inc(s["bn_a"], 1)
            pe.wait_ge(s["bn_b"], 1)
            mm(bank[5][:, 0:1], pathmean[:, :], sm[:, 0:1], True, True).then_inc(s["bn_a"], 1)
            pe.wait_ge(s["bn_b"], 2)
            mm(bank[5][:, 1:2], pathmean[:, :], sm[:, 2:3], True, True).then_inc(s["bn_a"], 1)
            pe.wait_ge(s["sig_out"], 2)
            pe.transpose(bank[6][:, 0:P], zc[:, :], ident[:, :]).then_inc(s["attT"], 1)

            pe.wait_ge(s["delta_ready"], 1)
            for t in range(T):
                if t >= 4:
                    pe.wait_ge(s["delta_added"], t - 3)
                for k in range(KD):
                    ins = pe.transpose(bank[t % 4][:, k * P:(k + 1) * P], xnT[:, k, t * P:(t + 1) * P], ident[:, :])
                ins.then_inc(s["delta_done"], 1)
            ln_turn(1)

            pe.wait_ge(s["lnT_evac"], 2 * T)
            for t in range(T):
                for k in range(KD):
                    ins = mm(bank[0][:, t * E:(t + 1) * E], xnT[:, k, t * P:(t + 1) * P], rw[:, k, :], k == 0, k == KD - 1)
            ins.then_inc(s["router_done"], 1)

            def expert(n, sl, turn):
                pe.wait_ge(wexp_loaded[sl], turn * 48)
                for h in range(2):
                    if not (isinstance(n, int) and n == 0):
                        pe.wait_ge(s["hT_ready"], 2 * n - 2 + h + 1)
                    for m in range(2):
                        for k in range(KD):
                            ins = mm(bank[2 * h + m], w12[sl][:, m, k, :], xnT[:, k, h * 512:(h + 1) * 512], k == 0, k == KD - 1)
                    ins.then_inc(s["h_done"], 1)
                for t in range(T):
                    if t % 4 == 0:
                        pe.wait_ge(s["hT_ready"], 2 * n + t // 4 + 1)
                    if not (isinstance(n, int) and n == 0 and t < 4):
                        pe.wait_ge(s["y_added"], n * T + t - 3)
                    ins = mm(bank[4 + t % 4], hT[:, t * P:(t + 1) * P], w3[sl], True, True)
                    ins.then_inc(s["y_done"], 1)
                pe.wait_ge(s["y_done"], (n + 1) * T)
                pe.sem_inc(s["wexp_used"], 1)

            pe.wait_ge(s["logits_exp"], 1)
            for k in range(KD):
                job(1, j_mq(k))
            job(2, j_uv)
            assert job.total == PRE_ACT

            for h in range(2):
                expert(h, h, 1)
            with pe.Fori(0, E // 2) as i:
                for p in range(2):
                    expert(2 * i + p + 2, p, i + 2)

            for t in range(T):
                pe.wait_ge(s["gates_ready"], 2)
                pe.wait_ge(s["hT_ready"], 2 * ES)
                ins = pe.transpose(bank[t // 4][0:E, (t % 4) * P:(t % 4 + 1) * P], gate[:, t, 0:E], ident[:, :])
            ins.then_inc(s["gateT_done"], 1)
            pe.wait_ge(s["gateT_evac"], 2)
            for t in range(T):
                pe.wait_ge(s["y_added"], ES * T + t - 3)
                mm(bank[4 + t % 4], gateT[:, t * P:(t + 1) * P], eb3[:, :], True, True).then_inc(s["y_done"], 1)
            ln_turn(2)

            pe.wait_ge(s["lnT_evac"], 3 * T)
            for y in range(2 * KD):
                if y >= 4:
                    pe.wait_ge(s["q_evac"], y - 3)
                for k in range(KD):
                    ins = mm(bank[4 + y % 4], mq[:, k, (y // 2) * P:(y // 2 + 1) * P],
                             xnT[:, k, (y % 2) * 512:(y % 2 + 1) * 512], k == 0, k == KD - 1)
                ins.then_inc(s["q_done"], 1)
            for t in range(T):
                for k in range(KD):
                    ins = mm(bank[0][:, t:t + 1], xnT[:, k, t * P:(t + 1) * P], uv[:, 0, k:k + 1], k == 0, k == KD - 1)
            ins.then_inc(s["qbk_done"], 1)
            pe.wait_ge(s["qbk_ready"], 1)
            pe.wait_ge(s["q_evac"], 2 * KD)

            def turn(pair, sl, u):
                g, a = u // 2, u % 2
                for k in range(KD):
                    nn = 4 * u + k
                    w, own = ("ft_act", "ft_dve")[nn % 2], nn // 2
                    pe.wait_ge(s[w], pair * 12 + own + 1)
                    for q in range(4):
                        ins = pe.transpose(bank[3 + nn % 4][:, q * SP:(q + 1) * SP],
                                           slot[sl + a][0:SP, 4 * g + q, k * P:(k + 1) * P], ident[0:SP, 0:SP])
                    ins.then_inc(s["ft_done"], 1)

            def score(pair, p, u):
                g, a = u // 2, u % 2
                pe.wait_ge(s["ft_act"], pair * 12 + 2 * (u + 1) + 2)
                pe.wait_ge(s["ft_dve"], pair * 12 + 2 * (u + 1) + 2)
                for k in range(KD):
                    ins = mm(bank[g][R * a:R * a + R, 0:GW], qring[:, p, k, R * a:R * a + R], FT[u % 2][:, k, :], k == 0, k == KD - 1)
                ins.then_inc(s["s_done"], 1)

            pe.sem_inc(s["ft_act"], 2)
            pe.sem_inc(s["ft_dve"], 2)
            pe.sem_inc(s["exp_done"], 1)
            pe.sem_inc(s["o_added"], 1)
            pe.sem_inc(s["pt_evac"], 1)
            with pe.Fori(0, T // 2) as i:
                for p in range(2):
                    pair = 2 * i + p
                    for a in range(2):
                        pe.wait_ge(cslot_loaded[2 * p + a], (i + 1) * 16)
                    pe.wait_ge(s["q_ring"], pair + 1)
                    pe.wait_ge(s["pt_evac"], pair * SG + 1)
                    turn(pair, 2 * p, 0)
                    for u in range(6):
                        if u < 5:
                            turn(pair, 2 * p, u + 1)
                        if u == 0:
                            pe.wait_ge(s["exp_done"], pair + 1)
                        score(pair, p, u)
                    pe.wait_ge(s["exp_done"], pair + 2)
                    pe.wait_ge(s["ft_act"], (pair + 1) * 12 + 2)
                    pe.wait_ge(s["ft_dve"], (pair + 1) * 12 + 2)
                    for g in range(SG):
                        for q in range(4):
                            ins = pe.transpose(bank[3 + g][0:SP, q * P:(q + 1) * P], probs[:, (4 * g + q) * SP:(4 * g + q + 1) * SP], ident[:, :])
                        ins.then_inc(s["pt_done"], 1)
                    pe.wait_ge(s["o_added"], pair + 1)
                    pe.wait_ge(s["pt_evac"], (pair + 1) * SG + 1)
                    for j in range(SJ):
                        for a in range(2):
                            ins = mm(bank[7][R * a:R * a + R, :], probsT[0:SP, j, R * a:R * a + R], slot[2 * p + a][0:SP, j, :],
                                     j == 0, j == SJ - 1)
                    ins.then_inc(s["o_done"], 1)
                    pe.wait_ge(s["o_done"], pair + 3)
                    pe.sem_inc(s["cslot_free"], 2)

            ln_turn(3)
            pe.wait_ge(s["lnT_evac"], 4 * T)
            for t in range(T):
                for k in range(KD):
                    ins = mm(bank[0][:, t * 9:(t + 1) * 9], xnT[:, k, t * P:(t + 1) * P], agT[:, k, P:P + 9], k == 0, k == KD - 1)
            ins.then_inc(s["gl_done"], 1)
            for t in range(T):
                for k in range(KD):
                    ins = mm(bank[2 + t // 4][:, (t % 4) * P:(t % 4 + 1) * P], xnT[:, k, t * P:(t + 1) * P], agT[:, k, 0:P], k == 0, k == KD - 1)
                if t % 4 == 3:
                    ins.then_inc(s["h9_done"], 1)
            for t in range(T):
                if t % 4 == 0:
                    pe.wait_ge(s["hw_ready"], t // 4 + 1)
                ins = pe.transpose(bank[2 + t // 4][:, (t % 4) * P:(t % 4 + 1) * P], pairs_hw(t), ident[:, :])
                if t % 4 == 3:
                    ins.then_inc(s["hwT_done"], 1)
            for t in range(T):
                if t >= 4:
                    pe.wait_ge(s["fin_added"], t - 3)
                for k in range(KD):
                    mm(bank[4 + t % 4], xnT[:, k, t * P:(t + 1) * P], wbT[:, k, :], k == 0, False)
                pe.wait_ge(s["hwT_evac"], t // 4 + 1)
                mm(bank[4 + t % 4], hT[:, t * P:(t + 1) * P], bT[:, :], False, True).then_inc(s["fin_done"], 1)

        @block.vector
        def _(dve):
            ln = Chain(dve, s["dve_ln"])

            def layernorm(stage):
                for t in range(T):
                    ln.step(dve.bn_stats(bnst[:, t, :], xnat[:, t, :]))
                ln.settle()
                for t in range(T):
                    ln.step(dve.bn_aggr(bnmv[:, t, :], bnst[:, t, :]))
                ln.settle()
                dve.tensor_scalar(lnv[:, :], bnmv[:, :, 1], EPS, None, ALU.add).then_inc(s["ln_var"], 1)
                dve.wait_ge(s["ln_root"], stage + 1)
                ln.link(dve.reciprocal(lnr[:, :], lns[:, :]))
                for t in range(T):
                    dve.tensor_scalar(normed[:, t, :], xnat[:, t, :], bnmv[:, t, 0:1], lnr[:, t:t + 1],
                                      ALU.subtract, ALU.mult).then_inc(s["ln_ready"], 1)

            dve.sem_inc(s["ctxT_free"], 2)
            dve.wait_ge(s["zeroed"], 2)
            dve.wait_ge(s["x_loaded"], 32)
            layernorm(0)

            dve.wait_ge(s["lnT_evac"], T)
            dve.wait_ge(s["zeroed"], 4)
            dve.wait_ge(s["const_loaded"], 64)

            ini = Chain(dve, s["pre_dve"])
            dve.tensor_copy(identb[:, :], ident[:, :]).then_inc(s["bf_ready"], 1)
            dve.memset(onesb[:, :], 1.0).then_inc(s["bf_ready"], 1)
            ini.link(dve.memset(full[:, :], 0.0))

            def bc(ap, n):
                return ap.unsqueeze(2).broadcast_to([P, KD, n])

            def over_wait():
                dve.sem_inc(s["wait_over"], 1)

            def select(ch, dst, T1, n_above):
                thr = bc(T1, C)
                ch.step(dve.tensor_scalar(s1[:, :], n_above, -1.0, float(TOPK), ALU.mult, ALU.add))
                ch.link(dve.tensor_tensor(f1[:, :, :], cand[:, :, :], thr, ALU.is_equal))
                ch.link(dve.tensor_tensor_scan(f2[:, :, :].rearrange("p k c -> p (k c)"), reset[:, :],
                                               f1[:, :, :].rearrange("p k c -> p (k c)"), 0.0, ALU.mult, ALU.add))
                ch.link(dve.tensor_tensor(f2[:, :, :], f2[:, :, :], f1[:, :, :], ALU.mult))
                ch.step(dve.tensor_tensor(f1[:, :, :], cand[:, :, :], thr, ALU.is_ge))
                ch.link(dve.tensor_tensor(f2[:, :, :], f2[:, :, :], bc(s1[:, :], C), ALU.is_le))
                return dve.tensor_tensor(dst, f1[:, :, :], f2[:, :, :], ALU.mult)

            def search(b, p):
                ch = Chain(dve, s["dve_s"], b * SEARCH_STEPS)
                dve.wait_ge(s["tp_evac"], (b + 1) * KD * SG + 4)
                ch.link(dve.tensor_copy(cand[:, :, :], ctxT[p][:, :, 0:C]))
                over_wait()
                for k in range(KD):
                    ch.step(dve.max(sorted15[:, k, 0:8], cand[:, k, :]))
                ch.settle()
                over_wait()
                for k in range(KD):
                    ch.step(dve.match_replace(out=f1[:, k, :], in_to_replace=sorted15[:, k, 0:8], in_values=cand[:, k, :], imm_value=-BIG))
                ch.settle()
                over_wait()
                for k in range(KD):
                    ch.step(dve.max(sorted15[:, k, 8:16], f1[:, k, :]))
                ch.step(dve.memset(thr_n[:, 0, :], BIG))
                ch.step(dve.memset(thr_n[:, 1, :], float(TOPK)))
                ch.settle()

                def compare(n, h):
                    w = 7 >> n
                    for k in (2 * h, 2 * h + 1):
                        dve.tensor_scalar(above[k], ctxT[p][:, k, :], sorted15[:, k, w:w + 1], None, ALU.is_gt).then_inc(s["cmp_done"], 1)

                def step(n, h):
                    w = 7 >> n
                    ks = slice(2 * h, 2 * h + 2)
                    counts = bank[6 + h][:, 0:2]
                    dve.wait_ge(s["counts_done"], b * 8 + 2 * n + h + 1)
                    ch.link(dve.tensor_scalar(okay[:, ks], counts, TOPK - 0.5, None, ALU.is_lt))
                    over_wait()
                    ch.step(dve.copy_predicated(thr_n[:, 0, ks], okay[:, ks], sorted15[:, ks, w]))
                    ch.step(dve.copy_predicated(thr_n[:, 1, ks], okay[:, ks], counts))
                    if n < 3:
                        ch.step(dve.copy_predicated(sorted15[:, ks, 0:w], okay[:, ks].unsqueeze(2).broadcast_to([P, 2, w]),
                                                    sorted15[:, ks, w + 1:2 * w + 1]))
                    ch.settle()

                compare(0, 0)
                compare(0, 1)
                for n in range(4):
                    for h in range(2):
                        step(n, h)
                        if n < 3:
                            compare(n + 1, h)
                ch.link(dve.tensor_tensor(f1[:, :, 0], sorted15[:, :, 14], thr_n[:, 0, :], ALU.is_ge))
                ch.link(dve.tensor_tensor(full[:, :], full[:, :], f1[:, :, 0], ALU.add))
                dve.wait_ge(s["pool_sel"], b + 1)
                select(ch, sel[p][:, :, :], thr_n[:, 0, :], thr_n[:, 1, :]).then_inc(s["sel_ready"], 1)
                dve.wait_ge(s["sel_ready"], b + 1)
                assert ch.n == SEARCH_STEPS, ch.n

            search(0, 0)
            with dve.Fori(0, T - 1) as i:
                for p in range(2):
                    search(2 * i + 1 + p, 1 - p)
            search(B - 1, 1)
            dve.wait_ge(s["pool_sel"], B + 2)
            ini.link(dve.tensor_reduce(fsum[:, :], full[:, :], AX.X, ALU.add))
            dve.sem_inc(s["full_ready"], 1)
            dve.wait_ge(s["fsum_done"], 1)
            dve.tensor_scalar(flag[:, :], bank[4][0:1, 0:1], 0.5, None, ALU.is_gt).then_inc(s["flag_ready"], 1)
            dve.wait_ge(s["flag_ready"], 1)

            with dve.If(dve.value_load(flag[0:1, 0:1], min_val=0, max_val=1) > 0):
                fb0 = Chain(dve, s["fb_done"])
                fb0.link(dve.tensor_tensor(xnT[:, :, :], xnT[:, :, :], crucial, ALU.add))
                with dve.Fori(0, T) as i:
                    for p in range(2):
                        b = 2 * i + p
                        ch = Chain(dve, s["dve_fb"], b * FALLBACK_STEPS)
                        dve.wait_ge(s["fb_evac"], (b + 1) * KD * SG + 4)
                        ch.link(dve.tensor_copy(cand[:, :, :], ctxT[p][:, :, 0:C]))
                        for r in range(NS // 8):
                            over_wait()
                            for k in range(KD):
                                ch.step(dve.max(top[:, k, 8 * r:8 * r + 8], ctxT[p][:, k, :]))
                            ch.settle()
                            if r < NS // 8 - 1:
                                over_wait()
                                for k in range(KD):
                                    ch.step(dve.match_replace(out=ctxT[p][:, k, :], in_to_replace=top[:, k, 8 * r:8 * r + 8],
                                                              in_values=ctxT[p][:, k, :], imm_value=-BIG))
                                ch.settle()
                        dve.sem_inc(s["ctxT_free"], 1)
                        thr = top[:, :, TOPK - 1]
                        ch.link(dve.tensor_tensor(f2[:, :, 0:TOPK], top[:, :, 0:TOPK], bc(thr, TOPK), ALU.is_gt))
                        ch.link(dve.tensor_reduce(thr_n[:, 1, :], f2[:, :, 0:TOPK], AX.X, ALU.add))
                        ch.link(select(ch, sel[p][:, :, :], thr, thr_n[:, 1, :]))
                        cols = bass.ds(b * R, C)
                        ch.link(dve.tensor_tensor(crucial[:, :, cols], sel[p][:, :, :], xnT[:, :, cols], ALU.mult))
                        ch.link(dve.tensor_tensor(xnT[:, :, cols], xnT[:, :, cols], crucial[:, :, cols], ALU.subtract))
                        assert ch.n == FALLBACK_STEPS, ch.n

            dve.sem_inc(s["searched"], 1)
            rd = Chain(dve, s["dve_red"])
            for path, a in ((0, crucial), (1, xnT)):
                for k in range(KD):
                    v = a[:, k, :].rearrange("p (b c) -> p b c", b=B)[:, :, 0:C]
                    for what, op in ((0, ALU.max), (1, ALU.add)):
                        rd.step(dve.tensor_reduce(st[:, what, k, path, :], v, AX.X, op))
            rd.settle()

            dve.wait_ge(s["pre_evac"], 7)
            rd.link(dve.tensor_tensor(bqk[:, 0:KD], cols12[:, 4:8], cols12[:, 8:12], ALU.mult))
            dve.tensor_reduce(bqk[:, 4:5], bqk[:, 0:KD], AX.X, ALU.add).then_inc(s["pre_cc"], 1)

            cv = Chain(dve, s["dve_conv"])
            cv.step(dve.tensor_scalar(st[:, 1, :, 0, :], st[:, 1, :, 0, :], 1.0 / C, float(C / TOPK), ALU.mult, ALU.mult))
            cv.link(dve.tensor_scalar(st[:, 1, :, 1, :], st[:, 1, :, 1, :], 1.0 / C, float(C / (C - TOPK)), ALU.mult, ALU.mult))
            dve.sem_inc(s["conv_in"], 1)
            dve.wait_ge(s["bn_a"], 1)
            turned = bank[4][:, 0:2 * P].rearrange("p (c n) -> p c n", c=2)
            cv.step(dve.tensor_copy(cpad[:, :, 3:3 + P], turned))
            for q in range(KD):
                here = slice(32 * q, 32 * q + 32)
                if q > 0:
                    cv.step(dve.tensor_copy(cpad[here, :, 0:3], turned[32 * q - 32:32 * q, :, P - 3:P]))
                if q < KD - 1:
                    cv.step(dve.tensor_copy(cpad[here, :, P + 3:P + 6], turned[32 * q + 32:32 * q + 64, :, 0:3]))
            cv.settle()
            dve.wait_ge(s["w_loaded"], W_LOADS * 16)
            for n in range(14):
                win = cpad[:, n // 7, n % 7:n % 7 + P]
                if n == 0:
                    cv.link(dve.tensor_scalar(zc[:, :], win, cw_bc[:, 0:1], None, ALU.mult))
                else:
                    cv.link(dve.scalar_tensor_tensor(out=zc[:, :], in0=win, scalar=cw_bc[:, n:n + 1], in1=zc[:, :],
                                                     op0=ALU.mult, op1=ALU.add))
            cv.link(dve.bn_stats(bnst[:, 0, :], zc[:, :]))
            cv.link(dve.bn_aggr(sm[:, 0:2], bnst[:, 0, :]))
            dve.sem_inc(s["bn_b"], 1)
            dve.wait_ge(s["bn_a"], 2)
            cv.link(dve.tensor_tensor(sm[:, 2:3], sm[:, 0:1], bank[5][:, 0:1], ALU.subtract))
            cv.step(dve.tensor_copy(sm[:, 6:7], bank[5][:, 0:1]))
            cv.link(dve.tensor_tensor(sm[:, 2:3], sm[:, 2:3], sm[:, 2:3], ALU.mult))
            cv.link(dve.tensor_tensor(sm[:, 2:3], sm[:, 2:3], sm[:, 1:2], ALU.add))
            dve.sem_inc(s["bn_b"], 1)
            dve.wait_ge(s["bn_a"], 3)
            cv.link(dve.tensor_scalar(sm[:, 3:4], bank[5][:, 1:2], EPS, None, ALU.add))
            dve.sem_inc(s["bn_c"], 1)
            dve.wait_ge(s["sig_out"], 1)
            cv.link(dve.reciprocal(sm[:, 5:6], sm[:, 4:5]))
            cv.link(dve.tensor_scalar(zc[:, :], zc[:, :], sm[:, 6:7], sm[:, 5:6], ALU.subtract, ALU.mult))
            cv.link(dve.tensor_scalar(zc[:, :], zc[:, :], cw_bc[:, 14:15], cw_bc[:, 15:16], ALU.mult, ALU.add))
            cv.link(dve.tensor_scalar(zc[:, :], zc[:, :], 0.0, None, ALU.max))
            dve.sem_inc(s["sig_in"], 1)
            dve.wait_ge(s["attT"], 1)
            cv.link(dve.tensor_copy(attA[:, :], bank[6][:, 0:P]))
            def gates_of(k, path):
                return attA[:, (2 * k + path) * B:(2 * k + path + 1) * B].unsqueeze(2).broadcast_to([P, B, R])

            for k in range(KD):
                for path, a in ((1, xnT), (0, crucial)):
                    v = a[:, k, :].rearrange("p (b c) -> p b c", b=B)
                    cv.step(dve.tensor_tensor(v, v, gates_of(k, path), ALU.mult))
            cv.settle()
            for k in range(KD):
                cv.step(dve.tensor_tensor(xnT[:, k, :], xnT[:, k, :], crucial[:, k, :], ALU.add))
            cv.settle()
            dve.sem_inc(s["delta_ready"], 1)
            for t in range(T):
                dve.wait_ge(s["delta_done"], t + 1)
                dve.tensor_tensor(xnat[:, t, :], xnat[:, t, :], bank[t % 4], ALU.add).then_inc(s["delta_added"], 1)
            dve.wait_ge(s["delta_added"], T)
            layernorm(1)

            rt = Chain(dve, s["dve_rt"])
            dve.wait_ge(s["router_done"], 1)
            rt.step(dve.memset(gate[:, :, E:ES], 1.0))
            logits = bank[0][:, 0:T * E].rearrange("p (t e) -> p t e", t=T)

            def over(ap, n):
                return ap.unsqueeze(2).broadcast_to([P, ap.shape[1], n])

            def per_tile(ap):
                return ap.unsqueeze(1).broadcast_to([P, T, ap.shape[1]])

            rt.link(dve.tensor_tensor(lg[:, :, :], logits, per_tile(rb_bc[:, 0, :]), ALU.add))
            rt.link(dve.tensor_reduce(tv[:, :, 0], lg[:, :, :], AX.X, ALU.max))
            rt.link(dve.tensor_tensor(lg[:, :, :], lg[:, :, :], over(tv[:, :, 0], E), ALU.subtract))
            dve.sem_inc(s["gates_ready"], 1)
            dve.wait_ge(s["logits_exp"], 1)
            rt.link(dve.tensor_reduce(tv[:, :, 1], lg2[:, :, :], AX.X, ALU.add))
            rt.link(dve.reciprocal(tv[:, :, 2], tv[:, :, 1]))
            rt.link(dve.tensor_tensor(lg[:, :, :], lg2[:, :, :], over(tv[:, :, 2], E), ALU.mult))
            rt.link(dve.tensor_tensor(lg[:, :, :], lg[:, :, :], per_tile(rb_bc[:, 1, :]), ALU.add))
            rt.link(dve.tensor_reduce(gm[:, :, :], lg[:, :, :].rearrange("p t (g m) -> p t g m", g=GR), AX.X, ALU.max))

            def ranks(v, n, low, q, q2, res):
                for t in range(T):
                    mine = v[:, t, :].unsqueeze(2).broadcast_to([P, n, n])
                    other = v[:, t, :].unsqueeze(1).broadcast_to([P, n, n])
                    rt.step(dve.tensor_tensor(q(t), other, mine, ALU.is_gt))
                    rt.link(dve.tensor_tensor(q2(t), other, mine, ALU.is_equal))
                    rt.link(dve.tensor_tensor(q2(t), q2(t), low, ALU.mult))
                    rt.link(dve.tensor_tensor(q(t), q(t), q2(t), ALU.add))
                    rt.link(dve.tensor_reduce(res[:, t, :], q(t), AX.X, ALU.add))

            dve.wait_ge(s["pre_evac"], PRE_ACT)

            def sq(tile, n):
                return lambda t: tile[:, t, :].rearrange("p (a b) -> p a b", a=n)

            ranks(gm, GR, lower[:, 0:GR * GR].rearrange("p (a b) -> p a b", a=GR), sq(gq, GR), sq(gq2, GR), tv)
            rt.link(dve.tensor_scalar(gm[:, :, :], tv[:, :, :], 2.0, None, ALU.is_lt))
            keep = gm[:, :, :].unsqueeze(3).broadcast_to([P, T, GR, E // GR])
            sc4 = lg2[:, :, :].rearrange("p t (g m) -> p t g m", g=GR)
            rt.link(dve.tensor_tensor(sc4, lg[:, :, :].rearrange("p t (g m) -> p t g m", g=GR), keep, ALU.mult))
            rt.link(dve.tensor_scalar(gm[:, :, :], gm[:, :, :], -1.0, BIG, ALU.add, ALU.mult))
            rt.link(dve.tensor_tensor(sc4, sc4, keep, ALU.add))
            big16 = lower[:, GR * GR:].rearrange("p (a b) -> p a b", a=E)
            ranks(lg2, E, big16, lambda t: pair2[:, 0:E * E].rearrange("p (a b) -> p a b", a=E), lambda t: pair2[:, E * E:2 * E * E].rearrange("p (a b) -> p a b", a=E), gate[:, :, 0:E])
            rt.link(dve.tensor_scalar(gate[:, :, 0:E], gate[:, :, 0:E], 2.0, None, ALU.is_lt))
            rt.link(dve.tensor_tensor(gate[:, :, 0:E], gate[:, :, 0:E], lg[:, :, :], ALU.mult))
            dve.sem_inc(s["gates_ready"], 1)

            def expert(n, e):
                for h in range(2):
                    dve.wait_ge(s["silu_done"], 2 * n + h + 1)
                    dve.scalar_tensor_tensor(out=hT[:, h * 512:(h + 1) * 512], in0=bank[2 * h + 1], scalar=b12[:, 1, e],
                                             in1=silu[h], op0=ALU.add, op1=ALU.mult).then_inc(s["hT_ready"], 1)
                for t in range(T):
                    dve.wait_ge(s["y_done"], n * T + t + 1)
                    if t == 0:
                        dve.wait_ge(s["y_added"], n * T)
                    dve.scalar_tensor_tensor(out=xnat[:, t, :], in0=bank[4 + t % 4], scalar=gate[:, t, e],
                                             in1=xnat[:, t, :], op0=ALU.mult, op1=ALU.add).then_inc(s["y_added"], 1)

            dve.wait_ge(s["pool_bias"], T)
            for h in range(2):
                expert(h, slice(E + h, E + h + 1))
            with dve.Fori(0, E // 2) as i:
                for p in range(2):
                    expert(2 * i + p + 2, bass.ds(2 * i + p, 1))
            dve.wait_ge(s["gateT_done"], 1)
            for t in range(2):
                dve.tensor_copy(gateT[:, t * 512:(t + 1) * 512], bank[t][0:E, :]).then_inc(s["gateT_evac"], 1)
            for t in range(T):
                dve.wait_ge(s["y_done"], ES * T + t + 1)
                dve.tensor_tensor(xnat[:, t, :], xnat[:, t, :], bank[4 + t % 4], ALU.add).then_inc(s["y_added"], 1)
            dve.wait_ge(s["y_added"], (ES + 1) * T)
            layernorm(2)

            dve.wait_ge(s["qbk_done"], 1)
            dve.tensor_scalar(qbk[:, :], bank[0][:, 0:T], bqk[:, 5:6], None, ALU.add).then_inc(s["qbk_ready"], 1)
            dve.wait_ge(s["qbk_ready"], 1)

            with dve.Fori(0, T // 2) as i:
                for p in range(2):
                    pair = 2 * i + p
                    at = Chain(dve, s["dve_at"], pair * 3)
                    for g in range(1, 24, 2):
                        dve.wait_ge(s["ft_done"], pair * 24 + g + 1)
                        dve.wait_ge(s["s_done"], pair * 6 + g // 4 + 1)
                        dve.tensor_copy(FT[g // 4 % 2][:, g % 4, :], bank[3 + g % 4][:, 0:GW]).then_inc(s["ft_dve"], 1)
                    dve.wait_ge(s["s_done"], (pair + 1) * 6 + 2)
                    at.link(dve.tensor_reduce(am[:, 0:1], PS3[:, :, 0:GW], AX.XY, ALU.max))
                    q = qbk[:, bass.ds(pair, 1)]
                    at.link(dve.tensor_scalar(am[:, 1:2], am[:, 0:1], q, None, ALU.add))
                    dve.tensor_scalar(am[:, 2:3], am[:, 1:2], q, -SCALE, ALU.subtract, ALU.mult).then_inc(s["neg_bias"], 1)
                    dve.wait_ge(s["exp_done"], pair + 2)
                    at.link(dve.reciprocal(am[:, 4:5], am[:, 3:4]))
                    dve.wait_ge(s["o_done"], pair + 3)
                    xr = xnat[:, bass.ds(pair, 1), :]
                    dve.scalar_tensor_tensor(out=xr, in0=bank[7].unsqueeze(1), scalar=am[:, 4:5], in1=xr,
                                             op0=ALU.mult, op1=ALU.add).then_inc(s["o_added"], 1)
            dve.wait_ge(s["o_added"], T + 1)
            layernorm(3)

            fc = Chain(dve, s["dve_fin"])
            dve.wait_ge(s["gl_done"], 1)
            g9 = bank[0][:, 0:T * 9].rearrange("p (t e) -> p t e", t=T)
            fc.link(dve.tensor_reduce(tv[:, :, 0], g9[:, :, 0:E1], AX.X, ALU.max))
            fc.step(dve.tensor_tensor(lg[:, :, 0:E1], g9[:, :, 0:E1], over(tv[:, :, 0], E1), ALU.subtract))
            fc.link(dve.tensor_scalar(lg[:, :, 8:9], g9[:, :, 8:9], bthr_bc[:, 0:1], -1.0, ALU.add, ALU.mult))
            dve.sem_inc(s["w_ready"], 1)
            dve.wait_ge(s["exp9"], 1)
            fc.step(dve.tensor_reduce(tv[:, :, 1], lg2[:, :, 0:E1], AX.X, ALU.add))
            fc.link(dve.tensor_scalar(tv[:, :, 2:3], lg2[:, :, 8:9], 1.0, None, ALU.add))
            fc.link(dve.reciprocal(tv[:, :, 1:3], tv[:, :, 1:3]))
            fc.step(dve.tensor_tensor(lg[:, :, 0:E1], lg2[:, :, 0:E1], over(tv[:, :, 1], E1), ALU.mult))
            fc.link(dve.tensor_scalar(tv[:, :, 3], tv[:, :, 2], 0.125, None, ALU.mult))
            fc.link(dve.tensor_tensor(lg[:, :, 0:E1], lg[:, :, 0:E1], over(tv[:, :, 3], E1), ALU.subtract))
            fc.link(dve.tensor_scalar(lg[:, :, 0:E1], lg[:, :, 0:E1], 0.0, None, ALU.max))
            fc.link(dve.tensor_reduce(tv[:, :, 0], lg[:, :, 0:E1], AX.X, ALU.add))
            fc.link(dve.tensor_scalar(tv[:, :, 1], tv[:, :, 0], 0.0, None, ALU.is_equal))
            fc.link(dve.tensor_tensor(tv[:, :, 0], tv[:, :, 0], tv[:, :, 1], ALU.add))
            fc.link(dve.reciprocal(tv[:, :, 1], tv[:, :, 0]))
            fc.link(dve.tensor_tensor(lg[:, :, 0:E1], lg[:, :, 0:E1], over(tv[:, :, 1], E1), ALU.mult))
            fc.link(dve.tensor_scalar(lg2[:, :, 0:E1], lg[:, :, 0:E1], 2.0, None, ALU.mult))
            for h in range(2):
                dve.wait_ge(s["h9_done"], h + 1)
                for t in range(4 * h, 4 * h + 4):
                    v = bank[2 + h][:, (t % 4) * P:(t % 4 + 1) * P].rearrange("p (e r) -> p e r", e=E1)
                    w = lg2[:, t, 0:E1].unsqueeze(2).broadcast_to([P, E1, RK])
                    fc.step(dve.tensor_tensor(pairs_hw(t).rearrange("p (e r) -> p e r", e=E1), v, w, ALU.mult))
                fc.settle()
                dve.sem_inc(s["hw_ready"], 1)
            dve.wait_ge(s["pool_bias"], 2 * T)
            for t in range(T):
                dve.wait_ge(s["fin_done"], t + 1)
                dve.tensor_tensor(xnat[:, t, :], xnat[:, t, :], bank[4 + t % 4], ALU.add).then_inc(s["fin_added"], 1)


PRE_ACT = 5 + 1 + 1 + 4 + 4 + 2
SEARCH_STEPS = 1 + 12 + 2 + 2 * (4 * 3 + 3) + 2 + 6
FALLBACK_STEPS = 1 + 20 + 16 + 2 + 7 + 2
NEXT = [[0, 1], [2], [3, 4], [5], [6, 7], [8], [9, 10], [11]]
W_LOADS = 4 + 4 + 1 + 1 + 2 + 3 + 1
ROW_LOADS = 3 + 1 + 4


_INS = ['x', 'ctx_4096', 'L0_xattn_conv_w', 'L0_xattn_bn_gamma', 'L0_xattn_bn_beta', 'L0_ffn_router_w', 'L0_ffn_router_b',
        'L0_ffn_router_bias', 'L0_ffn_ew1', 'L0_ffn_eb1', 'L0_ffn_ew2', 'L0_ffn_eb2', 'L0_ffn_ew3', 'L0_ffn_eb3',
        'L0_ffn_sw1', 'L0_ffn_sb1', 'L0_ffn_sw2', 'L0_ffn_sb2', 'L0_ffn_sw3', 'L0_ffn_sb3', 'L1_xattn_Wq', 'L1_xattn_bq',
        'L1_xattn_Wk', 'L1_xattn_bk', 'L1_ffn_W_base', 'L1_ffn_b_base', 'L1_ffn_W_gate', 'L1_ffn_W_thr', 'L1_ffn_b_thr',
        'L1_ffn_A_w', 'L1_ffn_B_w']


def _constants():
    import numpy as np
    p = np.arange(128)
    path = (p // 16) % 2
    low = [np.tril(np.ones((n, n), np.float32), -1).reshape(-1) for n in (4, 16)]
    reset = np.ones((4, 56), np.float32)
    reset[:, 0] = 0.0
    return {"ident": np.eye(128, dtype=np.float32),
            "pathmean": (path[:, None] == path[None, :]).astype(np.float32) / 64,
            "lower": np.tile(np.concatenate(low), (128, 1)),
            "reset": np.tile(reset.reshape(-1), (128, 1))}


def kernel(**inputs):
    import numpy as _np
    import concourse.bacc as _bacc
    from concourse import mybir as _mybir
    from concourse.bass_utils import run_bass_kernel_spmd as _run

    nc = _bacc.Bacc("TRN2", target_bir_lowering=False, num_devices=1)
    arrays, A = {}, {}
    given = {n: inputs[n] for n in _INS}
    given.update(_constants())
    for name, v in given.items():
        a = _np.ascontiguousarray(v)
        arrays[f"in_{name}_dram"] = a
        A[name] = nc.dram_tensor(f"in_{name}_dram", a.shape, _mybir.dt.from_np(a.dtype), kind="ExternalInput").ap()
    out = nc.dram_tensor("out_0_dram", (16, 56, 512), _mybir.dt.float32, kind="ExternalOutput").ap()
    bass_xattn_ffn_layers(nc, A, out)
    r = _run(nc, [arrays], core_ids=[0])
    return r.results[0]["out_0_dram"]
```

```python
from contextlib import ExitStack

import concourse.bass as bass
from concourse import mybir

F32 = mybir.dt.float32
F32R = mybir.dt.float32r
I32 = mybir.dt.int32
BF16 = mybir.dt.bfloat16
ALU = mybir.AluOpType
ACT = mybir.ActivationFunctionType
AX = mybir.AxisListType

P = 128
BIG = 3.4028235e38
EPS = 1e-5


class Chain:

    def __init__(self, eng, sem, base=0):
        self.eng, self.sem, self.base, self.n = eng, sem, base, 0

    def step(self, ins):
        self.n += 1
        return ins.then_inc(self.sem, 1)

    def settle(self, upto=None):
        self.eng.wait_ge(self.sem, self.base + (self.n if upto is None else upto))

    def link(self, ins):
        self.step(ins)
        self.settle()


def bass_xattn_ffn_layers(nc, A, out):
    x_dram, ctx_dram = A["x"], A["ctx_4096"]
    B, C, D = x_dram.shape
    S = ctx_dram.shape[1]
    KD = D // P
    SP = 125
    SJ = S // SP
    SG = SJ // 4
    GW = 4 * SP
    R = 64
    T = B // 2
    TOK = B * R
    TOPK = 34
    NS = 40
    E, INTER = A["L0_ffn_ew1"].shape[0], A["L0_ffn_ew1"].shape[2]
    ES = E + 2
    GR = 4
    E1, RK = A["L1_ffn_A_w"].shape[0], A["L1_ffn_A_w"].shape[1]
    SCALE = float(D) ** -0.5

    ctx = ExitStack()
    with ctx:
        def sb(name, shape, dt=F32):
            return ctx.enter_context(nc.sbuf_tensor(name, shape, dt))

        def sem(name):
            return ctx.enter_context(nc.semaphore(name))

        PS = [ctx.enter_context(nc.psum_tensor(f"bank{i}", [P, 512], F32)) for i in range(3, 8)]
        PS3 = ctx.enter_context(nc.psum_tensor("banks012", [P, 3, 512], F32))
        bank = [PS3[:, 0, :], PS3[:, 1, :], PS3[:, 2, :]] + [t[:, :] for t in PS]

        xnat = sb("xnat", [P, T, D])
        normed = sb("normed", [P, T, D])
        xnT = sb("xnT", [P, KD, TOK])
        crucial = normed[:, :, :].rearrange("p t d -> p (t d)").rearrange("p (k n) -> p k n", k=KD)
        qT = crucial
        slot0 = sb("slot0", [P, SJ * D])
        work = sb("work", [P, 7168])
        wq = work[:, 0:2048].rearrange("p (k n) -> p k n", k=KD)
        wk = work[:, 2048:4096].rearrange("p (k n) -> p k n", k=KD)
        wb = work[:, 4096:6144].rearrange("p (k n) -> p k n", k=KD)
        aw = work[:, 6144:6656]
        bw = work[:, 6656:7168].rearrange("p (c n) -> p c n", c=KD)
        wexp = [work[:, 1536 * s:1536 * s + 1536] for s in range(2)]
        w12 = [w[:, 0:1024].rearrange("p (m k n) -> p m k n", m=2, k=KD) for w in wexp]
        w3 = [w[:, 1024:1536] for w in wexp]
        hT = work[:, 3072:4096]
        silu = [work[:, 4096 + 512 * s:4608 + 512 * s] for s in range(2)]
        pair2 = work[:, 5120:6144]
        bias_bc = work[:, 6144:7168].rearrange("p (m n) -> p m n", m=2)
        FT = work[:, 0:4 * 2 * GW].rearrange("p (s a n) -> p s a n", s=4, a=2)
        gateT = work[0:E, 5120:6144]
        spare = xnT[:, :, :].rearrange("p k n -> p (k n)")
        qring = spare[:, 0:2 * KD * P].rearrange("p (s k n) -> p s k n", s=2, k=KD)
        probs = spare[:, 1024:1024 + S]
        probsT = spare[:, 2560:2560 + SJ * P].rearrange("p (j n) -> p j n", j=SJ)
        mq = sb("mq", [P, KD, D])
        wbT = sb("wbT", [P, KD, D])
        agT = sb("agT", [P, KD, P + 9])
        bT = sb("bT", [P, D])
        above = [t[:, :, :].rearrange("p k n -> p (k n)")[:, S // 2 * n:S // 2 * (n + 1)].bitcast(BF16)
                 for t in (mq, wbT) for n in range(2)]
        partial = [mq[:, :, :].rearrange("p k n -> p (k n)")[:, S + P * n:S + P * (n + 1)].bitcast(BF16) for n in range(2)]
        identb = sb("identb", [P, P], BF16)
        onesb = sb("onesb", [P, 2], BF16)
        tail = wbT[:, :, :].rearrange("p k n -> p (k n)")[:, S:]
        cands = [sb("cand", [P, KD, C])[:, :, :], tail[:, 0:KD * C].rearrange("p (k c) -> p k c", k=KD)]
        cand = cands[0]
        sorted15 = [sb("sorted15", [P, KD, 16]), tail[:, KD * C:KD * C + KD * 16].rearrange("p (k n) -> p k n", k=KD)]
        spare56 = tail[:, 304:528].rearrange("p (k c) -> p k c", k=KD)
        fnew = tail[:, 528:532]
        okay = sb("okay", [P, KD], I32)
        thr_ns = [tail[:, 288 + 8 * n:296 + 8 * n].rearrange("p (a k) -> p a k", a=2) for n in range(2)]
        full = sb("full", [P, KD])
        fsum = sb("fsum", [P, 1])
        flag = sb("flag", [1, 1], I32)
        rw = sb("rw", [P, KD, E])
        ident = sb("ident", [P, P])
        pathmean = sb("pathmean", [P, P])
        ones = sb("ones", [P, P])
        lower = sb("lower", [P, GR * GR + T * E])
        reset = sb("reset", [P, KD * C])
        eb3 = sb("eb3", [E, D])
        rb_bc = sb("rb_bc", [P, 2, E])
        cw_bc = sb("cw_bc", [P, 16])
        bthr_bc = sb("bthr_bc", [P, 1])
        cols12 = sb("cols12", [P, 12])
        b12 = sb("b12", [P, 2, ES])
        uv = sb("uv", [P, 2, KD])
        bqk = sb("bqk", [P, KD + 2])
        qbk = sb("qbk", [P, T])
        st = sb("st", [P, 2, KD, 2, B])
        cpad = sb("cpad", [P, 2, P + 6])
        zc = sb("zc", [P, P])
        attA = sb("attA", [P, P])
        bnst = sb("bnst", [P, T, 6])
        bnmv = sb("bnmv", [P, T, 2])
        lnv = sb("lnv", [P, T])
        lns = sb("lns", [P, T])
        lnr = sb("lnr", [P, T])
        top = sb("top", [P, KD, NS])
        sel = [sb(f"sel{n}", [P, KD, C]) for n in range(2)]
        f1 = sb("f1", [P, KD, C])
        f2 = sb("f2", [P, KD, C])
        s1 = sb("s1", [P, KD])
        sm = sb("sm", [P, 8])
        lg, lg2 = (t[:, :, :].rearrange("p k c -> p (k c)")[:, 0:T * E].rearrange("p (t e) -> p t e", t=T) for t in sel)
        tv = sb("tv", [P, T, 4])
        gm = sb("gm", [P, T, GR])
        pair_tables = normed[:, :, :].rearrange("p t d -> p (t d)").rearrange("p (a n) -> p a n", a=2)
        gate = cand[:, :, :].rearrange("p k c -> p (k c)")[:, 0:T * ES].rearrange("p (t e) -> p t e", t=T)
        am = sb("am", [P, 8])
        HG = P + E1 + 1
        gmax = am[:, 5:8]
        STEPS = KD * SG

        with nc.sbuf_tensor("slots123", [P, 3 * SJ * D], F32) as slots123:
            late = slots123[:, :]
        slot = [a.rearrange("p (j d) -> p j d", j=SJ) for a in [slot0[:, :]] + [late[:, s * SJ * D:(s + 1) * SJ * D] for s in range(3)]]
        ctxT = [late[:, SJ * D + s * KD * S:SJ * D + (s + 1) * KD * S].rearrange("p (k s) -> p k s", k=KD) for s in range(2)]
        with ExitStack() as parts:
            def split_parts(name, width):
                return [parts.enter_context(nc.sbuf_tensor(f"{name}_{part}", [P, width], F32R)) for part in ("high", "low")]
            x2 = split_parts("x", KD * TOK)
            w2 = [split_parts(f"w{n}", 3 * D) for n in range(2)]
            h2 = split_parts("h", TOK)
        rows12 = late[0:12, 14000:14000 + P]
        gaterows = late[0:E1, 14400:14400 + D]
        b12rows = late[0:ES, 15400:15400 + 2 * P].rearrange("e (m n) -> e m n", m=2)
        x_parts = [a[:, :].rearrange("p (k n) -> p k n", k=KD) for a in x2]
        w12_parts = [[a[:, 0:2 * D].rearrange("p (m k n) -> p m k n", m=2, k=KD) for a in w] for w in w2]
        w3_parts = [[a[:, 2 * D:] for a in w] for w in w2]
        h_parts = [a[:, :] for a in h2]

        names = """bf_ready searched rows_loaded sums_done partial_ready counts_done cmp_done dve_s pool_sel
            sel_ready flag_ready fb_tp_done fb_evac dve_fb dve_red pool_cr pool_over full_ready fsum_done
            fb_done wait_over act_over zeroed bias_loaded x_loaded const_loaded w_loaded tp_done tp_evac
            ctxT_free ln_var ln_root ln_ready lnT_done lnT_evac pre_done pre_evac conv_in bn_a bn_b bn_c
            sig_in sig_out attT delta_ready delta_done delta_added router_done gates_ready gateT_done
            gateT_evac y_added h_done silu_done hT_ready y_done dve_ln dve_conv dve_rt dve_at dve_fin
            pool_bias experts_done o_half q_done q_evac q_ring qbk_done qbk_ready ft_done ft_act ft_dve
            s_done neg_bias exp_done pt_done pt_evac o_done o_added gl_done exp9 w_ready hw_ready hwT_done
            hwT_evac fin_done fin_added stored pre_dve pre_cc logits_exp xh_done x_split wh_done w_split
            hh_done h_split stats_done dve_qb""".split()
        s = {n: sem(n) for n in names}
        ctx_loaded = [sem(f"ctx_loaded{n}") for n in range(2)]
        cslot_loaded = [sem(f"cslot_loaded{n}") for n in range(4)]
        fb_loaded = [sem(f"fb_loaded{n}") for n in range(2)]
        wexp_loaded = [sem(f"wexp_loaded{n}") for n in range(2)]

        def pairs_hw(t):
            return pair2[:, t * P:(t + 1) * P]

        block = ctx.enter_context(nc.Block())

        @block.sync
        def _(sp):
            sp.wait_ge(s["zeroed"], 1)
            for j in range(2):
                sp.dma_start(xnat[R * j:R * j + C, :, :],
                             x_dram.rearrange("(t j) c d -> j c t d", j=2)[j]).then_inc(s["x_loaded"], 16)
            sp.dma_start(ident[:, :], A["ident"]).then_inc(s["const_loaded"], 16)
            sp.dma_start(pathmean[:, :], A["pathmean"]).then_inc(s["const_loaded"], 16)
            sp.dma_start(lower[:, :], A["lower"]).then_inc(s["const_loaded"], 16)
            sp.dma_start(reset[:, :], A["reset"]).then_inc(s["const_loaded"], 16)
            def ctx_load(b, p):
                sp.dma_start(slot[p][0:SP], ctx_dram[b].rearrange("(j p) d -> p j d", p=SP)).then_inc(ctx_loaded[p], 16)

            for p in range(2):
                ctx_load(p, p)
            with sp.Fori(1, T) as i:
                for p in range(2):
                    sp.wait_ge(s["tp_done"], (2 * i + p - 1) * KD * SG)
                    ctx_load(2 * i + p, p)

            sp.wait_ge(s["flag_ready"], 1)
            with sp.If(sp.value_load(flag[0:1, 0:1], min_val=0, max_val=1) > 0):
                for p in range(2):
                    sp.dma_start(slot[p][0:SP], ctx_dram[p].rearrange("(j p) d -> p j d", p=SP)).then_inc(fb_loaded[p], 16)
                with sp.Fori(1, T) as i:
                    for p in range(2):
                        sp.wait_ge(s["fb_tp_done"], (2 * i + p - 1) * KD * SG)
                        sp.dma_start(slot[p][0:SP], ctx_dram[2 * i + p].rearrange("(j p) d -> p j d", p=SP)).then_inc(fb_loaded[p], 16)

            sp.wait_ge(s["searched"], 1)
            def load(dst, src):
                sp.dma_start(dst, src).then_inc(s["rows_loaded"], 16)

            load(rows12[0:4, :], A["L1_ffn_W_thr"].rearrange("(k p) -> k p", p=P))
            load(rows12[4:8, :], A["L1_xattn_bk"].rearrange("(k p) -> k p", p=P))
            load(rows12[8:12, :], A["L1_xattn_bq"].rearrange("(k p) -> k p", p=P))
            load(gaterows, A["L1_ffn_W_gate"])
            for m in range(2):
                load(b12rows[1:ES - 1, m, :], A[f"L0_ffn_eb{m + 1}"])
                for h in range(2):
                    load(b12rows[h * (ES - 1):h * (ES - 1) + 1, m, :], A[f"L0_ffn_sb{m + 1}"].rearrange("(h p) -> h p", p=P)[h:h + 1])

            def expert_load(n, sl, e=None, h=None):
                if not (isinstance(n, int) and n < 2):
                    sp.wait_ge(s["w_split"], n - 1)
                if h is None:
                    w1, w2, w3d = A["L0_ffn_ew1"][e], A["L0_ffn_ew2"][e], A["L0_ffn_ew3"][e]
                else:
                    c = slice(h * INTER, (h + 1) * INTER)
                    w1, w2, w3d = A["L0_ffn_sw1"][:, c], A["L0_ffn_sw2"][:, c], A["L0_ffn_sw3"][c, :]
                sp.dma_start(w12[sl][:, 0], w1.rearrange("(k p) n -> p k n", p=P)).then_inc(wexp_loaded[sl], 16)
                sp.dma_start(w12[sl][:, 1], w2.rearrange("(k p) n -> p k n", p=P)).then_inc(wexp_loaded[sl], 16)
                sp.dma_start(w3[sl], w3d).then_inc(wexp_loaded[sl], 16)

            sp.wait_ge(s["pre_evac"], PRE_ACT)
            for m, v in enumerate((A["L0_ffn_sb3"], A["L1_ffn_b_base"])):
                sp.dma_start(bias_bc[:, m, :], v.rearrange("(a n) -> a n", a=1).broadcast_to([P, D])).then_inc(s["bias_loaded"], 16)
            expert_load(0, 0, h=0)
            expert_load(1, 1, e=0)
            with sp.Fori(0, E // 2 - 1) as i:
                for p in range(2):
                    expert_load(2 * i + p + 2, p, e=2 * i + p + 1)
            expert_load(E, 0, e=E - 1)
            expert_load(E + 1, 1, h=1)

            sp.wait_ge(s["conv_in"], 1)
            def cslot_load(b, n, h):
                src = ctx_dram[b].rearrange("(j p) d -> p j d", p=SP)
                j = slice(h * SJ // 2, (h + 1) * SJ // 2)
                sp.dma_start(slot[n][0:SP, j], src[:, j]).then_inc(cslot_loaded[n], 16)

            for n in range(4):
                if n == 1:
                    sp.wait_ge(s["experts_done"], 1)
                for h in range(2):
                    cslot_load(n, n, h)
            with sp.Fori(0, T // 2 - 1) as i:
                for p in range(2):
                    for h in range(2):
                        sp.wait_ge(s[("o_half", "o_done")[h]], 2 * i + p + 1 + 2 * h)
                        for a in range(2):
                            cslot_load(4 * i + 2 * p + a + 4, 2 * p + a, h)
            for t in range(T):
                sp.wait_ge(s["fin_added"], t + 1)
                for j in range(2):
                    sp.dma_start(out[2 * t + j], xnat[R * j:R * j + C, t, :]).then_inc(s["stored"], 16)
            sp.wait_ge(s["stored"], 32 * T)

        @block.gpsimd
        def _(pool):
            pool.memset(xnat[:, :, :], 0.0).then_inc(s["zeroed"], 1)
            pool.memset(ones[:, :], 1.0).then_inc(s["zeroed"], 1)
            pool.memset(cpad[:, :, :], 0.0).then_inc(s["zeroed"], 1)
            pool.wait_ge(s["lnT_evac"], T)
            pool.memset(crucial, 0.0).then_inc(s["zeroed"], 1)

            pool.sem_inc(s["pool_sel"], 2)
            pool.wait_ge(s["zeroed"], 4)

            def split(b, p):
                pool.wait_ge(s["sel_ready"], b + 1)
                pool.sem_inc(s["pool_over"], 1)
                cols = bass.ds(b * R, C)
                pool.tensor_tensor(crucial[:, :, cols], sel[p][:, :, :], xnT[:, :, cols], ALU.mult).then_inc(s["pool_cr"], 1)
                pool.wait_ge(s["pool_cr"], b + 1)
                pool.sem_inc(s["pool_over"], 1)
                pool.tensor_tensor(xnT[:, :, cols], xnT[:, :, cols], crucial[:, :, cols], ALU.subtract).then_inc(s["pool_sel"], 1)

            with pool.Fori(0, T) as i:
                for p in range(2):
                    split(2 * i + p, p)
            def weights_low(n, p):
                pool.wait_ge(s["wh_done"], n + 1)
                pool.sem_inc(s["pool_over"], 1)
                pool.tensor_tensor(w2[p][1][:, :], wexp[p], w2[p][0][:, :].bitcast(F32), ALU.subtract).then_inc(s["w_split"], 1)

            weights_low(0, 0)
            weights_low(1, 1)
            pool.wait_ge(s["bias_loaded"], 32)
            for stage, which in ((2, 0), (4, 1)):
                pool.wait_ge(s["ln_ready"], stage * T)
                for t in range(T):
                    pool.tensor_tensor(xnat[:, t, :], xnat[:, t, :], bias_bc[:, which, :], ALU.add).then_inc(s["pool_bias"], 1)
                if which == 0:
                    with pool.Fori(0, E // 2) as i:
                        for p in range(2):
                            weights_low(2 * i + p + 2, p)
                    pool.wait_ge(s["q_evac"], 2 * KD)
                    with pool.Fori(0, T // 2) as i:
                        for p in range(2):
                            pool.wait_ge(s["o_done"], 2 * i + p + 1)
                            pool.tensor_copy(qring[:, p], qT[:, :, bass.ds((2 * i + p) * P, P)]).then_inc(s["q_ring"], 1)

        @block.scalar
        def _(act):
            def load(dst, src):
                act.dma_start(dst, src).then_inc(s["w_loaded"], 16)

            def row(a):
                return a.rearrange("(a n) -> a n", a=1)

            act.sem_inc(s["tp_evac"], 4)

            def ln_root(stage):
                act.wait_ge(s["ln_var"], stage + 1)
                act.activation(lns[:, :], lnv[:, :], ACT.Sqrt).then_inc(s["ln_root"], 1)

            def ln_evac(stage, parts=False):
                for t in range(T):
                    act.wait_ge(s["lnT_done"], stage * T + t + 1)
                    if parts:
                        act.activation(x_parts[0][:, :, t * P:(t + 1) * P],
                                       bank[4 + t % 4].rearrange("p (k n) -> p k n", k=KD), ACT.Copy).then_inc(s["xh_done"], 1)
                    act.activation(xnT[:, :, t * P:(t + 1) * P],
                                   bank[4 + t % 4].rearrange("p (k n) -> p k n", k=KD), ACT.Copy).then_inc(s["lnT_evac"], 1)

            def evac(b, p, m):
                g = ORDER[m]
                act.wait_ge(s["tp_done"], b * KD * SG + m + 1)
                act.activation(ctxT[p][:, g // SG, (g % SG) * GW:(g % SG + 1) * GW],
                               bank[m % 4][:, 0:GW], ACT.Copy).then_inc(s["tp_evac"], 1)

            def search(b, p, last=False):
                for hp in range(8):
                    act.wait_ge(s["sums_done"], b * 8 + hp + 1)
                    act.activation(partial[hp % 2][0:SP, :], bank[4 + hp % 2][0:SP, 0:2 * P], ACT.Copy).then_inc(s["partial_ready"], 1)
                    if not last:
                        if hp == 0 and not (isinstance(b, int) and b == 0):
                            act.wait_ge(s["cmp_done"], b * 16)
                        for g in NEXT[hp]:
                            evac(b + 1, 1 - p, g)

            ln_root(0)
            for g in range(KD * SG):
                evac(0, 0, g)
            ln_evac(0)
            load(wq, A["L1_xattn_Wq"].rearrange("(k p) n -> p k n", p=P))
            load(wk, A["L1_xattn_Wk"].rearrange("(k p) n -> p k n", p=P))
            load(wb, A["L1_ffn_W_base"].rearrange("(k p) n -> p k n", p=P))
            load(aw, A["L1_ffn_A_w"].rearrange("e r d -> (e r) d"))
            for c in range(KD):
                load(bw[:, c, :].rearrange("p (e r) -> p e r", e=E1),
                     A["L1_ffn_B_w"][:, c * P:(c + 1) * P, :].rearrange("e p r -> p e r"))
            load(rw[:, :, :], A["L0_ffn_router_w"].rearrange("(k p) n -> p k n", p=P))
            load(eb3[:, :], A["L0_ffn_eb3"])
            load(rb_bc[:, 0, :], row(A["L0_ffn_router_b"]).broadcast_to([P, E]))
            load(rb_bc[:, 1, :], row(A["L0_ffn_router_bias"]).broadcast_to([P, E]))
            load(cw_bc[:, 0:14], A["L0_xattn_conv_w"].rearrange("a c k -> a (c k)").broadcast_to([P, 14]))
            load(cw_bc[:, 14:15], row(A["L0_xattn_bn_gamma"]).broadcast_to([P, 1]))
            load(cw_bc[:, 15:16], row(A["L0_xattn_bn_beta"]).broadcast_to([P, 1]))
            load(bthr_bc[:, :], row(A["L1_ffn_b_thr"]).broadcast_to([P, 1]))
            search(0, 0)
            with act.Fori(0, T - 1) as i:
                for p in range(2):
                    search(2 * i + 1 + p, 1 - p)
            search(B - 1, 1, last=True)

            act.wait_ge(s["flag_ready"], 1)
            with act.If(act.value_load(flag[0:1, 0:1], min_val=0, max_val=1) > 0):
                act.sem_inc(s["fb_evac"], 4)
                with act.Fori(0, T) as i:
                    for p in range(2):
                        act.wait_ge(s["ctxT_free"], 2 * i + p + 1)
                        for g in range(KD * SG):
                            act.wait_ge(s["fb_tp_done"], (2 * i + p) * KD * SG + g + 1)
                            act.activation(ctxT[p][:, g // SG, (g % SG) * GW:(g % SG + 1) * GW],
                                           bank[g % 4][:, 0:GW], ACT.Copy).then_inc(s["fb_evac"], 1)

            n = [0]

            def pre(dst, src):
                act.activation(dst, src, ACT.Copy).then_inc(s["pre_evac"], 1)

            def pre_wait():
                n[0] += 1
                act.wait_ge(s["pre_done"], n[0])
                return bank[4 + (n[0] - 1) % 4]

            b = pre_wait()
            pre(agT[:, :, 0:P], b.rearrange("p (k n) -> p k n", k=KD))
            b = pre_wait()
            pre(bT[:, :], b)
            act.wait_ge(s["searched"], 1)
            for k in range(KD):
                b = pre_wait()
                pre(wbT[:, k, :], b)
            b = pre_wait()
            pre(cols12[:, :], b[:, 0:12])
            pre(b12[:, 0, :], b[:, 16:16 + ES])
            pre(b12[:, 1, :], b[:, 48:48 + ES])
            pre(agT[:, :, P:P + E1], b[:, 80:80 + KD * E1].rearrange("p (k n) -> p k n", k=KD))
            pre(agT[:, :, P + E1], b[:, 0:4])
            for k in range(KD):
                b = pre_wait()
                pre(mq[:, k, :], b)
            act.wait_ge(s["bn_c"], 1)
            act.activation(sm[:, 4:5], sm[:, 3:4], ACT.Sqrt).then_inc(s["sig_out"], 1)
            act.wait_ge(s["sig_in"], 1)
            act.activation(zc[:, :], zc[:, :], ACT.Sigmoid).then_inc(s["sig_out"], 1)

            b = pre_wait()
            pre(uv[:, :, :], b[:, 0:8].rearrange("p (m k) -> p m k", m=2))
            pre(bqk[:, 5:6], b[:, 8:9])

            def weights_high(sl, turn):
                act.wait_ge(wexp_loaded[sl], turn * 48)
                act.activation(w2[sl][0][:, :], wexp[sl], ACT.Copy).then_inc(s["wh_done"], 1)

            weights_high(0, 1)
            weights_high(1, 1)
            ln_root(1)
            ln_evac(1, True)

            act.wait_ge(s["gates_ready"], 1)
            act.activation(lg2[:, :, :], lg[:, :, :], ACT.Exp).then_inc(s["logits_exp"], 1)

            def hidden(n, h, e):
                cols = slice(h * 512, (h + 1) * 512)
                act.wait_ge(s["h_done"], 2 * n + h + 1)
                act.sem_inc(s["act_over"], 1)
                act.activation(silu[h], bank[2 * h], ACT.Silu,
                               bias=b12[:, 0, e]).then_inc(s["silu_done"], 1)
                act.wait_ge(s["hT_ready"], 2 * n + h + 1)
                act.activation(h_parts[0][:, cols], hT[:, cols], ACT.Copy).then_inc(s["hh_done"], 1)

            def expert(n, e, e_next, sl, turn, more=True):
                hidden(n, 1, e)
                if more:
                    hidden(n + 1, 0, e_next)
                    act.wait_ge(s["y_done"], (n + 1) * T)
                    weights_high(sl, turn)

            def col(e):
                return bass.ds(e, 1)

            hidden(0, 0, slice(0, 1))
            expert(0, slice(0, 1), slice(1, 2), 0, 2)
            with act.Fori(0, E // 2 - 1) as i:
                for p in range(2):
                    n = 2 * i + p + 1
                    expert(n, col(n), col(n + 1), 1 - p, i + 2 + p)
            n = E - 1
            expert(n, slice(n, n + 1), slice(n + 1, n + 2), 1, E // 2 + 1)
            hidden(E, 1, slice(E, E + 1))
            hidden(E + 1, 0, slice(E + 1, E + 2))
            hidden(E + 1, 1, slice(E + 1, E + 2))

            ln_root(2)
            ln_evac(2)
            act.wait_ge(s["qbk_ready"], 1)
            for y in range(2 * KD):
                act.wait_ge(s["q_done"], y + 1)
                act.activation(qT[:, y // 2, (y % 2) * 512:(y % 2 + 1) * 512], bank[4 + y % 4], ACT.Identity,
                               bias=uv[:, 1, y // 2:y // 2 + 1]).then_inc(s["q_evac"], 1)

            def f_evac(pair, e):
                act.wait_ge(s["ft_done"], pair * 2 * STEPS + 2 * e + 1)
                act.wait_ge(s["s_done"], pair * STEPS + e + 1)
                act.activation(FT[:, e % 4, 0, :], bank[3 + 2 * (e % 2)][:, 0:GW], ACT.Copy).then_inc(s["ft_act"], 1)

            def attention(pair, last=False):
                for e in range(4, STEPS):
                    f_evac(pair, e)
                if not last:
                    for e in range(2):
                        f_evac(pair + 1, e)
                act.wait_ge(s["neg_bias"], pair + 1)
                act.activation(probs.rearrange("p (g n) -> p g n", g=SG), PS3[:, :, 0:GW], ACT.Exp,
                               bias=am[:, 2:3], scale=SCALE, accum_out=am[:, 3:4]).then_inc(s["exp_done"], 1)
                if not last:
                    for e in range(2, 4):
                        f_evac(pair + 1, e)
                for g in range(SG):
                    act.wait_ge(s["pt_done"], pair * SG + g + 1)
                    act.activation(probsT[0:SP, 4 * g:4 * g + 4, :], bank[3 + g][0:SP, :].rearrange("p (j n) -> p j n", j=4),
                                   ACT.Copy).then_inc(s["pt_evac"], 1)

            for e in range(4):
                f_evac(0, e)
            with act.Fori(0, T - 1) as i:
                attention(i)
            attention(T - 1, last=True)

            ln_root(3)
            ln_evac(3)
            act.wait_ge(s["w_ready"], 1)
            act.activation(lg2[:, :, 0:9], lg[:, :, 0:9], ACT.Exp).then_inc(s["exp9"], 1)
            for t in range(2):
                act.wait_ge(s["hwT_done"], t + 1)
                act.activation(hT[:, t * 512:(t + 1) * 512], bank[t], ACT.Copy).then_inc(s["hwT_evac"], 1)

        @block.tensor
        def _(pe):
            pe.sem_inc(s["o_done"], 2)
            pe.sem_inc(s["s_done"], 4)

            def mm(o, l, r, first, last):
                return pe.matmul(o, l, r, start=first, stop=last)

            def ln_turn(stage):
                for t in range(T):
                    pe.wait_ge(s["ln_ready"], stage * T + t + 1)
                    if t >= 4:
                        pe.wait_ge(s["lnT_evac"], stage * T + t - 3)
                    for k in range(KD):
                        ins = pe.transpose(bank[4 + t % 4][:, k * P:(k + 1) * P], normed[:, t, k * P:(k + 1) * P], ident[:, :])
                    ins.then_inc(s["lnT_done"], 1)

            pe.wait_ge(s["const_loaded"], 64)

            def turn_ctx(b, p, m):
                g = ORDER[m]
                pe.wait_ge(s["tp_evac"], b * KD * SG + m + 1)
                for q in range(4):
                    ins = pe.transpose(bank[m % 4][:, q * SP:(q + 1) * SP],
                                       slot[p][0:SP, 4 * (g % SG) + q, (g // SG) * P:(g // SG + 1) * P], ident[0:SP, 0:SP])
                ins.then_inc(s["tp_done"], 1)

            def search(b, p, nxt=None, last=False):
                for hp in range(8):
                    h = hp % 2
                    ahead = [] if last else NEXT[hp]
                    for j in range(2):
                        if j == 1 and ahead:
                            if hp == 0:
                                pe.wait_ge(ctx_loaded[1 - p], nxt * 16)
                            turn_ctx(b + 1, 1 - p, ahead[0])
                        pe.wait_ge(s["cmp_done"], b * 16 + hp * 2 + j + 1)
                        for q in range(SJ):
                            ins = pe.matmul(bank[4 + h][0:SP, j * P:(j + 1) * P], above[2 * h + j][:, q * SP:(q + 1) * SP],
                                            identb[:, :], start=q == 0, stop=q == SJ - 1)
                    ins.then_inc(s["sums_done"], 1)
                    pe.wait_ge(s["partial_ready"], b * 8 + hp + 1)
                    for j in range(2):
                        ins = pe.matmul(bank[6 + h][:, j:j + 1], partial[h][0:SP, j * P:(j + 1) * P], onesb[0:SP, 0:1],
                                        start=True, stop=True)
                    ins.then_inc(s["counts_done"], 1)
                    for g in ahead[1:]:
                        turn_ctx(b + 1, 1 - p, g)

            pe.wait_ge(ctx_loaded[0], 16)
            for g in range(KD * SG):
                turn_ctx(0, 0, g)
            ln_turn(0)
            pe.wait_ge(s["lnT_evac"], T)
            pe.wait_ge(s["bf_ready"], 2)
            search(0, 0, 1)
            with pe.Fori(0, T - 1) as i:
                for p in range(2):
                    search(2 * i + 1 + p, 1 - p, i + 2)
            search(B - 1, 1, last=True)

            pe.wait_ge(s["full_ready"], 1)
            mm(bank[4][0:1, 0:1], ones[:, 0:1], fsum[:, :], True, True).then_inc(s["fsum_done"], 1)
            pe.wait_ge(s["flag_ready"], 1)
            with pe.If(pe.value_load(flag[0:1, 0:1], min_val=0, max_val=1) > 0):
                with pe.Fori(0, T) as i:
                    for p in range(2):
                        pe.wait_ge(fb_loaded[p], (i + 1) * 16)
                        for g in range(KD * SG):
                            pe.wait_ge(s["fb_evac"], (2 * i + p) * KD * SG + g + 1)
                            for q in range(4):
                                ins = pe.transpose(bank[g % 4][:, q * SP:(q + 1) * SP],
                                                   slot[p][0:SP, 4 * (g % SG) + q, (g // SG) * P:(g // SG + 1) * P], ident[0:SP, 0:SP])
                            ins.then_inc(s["fb_tp_done"], 1)

            n = [0]
            freed = [0, 0, 0, 0]

            def job(evacs, build):
                if n[0] >= 4:
                    pe.wait_ge(s["pre_evac"], freed[n[0] % 4])
                build(bank[4 + n[0] % 4]).then_inc(s["pre_done"], 1)
                n[0] += 1
                job.total += evacs
                freed[(n[0] - 1) % 4] = job.total
            job.total = 0

            def j_rows(b):
                pe.transpose(b[:, 0:12], rows12, ident[0:12, 0:12])
                for m in range(2):
                    pe.transpose(b[:, 16 + 32 * m:16 + 32 * m + ES], b12rows[:, m, :], ident[0:ES, 0:ES])
                for k in range(KD):
                    ins = pe.transpose(b[:, 80 + k * E1:80 + (k + 1) * E1], gaterows[:, k * P:(k + 1) * P], ident[0:E1, 0:E1])
                return ins

            def j_aw(b):
                for k in range(KD):
                    ins = pe.transpose(b[:, k * P:(k + 1) * P], aw[:, k * P:(k + 1) * P], ident[:, :])
                return ins

            def j_bw(b):
                for c in range(KD):
                    ins = pe.transpose(b[:, c * P:(c + 1) * P], bw[:, c, :], ident[:, :])
                return ins

            def j_wb(k):
                def build(b):
                    for c in range(KD):
                        ins = pe.transpose(b[:, c * P:(c + 1) * P], wb[:, c, k * P:(k + 1) * P], ident[:, :])
                    return ins
                return build

            def j_mq(x):
                def build(b):
                    for k in range(KD):
                        ins = mm(b, wq[:, k, x * P:(x + 1) * P], wk[:, k, :], k == 0, k == KD - 1)
                    return ins
                return build

            def j_uv(b):
                for m, (w, at) in enumerate(((wq, 4), (wk, 8))):
                    for x in range(KD):
                        for k in range(KD):
                            mm(b[:, 4 * m + x:4 * m + x + 1], w[:, k, x * P:(x + 1) * P], cols12[:, at + k:at + k + 1],
                               k == 0, k == KD - 1)
                pe.wait_ge(s["pre_cc"], 1)
                return mm(b[:, 8:9], ones[:, :], bqk[:, 4:5], True, True)

            pe.wait_ge(s["w_loaded"], W_LOADS * 16)
            job(1, j_aw)
            job(1, j_bw)
            for k in range(KD):
                job(1, j_wb(k))
            pe.wait_ge(s["rows_loaded"], ROW_LOADS * 16)
            job(5, j_rows)
            for k in range(KD):
                job(1, j_mq(k))
            pe.wait_ge(s["pre_evac"], PRE_ACT - 2)
            pe.wait_ge(s["conv_in"], 1)
            for ch in range(2):
                ins = pe.transpose(bank[4][:, ch * P:(ch + 1) * P], st[:, ch].rearrange("p k a b -> p (k a b)"), ident[:, :])
            ins.then_inc(s["bn_a"], 1)
            pe.wait_ge(s["bn_b"], 1)
            mm(bank[5][:, 0:1], pathmean[:, :], sm[:, 0:1], True, True).then_inc(s["bn_a"], 1)
            pe.wait_ge(s["bn_b"], 2)
            mm(bank[5][:, 1:2], pathmean[:, :], sm[:, 2:3], True, True).then_inc(s["bn_a"], 1)
            pe.wait_ge(s["sig_out"], 2)
            pe.transpose(bank[6][:, 0:P], zc[:, :], ident[:, :]).then_inc(s["attT"], 1)
            job(2, j_uv)
            assert job.total == PRE_ACT

            pe.wait_ge(s["delta_ready"], 1)
            for t in range(T):
                if t >= 4:
                    pe.wait_ge(s["delta_added"], t - 3)
                for k in range(KD):
                    ins = pe.transpose(bank[t % 4][:, k * P:(k + 1) * P], xnT[:, k, t * P:(t + 1) * P], ident[:, :])
                ins.then_inc(s["delta_done"], 1)
            ln_turn(1)

            pe.wait_ge(s["lnT_evac"], 2 * T)
            for t in range(T):
                for k in range(KD):
                    ins = mm(bank[0][:, t * E:(t + 1) * E], xnT[:, k, t * P:(t + 1) * P], rw[:, k, :], k == 0, k == KD - 1)
            ins.then_inc(s["router_done"], 1)

            PASSES = ((0, 0), (0, 1), (1, 0))

            def hidden(n, h, sl):
                if h == 0:
                    pe.wait_ge(s["w_split"], n + 1)
                if not (isinstance(n, int) and n == 0):
                    pe.wait_ge(s["hT_ready"], 2 * n - 2 + h + 1)
                for m in range(2):
                    for k in range(KD):
                        for a, b in PASSES:
                            ins = mm(bank[2 * h + m], w12_parts[sl][a][:, m, k, :], x_parts[b][:, k, h * 512:(h + 1) * 512],
                                     k == 0 and a + b == 0, k == KD - 1 and a == 1)
                ins.then_inc(s["h_done"], 1)

            def outputs(n, h, sl, bias=False):
                pe.wait_ge(s["h_split"], 2 * n + h + 1)
                for t in range(4 * h, 4 * h + 4):
                    if not (isinstance(n, int) and n == 0 and t < 4):
                        pe.wait_ge(s["y_added"], n * T + t - 3)
                    for a, b in PASSES:
                        ins = mm(bank[4 + t % 4], h_parts[a][:, t * P:(t + 1) * P], w3_parts[sl][b], a + b == 0, a == 1 and not bias)
                    if bias:
                        ins = mm(bank[4 + t % 4], gateT[:, t * P:(t + 1) * P], eb3[:, :], False, True)
                    ins.then_inc(s["y_done"], 1)

            def expert(n, sl):
                hidden(n, 1, sl)
                outputs(n, 0, sl)
                hidden(n + 1, 0, 1 - sl)
                outputs(n, 1, sl)

            pe.wait_ge(s["x_split"], T)
            pe.wait_ge(s["gates_ready"], 1)
            hidden(0, 0, 0)
            expert(0, 0)
            with pe.Fori(0, E // 2) as i:
                for p in range(2):
                    expert(2 * i + p + 1, 1 - p)
            pe.wait_ge(s["gates_ready"], 2)
            pe.wait_ge(s["hT_ready"], 2 * ES - 1)
            for t in range(T):
                ins = pe.transpose(bank[t // 4][0:E, (t % 4) * P:(t % 4 + 1) * P], gate[:, t, 1:ES - 1], ident[:, :])
            ins.then_inc(s["gateT_done"], 1)
            hidden(ES - 1, 1, 1)
            pe.wait_ge(s["gateT_evac"], 2)
            outputs(ES - 1, 0, 1, True)
            outputs(ES - 1, 1, 1, True)
            pe.wait_ge(s["y_done"], ES * T)
            pe.sem_inc(s["experts_done"], 1)
            for k in range(KD):
                ins = mm(bank[0][:, k * P:(k + 1) * P], uv[:, 0, k:k + 1].broadcast_to([P, P]), ident[:, :], True, True)
            ins.then_inc(s["qbk_done"], 1)
            ln_turn(2)

            pe.wait_ge(s["lnT_evac"], 3 * T)
            for y in range(2 * KD):
                if y >= 4:
                    pe.wait_ge(s["q_evac"], y - 3)
                for k in range(KD):
                    ins = mm(bank[4 + y % 4], mq[:, k, (y // 2) * P:(y // 2 + 1) * P],
                             xnT[:, k, (y % 2) * 512:(y % 2 + 1) * 512], k == 0, k == KD - 1)
                ins.then_inc(s["q_done"], 1)
            pe.wait_ge(s["qbk_ready"], 1)
            pe.wait_ge(s["q_evac"], 2 * KD)

            def turn(pair, p, e):
                g, k = e // KD, e % KD
                for a in range(2):
                    pe.wait_ge(s[("ft_act", "ft_dve")[a]], pair * STEPS + e + 1)
                    for q in range(4):
                        ins = pe.transpose(bank[3 + 2 * (e % 2) + a][:, q * SP:(q + 1) * SP],
                                           slot[2 * p + a][0:SP, 4 * g + q, k * P:(k + 1) * P], ident[0:SP, 0:SP])
                    ins.then_inc(s["ft_done"], 1)

            def score(pair, p, e):
                g, k = e // KD, e % KD
                pe.wait_ge(s["ft_act"], pair * STEPS + e + 3)
                pe.wait_ge(s["ft_dve"], pair * STEPS + e + 3)
                for a in range(2):
                    rows = slice(R * a, R * a + R)
                    ins = mm(bank[g][rows, 0:GW], qring[:, p, k, rows], FT[:, e % 4, a, :], k == 0, k == KD - 1)
                ins.then_inc(s["s_done"], 1)

            def attention(pair, p, loads):
                pe.wait_ge(s["q_ring"], pair + 1)
                for e in range(STEPS):
                    score(pair, p, e)
                    if e + 4 < STEPS:
                        turn(pair, p, e + 4)
                if loads is not None:
                    for a in range(2):
                        pe.wait_ge(cslot_loaded[2 * (1 - p) + a], loads * 32)
                    for e in range(4):
                        turn(pair + 1, 1 - p, e)
                    pe.wait_ge(s["ft_act"], (pair + 1) * STEPS + 6)
                    pe.wait_ge(s["ft_dve"], (pair + 1) * STEPS + 6)
                pe.wait_ge(s["exp_done"], pair + 1)
                for g in range(SG):
                    for q in range(4):
                        ins = pe.transpose(bank[3 + g][0:SP, q * P:(q + 1) * P], probs[:, (4 * g + q) * SP:(4 * g + q + 1) * SP], ident[:, :])
                    ins.then_inc(s["pt_done"], 1)
                pe.wait_ge(s["o_added"], pair + 1)
                for j in range(SJ):
                    if j % 4 == 0:
                        pe.wait_ge(s["pt_evac"], pair * SG + j // 4 + 1)
                    for a in range(2):
                        rows = slice(R * a, R * a + R)
                        ins = mm(bank[7][rows, :], probsT[0:SP, j, rows], slot[2 * p + a][0:SP, j, :], j == 0, j == SJ - 1)
                    if j == SJ // 2 - 1:
                        ins.then_inc(s["o_half"], 1)
                ins.then_inc(s["o_done"], 1)

            pe.sem_inc(s["ft_act"], 2)
            pe.sem_inc(s["ft_dve"], 2)
            pe.sem_inc(s["o_added"], 1)
            for a in range(2):
                pe.wait_ge(cslot_loaded[a], 32)
            for e in range(4):
                turn(0, 0, e)
            with pe.Fori(0, T // 2 - 1) as i:
                for p in range(2):
                    attention(2 * i + p, p, i + 1 + p)
            attention(T - 2, 0, T // 2)
            attention(T - 1, 1, None)

            ln_turn(3)
            pe.wait_ge(s["lnT_evac"], 4 * T)
            for t in range(T):
                for k in range(KD):
                    ins = mm(bank[t // 2][:, (t % 2) * HG:(t % 2 + 1) * HG], xnT[:, k, t * P:(t + 1) * P], agT[:, k, :], k == 0, k == KD - 1)
            ins.then_inc(s["gl_done"], 1)
            def base(t):
                if t >= 4:
                    pe.wait_ge(s["fin_added"], t - 3)
                for k in range(KD):
                    mm(bank[4 + t % 4], xnT[:, k, t * P:(t + 1) * P], wbT[:, k, :], k == 0, False)

            def low_rank(t):
                mm(bank[4 + t % 4], hT[:, t * P:(t + 1) * P], bT[:, :], False, True).then_inc(s["fin_done"], 1)

            for t in range(4):
                base(t)
            for t in range(T):
                if t % 4 == 0:
                    pe.wait_ge(s["hw_ready"], t // 4 + 1)
                ins = pe.transpose(bank[t // 4][:, (t % 4) * P:(t % 4 + 1) * P], pairs_hw(t), ident[:, :])
                if t % 4 == 3:
                    ins.then_inc(s["hwT_done"], 1)
            pe.wait_ge(s["hwT_evac"], 1)
            for t in range(4):
                low_rank(t)
            pe.wait_ge(s["hwT_evac"], 2)
            for t in range(4, T):
                base(t)
                low_rank(t)

        @block.vector
        def _(dve):
            ln = Chain(dve, s["dve_ln"])

            def layernorm(stage, stats=True):
                if stats:
                    for t in range(T):
                        ln.step(dve.bn_stats(bnst[:, t, :], xnat[:, t, :]))
                    ln.settle()
                for t in range(T):
                    ln.step(dve.bn_aggr(bnmv[:, t, :], bnst[:, t, :]))
                ln.settle()
                dve.tensor_scalar(lnv[:, :], bnmv[:, :, 1], EPS, None, ALU.add).then_inc(s["ln_var"], 1)
                dve.wait_ge(s["ln_root"], stage + 1)
                ln.link(dve.reciprocal(lnr[:, :], lns[:, :]))
                for t in range(T):
                    dve.tensor_scalar(normed[:, t, :], xnat[:, t, :], bnmv[:, t, 0:1], lnr[:, t:t + 1],
                                      ALU.subtract, ALU.mult).then_inc(s["ln_ready"], 1)

            dve.sem_inc(s["ctxT_free"], 2)
            dve.wait_ge(s["zeroed"], 2)
            dve.wait_ge(s["x_loaded"], 32)
            layernorm(0)

            dve.wait_ge(s["const_loaded"], 64)

            ini = Chain(dve, s["pre_dve"])
            dve.tensor_copy(identb[:, :], ident[:, :]).then_inc(s["bf_ready"], 1)
            dve.memset(onesb[:, :], 1.0).then_inc(s["bf_ready"], 1)
            ini.link(dve.memset(full[:, :], 0.0))

            def bc(ap, n):
                return ap.unsqueeze(2).broadcast_to([P, KD, n])

            def over_wait():
                dve.sem_inc(s["wait_over"], 1)

            def sort_1(ch, b, p):
                if ch.n:
                    ch.settle()
                dve.wait_ge(s["tp_evac"], b * KD * SG + KD + 4)
                ch.step(dve.tensor_copy(cands[p], ctxT[p][:, :, 0:C]))
                ch.step(dve.memset(thr_ns[p][:, 0, :], BIG))
                ch.step(dve.memset(thr_ns[p][:, 1, :], float(TOPK)))

            def sort_2(ch, p):
                ch.settle()
                over_wait()
                for k in range(KD):
                    ch.step(dve.max(sorted15[p][:, k, 0:8], cands[p][:, k, :]))

            def sort_3(ch, p, upto=None):
                ch.settle(upto)
                over_wait()
                for k in range(KD):
                    ch.step(dve.match_replace(out=spare56[:, k, :], in_to_replace=sorted15[p][:, k, 0:8], in_values=cands[p][:, k, :],
                                              imm_value=-BIG))

            def sort_4(ch, p, upto=None):
                ch.settle(upto)
                over_wait()
                for k in range(KD):
                    ch.step(dve.max(sorted15[p][:, k, 8:16], spare56[:, k, :]))

            def compare(p, n, h):
                w = 7 >> n
                for k in (2 * h, 2 * h + 1):
                    dve.tensor_scalar(above[k], ctxT[p][:, k, :], sorted15[p][:, k, w:w + 1], None, ALU.is_gt).then_inc(s["cmp_done"], 1)

            def picks(ch, b, p):
                thr = bc(thr_ns[p][:, 0, :], C)
                done = [0]
                flat = lambda t: t[:, :, :].rearrange("p k c -> p (k c)")

                def one():
                    ch.step(dve.tensor_tensor(fnew, sorted15[p][:, :, 14], thr_ns[p][:, 0, :], ALU.is_ge))
                    ch.step(dve.tensor_scalar(s1[:, :], thr_ns[p][:, 1, :], -1.0, float(TOPK), ALU.mult, ALU.add))
                    ch.step(dve.tensor_tensor(f1[:, :, :], cands[p], thr, ALU.is_equal))
                    done[0] = ch.n

                def two():
                    ch.settle(done[0])
                    ch.step(dve.tensor_tensor(full[:, :], full[:, :], fnew, ALU.add))
                    ch.step(dve.tensor_tensor_scan(flat(f2), reset[:, :], flat(f1), 0.0, ALU.mult, ALU.add))
                    done[0] = ch.n

                def three():
                    ch.settle(done[0])
                    ch.step(dve.tensor_tensor(f2[:, :, :], f2[:, :, :], f1[:, :, :], ALU.mult))
                    done[0] = ch.n

                def four():
                    ch.settle(done[0])
                    ch.step(dve.tensor_tensor(f1[:, :, :], cands[p], thr, ALU.is_ge))
                    ch.step(dve.tensor_tensor(f2[:, :, :], f2[:, :, :], bc(s1[:, :], C), ALU.is_le))
                    done[0] = ch.n

                def five():
                    ch.settle(done[0])
                    dve.wait_ge(s["pool_sel"], b + 1)
                    dve.tensor_tensor(sel[p][:, :, :], f1[:, :, :], f2[:, :, :], ALU.mult).then_inc(s["sel_ready"], 1)

                return [one, two, three, four, five]

            def search(b, p, first=False, last=False):
                ch = Chain(dve, s["dve_s"], SORT_STEPS if first else SORT_STEPS - PICK_STEPS + b * SEARCH_STEPS)
                pieces = [] if first else picks(ch, b - 1, 1 - p)

                sorted_to = [0]

                def step(n, h, between=None):
                    w = 7 >> n
                    ks = slice(2 * h, 2 * h + 2)
                    counts = bank[6 + h][:, 0:2]
                    dve.wait_ge(s["counts_done"], b * 8 + 2 * n + h + 1)
                    ch.step(dve.tensor_scalar(okay[:, ks], counts, TOPK - 0.5, None, ALU.is_lt))
                    judged = ch.n
                    if pieces:
                        pieces.pop(0)()
                    if between:
                        between(ch, 1 - p, sorted_to[0])
                        sorted_to[0] = ch.n
                    ch.settle(judged)
                    over_wait()
                    halved = None
                    if n < 3:
                        ch.step(dve.copy_predicated(sorted15[p][:, ks, 0:w], okay[:, ks].unsqueeze(2).broadcast_to([P, 2, w]),
                                                    sorted15[p][:, ks, w + 1:2 * w + 1]))
                        halved = ch.n
                    ch.step(dve.copy_predicated(thr_ns[p][:, 0, ks], okay[:, ks], sorted15[p][:, ks, w]))
                    ch.step(dve.copy_predicated(thr_ns[p][:, 1, ks], okay[:, ks], counts))
                    ch.settle(halved)

                for n in range(3):
                    for h in range(2):
                        step(n, h, sort_3 if (n, h) == (2, 1) and not last else None)
                        compare(p, n + 1, h)
                        if not last:
                            if (n, h) == (1, 1):
                                sort_1(ch, b + 1, 1 - p)
                            if (n, h) == (2, 0):
                                sort_2(ch, 1 - p)
                                sorted_to[0] = ch.n
                step(3, 0, None if last else sort_4)
                if not last:
                    dve.wait_ge(s["tp_evac"], (b + 2) * KD * SG + 4)
                    compare(1 - p, 0, 0)
                step(3, 1)
                if not last:
                    compare(1 - p, 0, 1)
                assert ch.n == SEARCH_STEPS - (SORT_STEPS if last else 0) - (PICK_STEPS if first else 0), ch.n

            ch0 = Chain(dve, s["dve_s"])
            sort_1(ch0, 0, 0)
            for sort in (sort_2, sort_3, sort_4):
                sort(ch0, 0)
            ch0.settle()
            dve.wait_ge(s["tp_evac"], KD * SG + 4)
            for h in range(2):
                compare(0, 0, h)
            search(0, 0, first=True)
            with dve.Fori(0, T - 1) as i:
                for p in range(2):
                    search(2 * i + 1 + p, 1 - p)
            search(B - 1, 1, last=True)
            end = Chain(dve, s["dve_s"], SORT_STEPS - PICK_STEPS + B * SEARCH_STEPS - SORT_STEPS)
            for piece in picks(end, B - 1, 1):
                piece()
            dve.wait_ge(s["pool_sel"], B + 2)
            ini.link(dve.tensor_reduce(fsum[:, :], full[:, :], AX.X, ALU.add))
            dve.sem_inc(s["full_ready"], 1)
            dve.wait_ge(s["fsum_done"], 1)
            dve.tensor_scalar(flag[:, :], bank[4][0:1, 0:1], 0.5, None, ALU.is_gt).then_inc(s["flag_ready"], 1)
            dve.wait_ge(s["flag_ready"], 1)

            with dve.If(dve.value_load(flag[0:1, 0:1], min_val=0, max_val=1) > 0):
                fb0 = Chain(dve, s["fb_done"])
                fb0.link(dve.tensor_tensor(xnT[:, :, :], xnT[:, :, :], crucial, ALU.add))
                with dve.Fori(0, T) as i:
                    for p in range(2):
                        b = 2 * i + p
                        ch = Chain(dve, s["dve_fb"], b * FALLBACK_STEPS)
                        dve.wait_ge(s["fb_evac"], (b + 1) * KD * SG + 4)
                        ch.link(dve.tensor_copy(cand[:, :, :], ctxT[p][:, :, 0:C]))
                        for r in range(NS // 8):
                            over_wait()
                            for k in range(KD):
                                ch.step(dve.max(top[:, k, 8 * r:8 * r + 8], ctxT[p][:, k, :]))
                            ch.settle()
                            if r < NS // 8 - 1:
                                over_wait()
                                for k in range(KD):
                                    ch.step(dve.match_replace(out=ctxT[p][:, k, :], in_to_replace=top[:, k, 8 * r:8 * r + 8],
                                                              in_values=ctxT[p][:, k, :], imm_value=-BIG))
                                ch.settle()
                        dve.sem_inc(s["ctxT_free"], 1)
                        thr = top[:, :, TOPK - 1]
                        ch.link(dve.tensor_tensor(f2[:, :, 0:TOPK], top[:, :, 0:TOPK], bc(thr, TOPK), ALU.is_gt))
                        ch.link(dve.tensor_reduce(thr_ns[0][:, 1, :], f2[:, :, 0:TOPK], AX.X, ALU.add))
                        ch.link(dve.tensor_copy(thr_ns[0][:, 0, :], thr))
                        pick = picks(ch, b, 0)[:-1]
                        for piece in pick:
                            piece()
                        ch.settle()
                        ch.link(dve.tensor_tensor(sel[p][:, :, :], f1[:, :, :], f2[:, :, :], ALU.mult))
                        cols = bass.ds(b * R, C)
                        ch.link(dve.tensor_tensor(crucial[:, :, cols], sel[p][:, :, :], xnT[:, :, cols], ALU.mult))
                        ch.link(dve.tensor_tensor(xnT[:, :, cols], xnT[:, :, cols], crucial[:, :, cols], ALU.subtract))
                        assert ch.n == FALLBACK_STEPS, ch.n

            dve.sem_inc(s["searched"], 1)
            rd = Chain(dve, s["dve_red"])
            for path, a in ((0, crucial), (1, xnT)):
                for k in range(KD):
                    v = a[:, k, :].rearrange("p (b c) -> p b c", b=B)[:, :, 0:C]
                    for what, op in ((0, ALU.max), (1, ALU.add)):
                        rd.step(dve.tensor_reduce(st[:, what, k, path, :], v, AX.X, op))
            rd.settle()

            dve.wait_ge(s["pre_evac"], 7)
            rd.link(dve.tensor_tensor(bqk[:, 0:KD], cols12[:, 4:8], cols12[:, 8:12], ALU.mult))
            dve.tensor_reduce(bqk[:, 4:5], bqk[:, 0:KD], AX.X, ALU.add).then_inc(s["pre_cc"], 1)

            cv = Chain(dve, s["dve_conv"])
            cv.step(dve.tensor_scalar(st[:, 1, :, 0, :], st[:, 1, :, 0, :], 1.0 / C, float(C / TOPK), ALU.mult, ALU.mult))
            cv.link(dve.tensor_scalar(st[:, 1, :, 1, :], st[:, 1, :, 1, :], 1.0 / C, float(C / (C - TOPK)), ALU.mult, ALU.mult))
            dve.sem_inc(s["conv_in"], 1)
            dve.wait_ge(s["bn_a"], 1)
            turned = bank[4][:, 0:2 * P].rearrange("p (c n) -> p c n", c=2)
            cv.step(dve.tensor_copy(cpad[:, :, 3:3 + P], turned))
            for q in range(KD):
                here = slice(32 * q, 32 * q + 32)
                if q > 0:
                    cv.step(dve.tensor_copy(cpad[here, :, 0:3], turned[32 * q - 32:32 * q, :, P - 3:P]))
                if q < KD - 1:
                    cv.step(dve.tensor_copy(cpad[here, :, P + 3:P + 6], turned[32 * q + 32:32 * q + 64, :, 0:3]))
            cv.settle()
            dve.wait_ge(s["w_loaded"], W_LOADS * 16)
            for n in range(14):
                win = cpad[:, n // 7, n % 7:n % 7 + P]
                if n == 0:
                    cv.link(dve.tensor_scalar(zc[:, :], win, cw_bc[:, 0:1], None, ALU.mult))
                else:
                    cv.link(dve.scalar_tensor_tensor(out=zc[:, :], in0=win, scalar=cw_bc[:, n:n + 1], in1=zc[:, :],
                                                     op0=ALU.mult, op1=ALU.add))
            cv.link(dve.bn_stats(bnst[:, 0, :], zc[:, :]))
            cv.link(dve.bn_aggr(sm[:, 0:2], bnst[:, 0, :]))
            dve.sem_inc(s["bn_b"], 1)
            dve.wait_ge(s["bn_a"], 2)
            cv.link(dve.tensor_tensor(sm[:, 2:3], sm[:, 0:1], bank[5][:, 0:1], ALU.subtract))
            cv.step(dve.tensor_copy(sm[:, 6:7], bank[5][:, 0:1]))
            cv.link(dve.tensor_tensor(sm[:, 2:3], sm[:, 2:3], sm[:, 2:3], ALU.mult))
            cv.link(dve.tensor_tensor(sm[:, 2:3], sm[:, 2:3], sm[:, 1:2], ALU.add))
            dve.sem_inc(s["bn_b"], 1)
            dve.wait_ge(s["bn_a"], 3)
            cv.link(dve.tensor_scalar(sm[:, 3:4], bank[5][:, 1:2], EPS, None, ALU.add))
            dve.sem_inc(s["bn_c"], 1)
            dve.wait_ge(s["sig_out"], 1)
            cv.link(dve.reciprocal(sm[:, 5:6], sm[:, 4:5]))
            cv.link(dve.tensor_scalar(zc[:, :], zc[:, :], sm[:, 6:7], sm[:, 5:6], ALU.subtract, ALU.mult))
            cv.link(dve.tensor_scalar(zc[:, :], zc[:, :], cw_bc[:, 14:15], cw_bc[:, 15:16], ALU.mult, ALU.add))
            cv.link(dve.tensor_scalar(zc[:, :], zc[:, :], 0.0, None, ALU.max))
            dve.sem_inc(s["sig_in"], 1)
            dve.wait_ge(s["attT"], 1)
            cv.link(dve.tensor_copy(attA[:, :], bank[6][:, 0:P]))
            def gates_of(k, path):
                return attA[:, (2 * k + path) * B:(2 * k + path + 1) * B].unsqueeze(2).broadcast_to([P, B, R])

            for k in range(KD):
                for path, a in ((1, xnT), (0, crucial)):
                    v = a[:, k, :].rearrange("p (b c) -> p b c", b=B)
                    cv.step(dve.tensor_tensor(v, v, gates_of(k, path), ALU.mult))
            cv.settle()
            for k in range(KD):
                cv.step(dve.tensor_tensor(xnT[:, k, :], xnT[:, k, :], crucial[:, k, :], ALU.add))
            cv.settle()
            dve.sem_inc(s["delta_ready"], 1)
            for t in range(T):
                dve.wait_ge(s["delta_done"], t + 1)
                dve.tensor_tensor(xnat[:, t, :], xnat[:, t, :], bank[t % 4], ALU.add).then_inc(s["delta_added"], 1)
            dve.wait_ge(s["delta_added"], T)
            layernorm(1)

            rt = Chain(dve, s["dve_rt"])
            for t in range(T):
                cols = slice(t * P, (t + 1) * P)
                dve.wait_ge(s["lnT_evac"], T + t + 1)
                dve.tensor_tensor(x_parts[1][:, :, cols], xnT[:, :, cols], x_parts[0][:, :, cols].bitcast(F32),
                                  ALU.subtract).then_inc(s["x_split"], 1)
            dve.wait_ge(s["router_done"], 1)
            rt.step(dve.memset(gate[:, :, 0:ES:ES - 1], 1.0))
            logits = bank[0][:, 0:T * E].rearrange("p (t e) -> p t e", t=T)

            def over(ap, n):
                return ap.unsqueeze(2).broadcast_to([P, ap.shape[1], n])

            def per_tile(ap):
                return ap.unsqueeze(1).broadcast_to([P, T, ap.shape[1]])

            rt.link(dve.tensor_tensor(lg[:, :, :], logits, per_tile(rb_bc[:, 0, :]), ALU.add))
            rt.link(dve.tensor_reduce(tv[:, :, 0], lg[:, :, :], AX.X, ALU.max))
            rt.link(dve.tensor_tensor(lg[:, :, :], lg[:, :, :], over(tv[:, :, 0], E), ALU.subtract))
            dve.sem_inc(s["gates_ready"], 1)
            dve.wait_ge(s["logits_exp"], 1)
            rt.link(dve.tensor_reduce(tv[:, :, 1], lg2[:, :, :], AX.X, ALU.add))
            rt.link(dve.reciprocal(tv[:, :, 2], tv[:, :, 1]))
            rt.link(dve.tensor_tensor(lg[:, :, :], lg2[:, :, :], over(tv[:, :, 2], E), ALU.mult))
            rt.link(dve.tensor_tensor(lg[:, :, :], lg[:, :, :], per_tile(rb_bc[:, 1, :]), ALU.add))
            rt.link(dve.tensor_reduce(gm[:, :, :], lg[:, :, :].rearrange("p t (g m) -> p t g m", g=GR), AX.X, ALU.max))

            def ranks(v, n, low, res):
                q, q2 = (pair_tables[:, a, 0:T * n * n].rearrange("p (t a b) -> p t a b", t=T, a=n) for a in range(2))
                mine = v.unsqueeze(3).broadcast_to([P, T, n, n])
                other = v.unsqueeze(2).broadcast_to([P, T, n, n])
                rt.step(dve.tensor_tensor(q, other, mine, ALU.is_gt))
                rt.link(dve.tensor_tensor(q2, other, mine, ALU.is_equal))
                rt.link(dve.tensor_tensor(q2, q2, low.unsqueeze(1).broadcast_to([P, T, n, n]), ALU.mult))
                rt.link(dve.tensor_tensor(q, q, q2, ALU.add))
                rt.link(dve.tensor_reduce(res, q, AX.X, ALU.add))

            ranks(gm[:, :, :], GR, lower[:, 0:GR * GR].rearrange("p (a b) -> p a b", a=GR), tv[:, :, :])
            rt.link(dve.tensor_scalar(gm[:, :, :], tv[:, :, :], 2.0, None, ALU.is_lt))
            keep = gm[:, :, :].unsqueeze(3).broadcast_to([P, T, GR, E // GR])
            sc4 = lg2[:, :, :].rearrange("p t (g m) -> p t g m", g=GR)
            rt.link(dve.tensor_tensor(sc4, lg[:, :, :].rearrange("p t (g m) -> p t g m", g=GR), keep, ALU.mult))
            rt.link(dve.tensor_scalar(gm[:, :, :], gm[:, :, :], -1.0, BIG, ALU.add, ALU.mult))
            rt.link(dve.tensor_tensor(sc4, sc4, keep, ALU.add))
            best, above2, equal2, order2 = (pair_tables[:, 0, T * E * n:T * E * (n + 1)].rearrange("p (t e) -> p t e", t=T) for n in range(4))
            for t in range(T):
                rt.step(dve.max(best[:, t, 0:8], lg2[:, t, :]))
            rt.settle()
            second = over(best[:, :, 1], E)
            rt.step(dve.tensor_tensor(above2, lg2[:, :, :], second, ALU.is_gt))
            rt.link(dve.tensor_tensor(equal2, lg2[:, :, :], second, ALU.is_equal))
            rt.step(dve.tensor_reduce(tv[:, :, 0], above2, AX.X, ALU.add))
            rt.link(dve.tensor_tensor_scan(order2.rearrange("p t e -> p (t e)"), lower[:, GR * GR:],
                                           equal2.rearrange("p t e -> p (t e)"), 0.0, ALU.mult, ALU.add))
            rt.step(dve.tensor_tensor(order2, order2, over(tv[:, :, 0], E), ALU.add))
            rt.settle()
            rt.link(dve.scalar_tensor_tensor(out=equal2, in0=order2, scalar=2.0, in1=equal2, op0=ALU.is_le, op1=ALU.mult))
            rt.link(dve.tensor_tensor(gate[:, :, 1:ES - 1], above2, equal2, ALU.add))
            rt.link(dve.tensor_tensor(gate[:, :, 1:ES - 1], gate[:, :, 1:ES - 1], lg[:, :, :], ALU.mult))
            dve.sem_inc(s["gates_ready"], 1)

            def hidden(n, h, e):
                cols = slice(h * 512, (h + 1) * 512)
                dve.wait_ge(s["silu_done"], 2 * n + h + 1)
                dve.scalar_tensor_tensor(out=hT[:, cols], in0=bank[2 * h + 1], scalar=b12[:, 1, e],
                                         in1=silu[h], op0=ALU.add, op1=ALU.mult).then_inc(s["hT_ready"], 1)
                dve.wait_ge(s["hh_done"], 2 * n + h + 1)
                dve.tensor_tensor(h_parts[1][:, cols], hT[:, cols], h_parts[0][:, cols].bitcast(F32), ALU.subtract).then_inc(s["h_split"], 1)

            def outputs(n, h, e):
                for t in range(4 * h, 4 * h + 4):
                    dve.wait_ge(s["y_done"], n * T + t + 1)
                    if t == 0 and not (isinstance(n, int) and n == 0):
                        dve.wait_ge(s["y_added"], n * T)
                    dve.scalar_tensor_tensor(out=xnat[:, t, :], in0=bank[4 + t % 4], scalar=gate[:, t, e],
                                             in1=xnat[:, t, :], op0=ALU.mult, op1=ALU.add).then_inc(s["y_added"], 1)

            def expert(n, e, e_next):
                hidden(n, 1, e)
                outputs(n, 0, e)
                hidden(n + 1, 0, e_next)
                outputs(n, 1, e)

            def col(e):
                return bass.ds(e, 1)

            hidden(0, 0, slice(0, 1))
            dve.wait_ge(s["pool_bias"], T)
            expert(0, slice(0, 1), slice(1, 2))
            with dve.Fori(0, E // 2) as i:
                for p in range(2):
                    n = 2 * i + p + 1
                    expert(n, col(n), col(n + 1))
            last = slice(ES - 1, ES)
            dve.wait_ge(s["gateT_done"], 1)
            for t in range(2):
                dve.tensor_copy(gateT[:, t * 512:(t + 1) * 512], bank[t][0:E, :]).then_inc(s["gateT_evac"], 1)
            hidden(ES - 1, 1, last)
            outputs(ES - 1, 0, last)
            outputs(ES - 1, 1, last)
            dve.wait_ge(s["y_added"], ES * T)
            layernorm(2)

            dve.wait_ge(s["qbk_done"], 1)
            dve.wait_ge(s["ln_ready"], 3 * T)
            products = work[:, 0:T * D].rearrange("p (t d) -> p t d", t=T)
            qb = Chain(dve, s["dve_qb"])
            qb.link(dve.tensor_tensor(products, normed[:, :, :], bank[0].unsqueeze(1).broadcast_to([P, T, D]), ALU.mult))
            qb.link(dve.tensor_reduce(qbk[:, :], products, AX.X, ALU.add))
            dve.tensor_scalar(qbk[:, :], qbk[:, :], bqk[:, 5:6], None, ALU.add).then_inc(s["qbk_ready"], 1)
            dve.wait_ge(s["qbk_ready"], 1)

            def f_evac(pair, e):
                dve.wait_ge(s["ft_done"], pair * 2 * STEPS + 2 * e + 2)
                dve.wait_ge(s["s_done"], pair * STEPS + e + 1)
                dve.tensor_copy(FT[:, e % 4, 1, :], bank[4 + 2 * (e % 2)][:, 0:GW]).then_inc(s["ft_dve"], 1)

            def attention(pair, last=False):
                at = Chain(dve, s["dve_at"], pair * 6)

                def group_max(g):
                    dve.wait_ge(s["s_done"], pair * STEPS + KD * (g + 1) + 4)
                    at.step(dve.tensor_reduce(gmax[:, g:g + 1], bank[g][:, 0:GW], AX.X, ALU.max))

                for e in range(4, STEPS):
                    f_evac(pair, e)
                    if e == 7:
                        group_max(0)
                group_max(1)
                group_max(2)
                at.settle()
                at.link(dve.tensor_reduce(am[:, 0:1], gmax[:, 0:SG], AX.X, ALU.max))
                q = qbk[:, bass.ds(pair, 1)]
                at.link(dve.tensor_scalar(am[:, 1:2], am[:, 0:1], q, None, ALU.add))
                dve.tensor_scalar(am[:, 2:3], am[:, 1:2], q, -SCALE, ALU.subtract, ALU.mult).then_inc(s["neg_bias"], 1)
                if not last:
                    for e in range(4):
                        f_evac(pair + 1, e)
                dve.wait_ge(s["exp_done"], pair + 1)
                at.link(dve.reciprocal(am[:, 4:5], am[:, 3:4]))
                dve.wait_ge(s["o_done"], pair + 3)
                xr = xnat[:, bass.ds(pair, 1), :]
                dve.scalar_tensor_tensor(out=xr, in0=bank[7].unsqueeze(1), scalar=am[:, 4:5], in1=xr,
                                         op0=ALU.mult, op1=ALU.add).then_inc(s["o_added"], 1)
                dve.wait_ge(s["o_added"], pair + 2)
                over_wait()
                dve.bn_stats(bnst[:, bass.ds(pair, 1), :], xr).then_inc(s["stats_done"], 1)

            for e in range(4):
                f_evac(0, e)
            with dve.Fori(0, T - 1) as i:
                attention(i)
            attention(T - 1, last=True)
            dve.wait_ge(s["stats_done"], T)
            layernorm(3, stats=False)

            fc = Chain(dve, s["dve_fin"])
            dve.wait_ge(s["gl_done"], 1)
            g9 = f1[:, :, :].rearrange("p k c -> p (k c)")[:, 0:T * 9].rearrange("p (t e) -> p t e", t=T)
            fc.step(dve.tensor_copy(g9[:, 0:6, :].rearrange("p (b t) e -> p b t e", b=3),
                                    PS3[:, :, 0:2 * HG].rearrange("p b (t e) -> p b t e", t=2)[:, :, :, P:HG]))
            fc.link(dve.tensor_copy(g9[:, 6:8, :], bank[3][:, 0:2 * HG].rearrange("p (t e) -> p t e", t=2)[:, :, P:HG]))
            fc.link(dve.tensor_reduce(tv[:, :, 0], g9[:, :, 0:E1], AX.X, ALU.max))
            fc.step(dve.tensor_tensor(lg[:, :, 0:E1], g9[:, :, 0:E1], over(tv[:, :, 0], E1), ALU.subtract))
            fc.link(dve.tensor_scalar(lg[:, :, 8:9], g9[:, :, 8:9], bthr_bc[:, 0:1], -1.0, ALU.add, ALU.mult))
            dve.sem_inc(s["w_ready"], 1)
            dve.wait_ge(s["exp9"], 1)
            fc.step(dve.tensor_reduce(tv[:, :, 1], lg2[:, :, 0:E1], AX.X, ALU.add))
            fc.link(dve.tensor_scalar(tv[:, :, 2:3], lg2[:, :, 8:9], 1.0, None, ALU.add))
            fc.link(dve.reciprocal(tv[:, :, 1:3], tv[:, :, 1:3]))
            fc.step(dve.tensor_tensor(lg[:, :, 0:E1], lg2[:, :, 0:E1], over(tv[:, :, 1], E1), ALU.mult))
            fc.link(dve.tensor_scalar(tv[:, :, 3], tv[:, :, 2], 0.125, None, ALU.mult))
            fc.link(dve.tensor_tensor(lg[:, :, 0:E1], lg[:, :, 0:E1], over(tv[:, :, 3], E1), ALU.subtract))
            fc.link(dve.tensor_scalar(lg[:, :, 0:E1], lg[:, :, 0:E1], 0.0, None, ALU.max))
            fc.link(dve.tensor_reduce(tv[:, :, 0], lg[:, :, 0:E1], AX.X, ALU.add))
            fc.link(dve.tensor_scalar(tv[:, :, 1], tv[:, :, 0], 0.0, None, ALU.is_equal))
            fc.link(dve.tensor_tensor(tv[:, :, 0], tv[:, :, 0], tv[:, :, 1], ALU.add))
            fc.link(dve.reciprocal(tv[:, :, 1], tv[:, :, 0]))
            fc.link(dve.tensor_tensor(lg[:, :, 0:E1], lg[:, :, 0:E1], over(tv[:, :, 1], E1), ALU.mult))
            fc.link(dve.tensor_scalar(lg2[:, :, 0:E1], lg[:, :, 0:E1], 2.0, None, ALU.mult))
            for h in range(2):
                for t in range(4 * h, 4 * h + 4):
                    v = bank[t // 2][:, (t % 2) * HG:(t % 2) * HG + P].rearrange("p (e r) -> p e r", e=E1)
                    w = lg2[:, t, 0:E1].unsqueeze(2).broadcast_to([P, E1, RK])
                    fc.step(dve.tensor_tensor(pairs_hw(t).rearrange("p (e r) -> p e r", e=E1), v, w, ALU.mult))
                fc.settle()
                dve.sem_inc(s["hw_ready"], 1)
            dve.wait_ge(s["pool_bias"], 2 * T)
            for t in range(T):
                dve.wait_ge(s["fin_done"], t + 1)
                dve.tensor_tensor(xnat[:, t, :], xnat[:, t, :], bank[4 + t % 4], ALU.add).then_inc(s["fin_added"], 1)


PRE_ACT = 5 + 1 + 1 + 4 + 4 + 2
SORT_STEPS = 3 + 12
PICK_STEPS = 3 + 2 + 1 + 2
SEARCH_STEPS = SORT_STEPS + PICK_STEPS + 2 * (4 * 3 + 3)
FALLBACK_STEPS = 1 + 20 + 16 + 3 + PICK_STEPS + 1 + 2
ORDER = [0, 3, 6, 9, 1, 2, 4, 5, 7, 8, 10, 11]
NEXT = [[0, 1], [2, 3], [4, 5], [6, 7], [8, 9], [10, 11], [], []]
W_LOADS = 4 + 4 + 1 + 1 + 2 + 3 + 1
ROW_LOADS = 3 + 1 + 6


_INS = ['x', 'ctx_4096', 'L0_xattn_conv_w', 'L0_xattn_bn_gamma', 'L0_xattn_bn_beta', 'L0_ffn_router_w', 'L0_ffn_router_b',
        'L0_ffn_router_bias', 'L0_ffn_ew1', 'L0_ffn_eb1', 'L0_ffn_ew2', 'L0_ffn_eb2', 'L0_ffn_ew3', 'L0_ffn_eb3',
        'L0_ffn_sw1', 'L0_ffn_sb1', 'L0_ffn_sw2', 'L0_ffn_sb2', 'L0_ffn_sw3', 'L0_ffn_sb3', 'L1_xattn_Wq', 'L1_xattn_bq',
        'L1_xattn_Wk', 'L1_xattn_bk', 'L1_ffn_W_base', 'L1_ffn_b_base', 'L1_ffn_W_gate', 'L1_ffn_W_thr', 'L1_ffn_b_thr',
        'L1_ffn_A_w', 'L1_ffn_B_w']


def _constants():
    import numpy as np
    p = np.arange(128)
    path = (p // 16) % 2
    first = np.ones((8, 16), np.float32)
    first[:, 0] = 0.0
    low = [np.tril(np.ones((4, 4), np.float32), -1).reshape(-1), first.reshape(-1)]
    reset = np.ones((4, 56), np.float32)
    reset[:, 0] = 0.0
    return {"ident": np.eye(128, dtype=np.float32),
            "pathmean": (path[:, None] == path[None, :]).astype(np.float32) / 64,
            "lower": np.tile(np.concatenate(low), (128, 1)),
            "reset": np.tile(reset.reshape(-1), (128, 1))}


def kernel(**inputs):
    import numpy as _np
    import concourse.bacc as _bacc
    from concourse import mybir as _mybir
    from concourse.bass_utils import run_bass_kernel_spmd as _run

    nc = _bacc.Bacc("TRN2", target_bir_lowering=False, num_devices=1)
    arrays, A = {}, {}
    given = {n: inputs[n] for n in _INS}
    given.update(_constants())
    for name, v in given.items():
        a = _np.ascontiguousarray(v)
        arrays[f"in_{name}_dram"] = a
        A[name] = nc.dram_tensor(f"in_{name}_dram", a.shape, _mybir.dt.from_np(a.dtype), kind="ExternalInput").ap()
    out = nc.dram_tensor("out_0_dram", (16, 56, 512), _mybir.dt.float32, kind="ExternalOutput").ap()
    bass_xattn_ffn_layers(nc, A, out)
    r = _run(nc, [arrays], core_ids=[0])
    return r.results[0]["out_0_dram"]
```
